# Optimizing a Trainium2 kernel written in Bass

```python
import numpy as np
import jax
import jax.numpy as jnp

def _softmax(x, axis=-1):
    return jax.nn.softmax(x, axis=axis)

def _gelu(x):
    return jax.nn.gelu(x, approximate=True)

def _silu(x):
    return jax.nn.silu(x)

def _sigmoid(x):
    return jax.nn.sigmoid(x)

def _layernorm(x, axis=-1, eps=1e-05):
    m = jnp.mean(x, axis=axis, keepdims=True)
    v = jnp.var(x, axis=axis, keepdims=True)
    return (x - m) / jnp.sqrt(v + eps)

def _scatter_add(tgt, idx, src, axis=0):
    return tgt.at[idx].add(src)

def _segment_sum(src, seg, n):
    return jax.ops.segment_sum(src, seg, n)
kernel_name = 'mk_gnn_preln_d4_gnn_r8_241e1e'

def setup_inputs(seed: int=0):
    np.random.seed(seed)
    _w = jnp.asarray

    def _rec_inputs():
        import jax
        import jax.numpy as jnp
        _gk = jax.random.key(seed)
        x = -0.0005121 + 1.001 * jax.random.normal(jax.random.fold_in(_gk, 1), (12500, 32), jnp.float32)
        _s = jax.random.randint(jax.random.fold_in(_gk, 2), (100000,), 0, 12500, jnp.int32)
        _d = jax.random.randint(jax.random.fold_in(_gk, 3), (100000,), 0, 12500, jnp.int32)
        _loop = jnp.arange(12500, dtype=jnp.int32)
        src = jnp.concatenate([_s, _d, _loop])
        dst = jnp.concatenate([_d, _s, _loop])
        _o = jnp.argsort(dst, stable=True)
        src = src[_o]
        dst = dst[_o]
        edge_attr_3 = 0.000844983 + 0.999762 * jax.random.normal(jax.random.fold_in(_gk, 12), (212500, 3), jnp.float32)
        edge_weight = jax.random.uniform(jax.random.fold_in(_gk, 14), (212500,), jnp.float32, 0.0, 1)
        return (x, src, dst, edge_attr_3, edge_weight)
    x, src, dst, edge_attr_3, edge_weight = _rec_inputs()

    def _L0_gnn_setup():
        import jax, jax.numpy as jnp
        import numpy as np
        N = 12500
        E = 200000
        F_IN = 32
        F_OUT = 32
        key = jax.random.key(seed)
        k1, k2, k3, k4, k5 = jax.random.split(key, 5)
        x = jax.random.normal(k1, (N, F_IN), dtype=jnp.float32)
        edge_src = jax.random.randint(k2, (E,), 0, N, dtype=jnp.int32)
        edge_dst = jax.random.randint(k3, (E,), 0, N, dtype=jnp.int32)
        bound = 1.0 / np.sqrt(2 * F_IN)
        W = jax.random.uniform(k4, (2 * F_IN, F_OUT), minval=-bound, maxval=bound, dtype=jnp.float32)
        b = jax.random.uniform(k5, (F_OUT,), minval=-bound, maxval=bound, dtype=jnp.float32)
        return {'x': x, 'W': W, 'b': b, 'edge_src': edge_src, 'edge_dst': edge_dst}
    _L0_gnn_all = _L0_gnn_setup()
    _L0_gnn_in = {k: v for k, v in _L0_gnn_all.items() if k in ('W', 'b')}
    del _L0_gnn_all

    def _L1_gnn_setup():
        import jax, jax.numpy as jnp
        import numpy as np
        N_NODES = 12500
        N_EDGES = 200000
        N_FEAT = 32
        key = jax.random.key(seed)
        k1, k2, k3, k4 = jax.random.split(key, 4)
        u = jax.random.normal(k1, (N_NODES, N_FEAT), dtype=jnp.float32)
        weights = jax.random.uniform(k2, (N_EDGES,), dtype=jnp.float32)
        row = jax.random.randint(k3, (N_EDGES,), 0, N_NODES)
        col = jax.random.randint(k4, (N_EDGES,), 0, N_NODES)
        edge_index = jnp.stack([row, col]).astype(jnp.int64)
        return {'u': u, 'weights': weights, 'edge_index': edge_index}
    _L1_gnn_all = _L1_gnn_setup()
    _L1_gnn_in = {k: v for k, v in _L1_gnn_all.items() if k in ()}
    del _L1_gnn_all

    def _L2_gnn_setup():
        import jax, jax.numpy as jnp
        import numpy as np
        from math import factorial, pi, sqrt
        MUL = 8
        RS = [(MUL, 0), (MUL, 1)]
        N_NODES = 2500
        N_EDGES = 80000
        FEAT_DIM = sum((m * (2 * l + 1) for m, l in RS))
        R_DIM = sum((mo * mi * (2 * min(lo, li) + 1) for mo, lo in RS for mi, li in RS))
        HIDDEN = 64

        def _cg(j1, j2, j3, m1, m2, m3):
            if m1 + m2 != m3:
                return 0.0
            f = factorial
            pre = sqrt((2 * j3 + 1) * f(j3 + j1 - j2) * f(j3 - j1 + j2) * f(j1 + j2 - j3) / f(j1 + j2 + j3 + 1))
            pre *= sqrt(f(j3 + m3) * f(j3 - m3) * f(j1 - m1) * f(j1 + m1) * f(j2 - m2) * f(j2 + m2))
            kmin = max(0, j2 - j3 - m1, j1 - j3 + m2)
            kmax = min(j1 + j2 - j3, j1 - m1, j2 + m2)
            s = 0.0
            for k in range(kmin, kmax + 1):
                s += (-1) ** k / (f(k) * f(j1 + j2 - j3 - k) * f(j1 - m1 - k) * f(j2 + m2 - k) * f(j3 - j2 + m1 + k) * f(j3 - j1 - m2 + k))
            return pre * s

        def _w3j_complex(l1, l2, l3):
            w = np.zeros((2 * l1 + 1, 2 * l2 + 1, 2 * l3 + 1))
            for m1 in range(-l1, l1 + 1):
                for m2 in range(-l2, l2 + 1):
                    m3 = -(m1 + m2)
                    if abs(m3) <= l3:
                        w[m1 + l1, m2 + l2, m3 + l3] = (-1) ** (l1 - l2 - m3) / sqrt(2 * l3 + 1) * _cg(l1, l2, l3, m1, m2, -m3)
            return w

        def _A(l):
            A = np.zeros((2 * l + 1, 2 * l + 1), dtype=complex)
            A[l, l] = 1.0
            for m in range(1, l + 1):
                A[l + m, l + m] = (-1) ** m / sqrt(2)
                A[l + m, l - m] = 1.0 / sqrt(2)
                A[l - m, l - m] = 1j / sqrt(2)
                A[l - m, l + m] = -1j * (-1) ** m / sqrt(2)
            return A

        def real_w3j(l1, l2, l3):
            wc = _w3j_complex(l1, l2, l3).astype(complex)
            wr = np.einsum('abc,ma,nb,oc->mno', wc, _A(l1).conj(), _A(l2).conj(), _A(l3).conj())
            i = int(np.argmax(np.abs(wr)))
            ph = wr.flat[i] / abs(wr.flat[i])
            wr = wr / ph
            assert np.abs(wr.imag).max() < 1e-10
            return np.real(wr).astype(np.float32)
        _W3J = {}
        for _mo, _lo in RS:
            for _mi, _li in RS:
                for _lf in range(abs(_lo - _li), _lo + _li + 1):
                    if (_lo, _lf, _li) not in _W3J:
                        _W3J[_lo, _lf, _li] = jnp.asarray(real_w3j(_lo, _lf, _li))
        _NORM = []
        for _mo, _lo in RS:
            _num = sum((mi * (2 * min(_lo, li) + 1) for mi, li in RS))
            _NORM.append(sqrt(4.0 * pi) * sqrt(2.0 * _lo + 1.0) / sqrt(_num))
        _F_OFFS = [0] + list(np.cumsum([mi * (2 * li + 1) for mi, li in RS]))

        def spherical_harmonics(rel_vec):
            r = rel_vec / jnp.linalg.norm(rel_vec, axis=-1, keepdims=True)
            x, y, z = (r[:, 0], r[:, 1], r[:, 2])
            y0 = jnp.full_like(x, 0.5 / sqrt(pi))[:, None]
            c1 = sqrt(3.0 / (4.0 * pi))
            y1 = c1 * jnp.stack([y, z, x], axis=-1)
            c2a = 0.5 * sqrt(15.0 / pi)
            c2b = 0.25 * sqrt(5.0 / pi)
            c2c = 0.25 * sqrt(15.0 / pi)
            y2 = jnp.stack([c2a * x * y, c2a * y * z, c2b * (3.0 * z * z - 1.0), c2a * x * z, c2c * (x * x - y * y)], axis=-1)
            return jnp.concatenate([y0, y1, y2], axis=-1)
        key = jax.random.key(seed)
        ks = jax.random.split(key, 6)
        features = jax.random.normal(ks[0], (N_NODES, FEAT_DIM), dtype=jnp.float32)
        abs_distances = jax.random.uniform(ks[1], (N_EDGES,), dtype=jnp.float32, minval=0.1, maxval=1.0)
        rel_vec = jax.random.normal(ks[2], (N_EDGES, 3), dtype=jnp.float32)
        edge_index = jax.random.randint(ks[3], (2, N_EDGES), 0, N_NODES, dtype=jnp.int32)
        w1 = jax.random.normal(ks[4], (1, HIDDEN), dtype=jnp.float32)
        b1 = jnp.zeros((HIDDEN,), jnp.float32)
        w2 = jax.random.normal(ks[5], (HIDDEN, R_DIM), dtype=jnp.float32) / sqrt(HIDDEN)
        b2 = jnp.zeros((R_DIM,), jnp.float32)
        return {'features': features, 'abs_distances': abs_distances, 'rel_vec': rel_vec, 'edge_index': edge_index, 'w1': w1, 'b1': b1, 'w2': w2, 'b2': b2}
    _L2_gnn_all = _L2_gnn_setup()
    _L2_gnn_in = {k: v for k, v in _L2_gnn_all.items() if k in ('w1', 'b1', 'w2', 'b2')}
    del _L2_gnn_all

    def _L3_gnn_setup():
        import jax, jax.numpy as jnp
        import numpy as np
        N_NODES = 12500
        N_EDGES = 200000
        IN_FEATS = 32
        OUT_FEATS = 32
        key = jax.random.key(seed)
        k1, k2, k3, k4, k5 = jax.random.split(key, 5)
        feature = jax.random.normal(k1, (N_NODES, IN_FEATS), dtype=jnp.float32)
        src = jax.random.randint(k2, (N_EDGES,), 0, N_NODES, dtype=jnp.int64)
        dst = jax.random.randint(k3, (N_EDGES,), 0, N_NODES, dtype=jnp.int64)
        dst = jnp.where(dst == src, (dst + 1) % N_NODES, dst)
        W = jax.random.normal(k4, (OUT_FEATS, IN_FEATS), dtype=jnp.float32) / np.sqrt(IN_FEATS)
        bias = jnp.zeros((OUT_FEATS,), dtype=jnp.float32)
        return {'feature': feature, 'src': src, 'dst': dst, 'W': W, 'bias': bias}
    _L3_gnn_all = _L3_gnn_setup()
    _L3_gnn_in = {k: v for k, v in _L3_gnn_all.items() if k in ('W', 'bias')}
    del _L3_gnn_all
    return {'x': x, 'src': src, 'dst': dst, 'edge_attr_3': edge_attr_3, 'edge_weight': edge_weight, 'L0_gnn_W': _L0_gnn_in['W'], 'L0_gnn_b': _L0_gnn_in['b'], 'L2_gnn_w1': _L2_gnn_in['w1'], 'L2_gnn_b1': _L2_gnn_in['b1'], 'L2_gnn_w2': _L2_gnn_in['w2'], 'L2_gnn_b2': _L2_gnn_in['b2'], 'L3_gnn_W': _L3_gnn_in['W'], 'L3_gnn_bias': _L3_gnn_in['bias']}

def reference(x, src, dst, edge_attr_3, edge_weight, L0_gnn_W, L0_gnn_b, L2_gnn_w1, L2_gnn_b1, L2_gnn_w2, L2_gnn_b2, L3_gnn_W, L3_gnn_bias):
    import jax
    import jax.numpy as jnp

    def _L0_gnn_ref(x, W, b, edge_src, edge_dst):
        import jax, jax.numpy as jnp
        import numpy as np
        N = 12500
        E = 200000
        F_IN = 32
        F_OUT = 32
        n = x.shape[0]
        msgs = x[edge_src]
        summed = jax.ops.segment_sum(msgs, edge_dst, num_segments=n)
        cnt = jax.ops.segment_sum(jnp.ones_like(edge_dst, dtype=x.dtype), edge_dst, num_segments=n)
        neigh_mean = summed / jnp.maximum(cnt, 1.0)[:, None]
        h = jnp.concatenate([x, neigh_mean], axis=1)
        return jax.nn.relu(h @ W + b)

    def _L1_gnn_ref(u, weights, edge_index):
        import jax, jax.numpy as jnp
        import numpy as np
        N_NODES = 12500
        N_EDGES = 200000
        N_FEAT = 32
        row, col = (edge_index[0], edge_index[1])
        diff = u[col] - u[row]
        weighted_diff = weights[:, None] * diff
        laplacian = jax.ops.segment_sum(weighted_diff, row, num_segments=u.shape[0])
        return laplacian

    def _L2_gnn_ref(features, abs_distances, rel_vec, edge_index, w1, b1, w2, b2):
        import jax, jax.numpy as jnp
        import numpy as np
        from math import factorial, pi, sqrt
        MUL = 8
        RS = [(MUL, 0), (MUL, 1)]
        N_NODES = 2500
        N_EDGES = 80000
        FEAT_DIM = sum((m * (2 * l + 1) for m, l in RS))
        R_DIM = sum((mo * mi * (2 * min(lo, li) + 1) for mo, lo in RS for mi, li in RS))
        HIDDEN = 64

        def _cg(j1, j2, j3, m1, m2, m3):
            if m1 + m2 != m3:
                return 0.0
            f = factorial
            pre = sqrt((2 * j3 + 1) * f(j3 + j1 - j2) * f(j3 - j1 + j2) * f(j1 + j2 - j3) / f(j1 + j2 + j3 + 1))
            pre *= sqrt(f(j3 + m3) * f(j3 - m3) * f(j1 - m1) * f(j1 + m1) * f(j2 - m2) * f(j2 + m2))
            kmin = max(0, j2 - j3 - m1, j1 - j3 + m2)
            kmax = min(j1 + j2 - j3, j1 - m1, j2 + m2)
            s = 0.0
            for k in range(kmin, kmax + 1):
                s += (-1) ** k / (f(k) * f(j1 + j2 - j3 - k) * f(j1 - m1 - k) * f(j2 + m2 - k) * f(j3 - j2 + m1 + k) * f(j3 - j1 - m2 + k))
            return pre * s

        def _w3j_complex(l1, l2, l3):
            w = np.zeros((2 * l1 + 1, 2 * l2 + 1, 2 * l3 + 1))
            for m1 in range(-l1, l1 + 1):
                for m2 in range(-l2, l2 + 1):
                    m3 = -(m1 + m2)
                    if abs(m3) <= l3:
                        w[m1 + l1, m2 + l2, m3 + l3] = (-1) ** (l1 - l2 - m3) / sqrt(2 * l3 + 1) * _cg(l1, l2, l3, m1, m2, -m3)
            return w

        def _A(l):
            A = np.zeros((2 * l + 1, 2 * l + 1), dtype=complex)
            A[l, l] = 1.0
            for m in range(1, l + 1):
                A[l + m, l + m] = (-1) ** m / sqrt(2)
                A[l + m, l - m] = 1.0 / sqrt(2)
                A[l - m, l - m] = 1j / sqrt(2)
                A[l - m, l + m] = -1j * (-1) ** m / sqrt(2)
            return A

        def real_w3j(l1, l2, l3):
            wc = _w3j_complex(l1, l2, l3).astype(complex)
            wr = np.einsum('abc,ma,nb,oc->mno', wc, _A(l1).conj(), _A(l2).conj(), _A(l3).conj())
            i = int(np.argmax(np.abs(wr)))
            ph = wr.flat[i] / abs(wr.flat[i])
            wr = wr / ph
            assert np.abs(wr.imag).max() < 1e-10
            return np.real(wr).astype(np.float32)
        _W3J = {}
        for _mo, _lo in RS:
            for _mi, _li in RS:
                for _lf in range(abs(_lo - _li), _lo + _li + 1):
                    if (_lo, _lf, _li) not in _W3J:
                        _W3J[_lo, _lf, _li] = jnp.asarray(real_w3j(_lo, _lf, _li))
        _NORM = []
        for _mo, _lo in RS:
            _num = sum((mi * (2 * min(_lo, li) + 1) for mi, li in RS))
            _NORM.append(sqrt(4.0 * pi) * sqrt(2.0 * _lo + 1.0) / sqrt(_num))
        _F_OFFS = [0] + list(np.cumsum([mi * (2 * li + 1) for mi, li in RS]))

        def spherical_harmonics(rel_vec):
            r = rel_vec / jnp.linalg.norm(rel_vec, axis=-1, keepdims=True)
            x, y, z = (r[:, 0], r[:, 1], r[:, 2])
            y0 = jnp.full_like(x, 0.5 / sqrt(pi))[:, None]
            c1 = sqrt(3.0 / (4.0 * pi))
            y1 = c1 * jnp.stack([y, z, x], axis=-1)
            c2a = 0.5 * sqrt(15.0 / pi)
            c2b = 0.25 * sqrt(5.0 / pi)
            c2c = 0.25 * sqrt(15.0 / pi)
            y2 = jnp.stack([c2a * x * y, c2a * y * z, c2b * (3.0 * z * z - 1.0), c2a * x * z, c2c * (x * x - y * y)], axis=-1)
            return jnp.concatenate([y0, y1, y2], axis=-1)
        src, dst = (edge_index[0], edge_index[1])
        R = jax.nn.relu(abs_distances[:, None] @ w1 + b1) @ w2 + b2
        Y = spherical_harmonics(rel_vec)
        Fj = features[src]
        E = Fj.shape[0]
        msg_blocks = []
        r_off = 0
        for i, (mo, lo) in enumerate(RS):
            acc = jnp.zeros((E, mo, 2 * lo + 1), dtype=features.dtype)
            for j, (mi, li) in enumerate(RS):
                n_lf = 2 * min(lo, li) + 1
                sz = mo * mi * n_lf
                Rb = R[:, r_off:r_off + sz].reshape(E, mo, mi, n_lf)
                r_off += sz
                Fb = Fj[:, _F_OFFS[j]:_F_OFFS[j + 1]].reshape(E, mi, 2 * li + 1)
                for k, lf in enumerate(range(abs(lo - li), lo + li + 1)):
                    C = _W3J[lo, lf, li]
                    Yf = Y[:, lf * lf:(lf + 1) * (lf + 1)]
                    acc = acc + _NORM[i] * jnp.einsum('euv,ef,evi,ofi->euo', Rb[..., k], Yf, Fb, C)
            msg_blocks.append(acc.reshape(E, -1))
        msg = jnp.concatenate(msg_blocks, axis=-1)
        out = jnp.zeros((features.shape[0], msg.shape[1]), dtype=features.dtype)
        out = out.at[dst].add(msg)
        return out

    def _L3_gnn_ref(feature, src, dst, W, bias):
        import jax, jax.numpy as jnp
        import numpy as np
        N_NODES = 12500
        N_EDGES = 200000
        IN_FEATS = 32
        OUT_FEATS = 32
        n = feature.shape[0]
        loops = jnp.arange(n, dtype=src.dtype)
        src_all = jnp.concatenate([src, loops])
        dst_all = jnp.concatenate([dst, loops])
        deg = jax.ops.segment_sum(jnp.ones_like(dst_all, dtype=feature.dtype), dst_all, num_segments=n)
        deg = jnp.maximum(deg, 1.0)[:, None]
        inv_sqrt_deg = jax.lax.rsqrt(deg)
        h = jnp.einsum('ni,oi->no', feature * inv_sqrt_deg, W)
        agg = jax.ops.segment_sum(h[src_all], dst_all, num_segments=n)
        out = jax.nn.relu(agg * inv_sqrt_deg + bias)
        return out
    edge_index = jnp.stack([src, dst])
    h = jnp.maximum(_layernorm(x, axis=-1), 0.0)
    x = x + _L0_gnn_ref(h, L0_gnn_W, L0_gnn_b, src, dst)
    h = jnp.maximum(_layernorm(x, axis=-1), 0.0)
    x = x + _L1_gnn_ref(h, edge_weight, edge_index)
    h = jnp.maximum(_layernorm(x, axis=-1), 0.0)
    x = x + _L2_gnn_ref(h, edge_weight, edge_attr_3, edge_index, L2_gnn_w1, L2_gnn_b1, L2_gnn_w2, L2_gnn_b2)
    h = jnp.maximum(_layernorm(x, axis=-1), 0.0)
    x = x + _L3_gnn_ref(h, src, dst, L3_gnn_W, L3_gnn_bias)
    return x

_drawn_inputs = setup_inputs


def setup_inputs(seed=0):
    import zlib

    import numpy as np

    out = dict(_drawn_inputs(seed))
    spreads = {'L2_gnn_b1': (0.0, 0.1), 'L2_gnn_b2': (0.0, 0.1), 'L3_gnn_bias': (0.0, 0.624)}
    factors = {}
    for name, (base, spread) in spreads.items():
        noise = np.random.default_rng([zlib.crc32(name.encode()), seed]).standard_normal(out[name].shape)
        drawn = base * np.exp(spread * noise) if base else spread * noise
        out[name] = jnp.asarray(drawn.astype(out[name].dtype))
    for name, factor in factors.items():
        out[name] = (out[name] * factor).astype(out[name].dtype)
    return out
```

```python
import concourse.bass as bass
from concourse import mybir
from contextlib import ExitStack
from math import pi, sqrt

fp32 = mybir.dt.float32
bf16 = mybir.dt.bfloat16
i32 = mybir.dt.int32
ALU = mybir.AluOpType
ACT = mybir.ActivationFunctionType
AX = mybir.AxisListType.X

P = 128
N, F = 12500, 32
E = 212500
J = -(-N // P)
NP = P * J
C = 32
ITERS = -(-E // (P * C * 2))
T = ITERS * 2 * C
EP = P * T
W1 = C + 1
FM = F + 1
TABLES = 8
G = 4
HID = 64
MUL = 8
NB = 14
TURN = {0: 1, 2: 2, 3: 3}
EPS = 1e-5


def gnn_program(nc, x, src, dst, attr, weight, w_sage, b_sage, w1, b1, w2, b2, w_gcn, b_gcn, out):
    ctx = ExitStack()

    def sb(name, shape, dt=fp32):
        return ctx.enter_context(nc.sbuf_tensor(name, shape, dt))

    def pb(name):
        return ctx.enter_context(nc.psum_tensor(name, [P, 512], fp32))

    def sem(name):
        return ctx.enter_context(nc.semaphore(name))

    def dram(name, shape, dt=fp32):
        return nc.dram_tensor(name, shape, dt, kind="Internal").ap()

    with ctx:
        table = [dram(f"node_table{k}", (NP, F)) for k in range(4)]
        scans = {k: dram(f"edge_scans{k}", (EP + 1, F)) for k in (0, 2, 3)}
        spread = dram("edge_spread", (EP + NP, F))
        carried = {k: dram(f"carried{k}", (NP + P, F)) for k in (0, 2, 3)}
        part = [dram(f"source_sums{k}", (NP + P, FM)) for k in range(TABLES)]

        src_i = sb("src_i", [P, T + C], i32)
        wgt = sb("wgt", [P, T + C])
        dst_f = sb("dst_f", [P, T])
        same = sb("same", [P, T])
        rvec = sb("rvec", [P, T, 3])
        share_a = sb("share_a", [P, 2 * T])
        lo, hi = share_a[:, 0:T], share_a[:, T:2 * T]
        share_b = sb("share_b", [P, 3328])
        zeros = share_b[:, :]
        xs = sb("xs", [P, J, F])
        hn = sb("hn", [P, J, F])
        ag = sb("ag", [P, J, F])
        tmp = sb("tmp", [P, J * FM])
        tmpv = tmp[:, 0:J * F].rearrange("p (j f) -> p j f", f=F)
        got = sb("got", [P, 2, C, F])
        xT = sb("xT", [P, 2, F, W1])
        keep = sb("keep", [P, 2, F, W1])
        sc = sb("sc", [P, 2, F, W1])
        rows = sb("rows", [P, 2, C, F])
        dst_i = rows[:, :, :, :].rearrange("p h t f -> p (h t f)").bitcast(i32)[:, 0:T]
        idx = sb("idx", [P, 2, C], i32)
        idxf = sb("idxf", [P, 2, C])
        msg = share_a[:, 0:2 * C * FM].rearrange("p (h t f) -> p h t f", h=2, f=FM)
        sums = share_b[:, 0:2 * C * FM].rearrange("p (h t f) -> p h t f", h=2, f=FM)
        share_c = sb("share_c", [P, 15 * C * MUL])
        eq = share_c[:, 0:2 * G * P].rearrange("p (h q) -> p h q", h=2)
        earlier = share_c[:, 2 * G * P:3 * G * P]
        dup = sb("dup", [P, C])
        widx_f = sb("widx_f", [P, C])
        VEC, PAIR = 6 * MUL, 2 * MUL
        red = share_a[:, 0:2 * C * VEC].rearrange("p (h t q) -> p h t q", h=2, q=VEC)
        prod = share_b[:, 0:4 * VEC * MUL].rearrange("p (s q) -> p s q", q=VEC * MUL)
        pairs_of = [tile.rearrange("p (w t q) -> p w t q", w=PAIR, q=PAIR)
                    for tile in (tmp[:, 0:2 * G * PAIR * PAIR],
                                 ag[:, :, :].rearrange("p j f -> p (j f)")[:, 0:2 * G * PAIR * PAIR])]
        CM = C * MUL
        d16 = share_c[:, 0:4 * CM].rearrange("p (h t v) -> p h t v", h=2, t=C)
        fr = share_c[:, 4 * CM:7 * CM].rearrange("p (t o v) -> p t o v", t=C, o=3)
        fr2 = share_c[:, 7 * CM:10 * CM].rearrange("p (t o v) -> p t o v", t=C, o=3)
        c5 = share_c[:, 10 * CM:15 * CM].rearrange("p (t o v) -> p t o v", t=C, o=5)
        r5 = sb("r5", [P, 2, C, 5])
        sv = sb("sv", [P, 2, C, MUL])
        hid = sb("hid", [HID + 1, 2, G * P])
        w2s = sb("w2s", [HID + 1, 384])
        w2p = sb("w2p", [HID + 1, 384])
        w1c = sb("w1c", [HID, 1])
        b1c = sb("b1c", [HID, 1])
        one_lo = sb("one_lo", [P, 2, G, J], bf16)
        one_hi = sb("one_hi", [P, 2, G, P], bf16)
        ident = sb("ident", [P, P])
        upper = sb("upper", [P, P])
        lower = sb("lower", [P, P])
        joins = sb("joins", [P, P])
        ends_after = sb("ends_after", [P, P])
        ji_i = sb("ji_i", [P, J], i32)
        ji = sb("ji", [P, J])
        pi_i = sb("pi_i", [P, P], i32)
        pif = sb("pif", [P, P])
        dump_i = sb("dump_i", [P, 1], i32)
        dump = sb("dump", [P, 1])
        cnt = sb("cnt", [P, J])
        run = sb("run", [P, J])
        first_f = sb("first_f", [P, J])
        last_f = sb("last_f", [P, J])
        nzero = sb("nzero", [P, J])
        sdump_i = sb("sdump_i", [P, J], i32)
        sdump = sb("sdump", [P, J])
        first_i = sb("first_i", [P, J], i32)
        last_i = sb("last_i", [P, J], i32)
        rcnt = sb("rcnt", [P, J])
        isd = sb("isd", [P, J])
        st1 = sb("st1", [P, J])
        st2 = sb("st2", [P, J])
        st3 = sb("st3", [P, J])
        ones = sb("ones", [P, J])
        offs = sb("offs", [P, 1])
        cidx_f = sb("cidx_f", [P, 1])
        cidx_t = sb("cidx_t", [P, 1])
        cidx = sb("cidx", [P, 1], i32)
        dst0_i = sb("dst0_i", [P, 1], i32)
        tails = sb("tails", [P, F])
        carry = sb("carry", [P, F])
        head = sb("head", [P, F])
        stage = share_c[:, 0:NB * 2 * F].rearrange("p (j f) -> p j f", j=NB)
        turned = share_c[0:2 * F, NB * 2 * F:NB * (2 * F + P // 2)]
        w_sage_s = sb("w_sage_s", [2 * F, F])
        w_gcn_s = sb("w_gcn_s", [F, F])
        b_sage_s = sb("b_sage_s", [P, F])
        b_gcn_s = sb("b_gcn_s", [P, F])

        pbc = [pb(f"pbc{k}") for k in range(2)]
        pr = [pb(f"pr{k}") for k in range(4)]
        pm = [pb(f"pm{k}") for k in range(2)]
        hist = pr[0][:, 0:J]

        S = {}

        def s(name):
            if name not in S:
                S[name] = sem(name)
            return S[name]

        def past(value):
            return not isinstance(value, int) or value > 0

        def steps(eng, body):
            body(0)
            with eng.Fori(1, ITERS) as it:
                body(it)

        def body_steps(eng, body):
            body(0)
            with eng.Fori(1, J // NB) as it:
                body(it)

        class Chain:

            def __init__(self, eng, name, per_step=0, before=0):
                self.eng, self.name, self.per, self.n, self.before, self.it = eng, name, per_step, 0, before, 0

            def step(self, it):
                self.it, self.n = it, 0

            def do(self, ins, wait_now=True):
                self.n += 1
                ins.then_inc(s(self.name), 1)
                if wait_now:
                    self.now()
                return self.n

            def now(self, n=None):
                self.eng.wait_ge(s(self.name), self.it * self.per + (self.n if n is None else n) + self.before)

        def node_rows(t):
            return t.rearrange("(p j) f -> p (j f)", p=P)

        ZERO_RUNS = [(spread[0:EP, :].rearrange("(p t) f -> p (t f)", p=P), T * F)]
        for k in range(TABLES):
            ZERO_RUNS.append((part[k].rearrange("(p j) f -> p (j f)", p=P), (NP + P) // P * FM))
        for k in (0, 2, 3):
            ZERO_RUNS.append((carried[k].rearrange("(p j) f -> p (j f)", p=P), (NP + P) // P * F))
        ZEROED = sum(-(-n // 3328) for _, n in ZERO_RUNS) + 3

        block = ctx.enter_context(nc.Block())

        @block.sync
        def _(sp):
            sp.wait_ge(s("pads_set"), 6)
            full, rest = E // T, E % T
            for name, tile, src_ap in (("dst_in", dst_i, dst), ("src_in", src_i, src), ("wgt_in", wgt, weight)):
                sp.dma_start(tile[0:full, 0:T], src_ap[0:full * T].rearrange("(p t) -> p t", t=T)).then_inc(s(name), 16)
                sp.dma_start(tile[full:full + 1, 0:rest], src_ap[full * T:E].rearrange("(p t) -> p t", p=1)).then_inc(s(name), 16)
            rv = rvec[:, :, :].rearrange("p t c -> p (t c)")
            sp.dma_start(rv[0:full, :], attr[0:full * T, :].rearrange("(p t) c -> p (t c)", t=T)).then_inc(s("attr_in"), 16)
            sp.dma_start(rv[full:full + 1, 0:3 * rest], attr[full * T:E, :].rearrange("(p t) c -> p (t c)", p=1)).then_inc(s("attr_in"), 16)
            nfull, nrest = N // J, N % J
            xv = xs[:, :, :].rearrange("p j f -> p (j f)")
            sp.dma_start(xv[0:nfull, :], x[0:nfull * J, :].rearrange("(p j) f -> p (j f)", j=J)).then_inc(s("x_in"), 16)
            sp.dma_start(xv[nfull:nfull + 1, 0:nrest * F], x[nfull * J:N, :].rearrange("(p j) f -> p (j f)", p=1)).then_inc(s("x_in"), 16)
            sp.dma_start(w_sage_s[:, :], w_sage).then_inc(s("weights_in"), 16)
            sp.dma_start(w_gcn_s[:, :], w_gcn.rearrange("o i -> i o"), allow_slow_non_contiguous=True).then_inc(s("weights_in"), 16)
            sp.dma_start(b_sage_s[:, :], b_sage.rearrange("(a f) -> a f", a=1).broadcast_to([P, F])).then_inc(s("weights_in"), 16)
            sp.dma_start(b_gcn_s[:, :], b_gcn.rearrange("(a f) -> a f", a=1).broadcast_to([P, F])).then_inc(s("weights_in"), 16)
            sp.dma_start(w1c[:, :], w1.rearrange("a (h c) -> (a h) c", c=1)).then_inc(s("weights_in"), 16)
            sp.dma_start(b1c[:, :], b1.rearrange("(h a) -> h a", a=1)).then_inc(s("weights_in"), 16)
            sp.dma_start(w2s[0:HID, :], w2).then_inc(s("weights_in"), 16)
            sp.dma_start(w2s[HID:HID + 1, :], b2.rearrange("(a f) -> a f", a=1)).then_inc(s("weights_in"), 16)

            def store_scans(k):
                view = scans[k][0:EP, :].rearrange("(p t) f -> p t f", t=T)

                def body(it):
                    for h in range(2):
                        sp.wait_ge(s(f"rows_ready{k}_{h}"), it + 1)
                        sp.dma_start(view[:, bass.ds(it * (2 * C) + h * C, C), :], rows[:, h, :, :]).then_inc(s(f"rows_stored{k}_{h}"), 16)
                steps(sp, body)

            def load_carried(k):
                sp.wait_ge(s("carry_sent"), 16 * TURN[k])
                sp.dma_start(tmp[:, 0:J * F], node_rows(carried[k][0:NP, :])).then_inc(s("carried_in"), 16)

            def store_table(k):
                sp.wait_ge(s("normed"), k + 1)
                sp.dma_start(node_rows(table[k]), hn[:, :, :].rearrange("p j f -> p (j f)")).then_inc(s("table_stored"), 16)

            store_table(0)
            store_scans(0)
            load_carried(0)
            store_table(1)

            sp.wait_ge(s("starts_sent"), 16 * J)
            sp.wait_ge(s("heads_in"), 16)
            sp.dma_start(spread[0:EP, :].rearrange("(p t) f -> p t f", t=T)[:, 0, :], head[:, :]).then_inc(s("heads_stored"), 16)
            sp.wait_ge(s("heads_stored"), 16)
            view = spread[0:EP, :].rearrange("(p t) f -> p t f", t=T)

            def load_spread(it):
                for h in range(2):
                    if past(it):
                        sp.wait_ge(s(f"turned_in1_{h}"), it)
                    sp.dma_start(got[:, h, :, :], view[:, bass.ds(it * (2 * C) + h * C, C), :]).then_inc(s(f"spread_in_{h}"), 16)
            steps(sp, load_spread)
            sp.wait_ge(s("adds_done"), 1)
            for k in range(TABLES):
                if k >= 1:
                    sp.wait_ge(s("part_added"), k)
                sp.dma_start(tmp[:, 0:J * FM], node_rows(part[k][0:NP, :])).then_inc(s("part_in"), 16)
            store_table(2)
            store_scans(2)
            load_carried(2)
            store_table(3)
            store_scans(3)
            load_carried(3)
            sp.wait_ge(s("x_done"), 1)
            sp.dma_start(out[0:nfull * J, :].rearrange("(p j) f -> p (j f)", j=J), xv[0:nfull, :]).then_inc(s("out_stored"), 16)
            sp.dma_start(out[nfull * J:N, :].rearrange("(p j) f -> p (j f)", p=1), xv[nfull:nfull + 1, 0:nrest * F]).then_inc(s("out_stored"), 16)
            sp.wait_ge(s("out_stored"), 32)

        @block.gpsimd
        def _(pool):
            pool.memset(ident[:, :], 0.0).then_inc(s("const0"), 1)
            pool.memset(upper[:, :], 1.0).then_inc(s("const0"), 1)
            pool.memset(lower[:, :], 1.0).then_inc(s("const0"), 1)
            pool.iota(ji_i[:, :], pattern=[[1, J]], base=0, channel_multiplier=0).then_inc(s("const1"), 1)
            pool.iota(pi_i[:, :], pattern=[[J, P]], base=0, channel_multiplier=0).then_inc(s("const1"), 1)
            pool.iota(dump_i[:, :], pattern=[[0, 1]], base=NP, channel_multiplier=1).then_inc(s("const1"), 1)
            pool.iota(sdump_i[:, :], pattern=[[1, J]], base=EP, channel_multiplier=J).then_inc(s("const1"), 1)
            pool.wait_ge(s("const0"), 3)
            pool.affine_select(out=ident[:, :], in_=ident[:, :], compare_op=ALU.not_equal, fill=1.0, base=0,
                               pattern=[[-1, P]], channel_multiplier=1).then_inc(s("const1"), 1)
            pool.affine_select(out=upper[:, :], in_=upper[:, :], compare_op=ALU.is_gt, fill=0.0, base=0,
                               pattern=[[1, P]], channel_multiplier=-1).then_inc(s("const1"), 1)
            pool.affine_select(out=lower[:, :], in_=lower[:, :], compare_op=ALU.is_gt, fill=0.0, base=0,
                               pattern=[[-1, P]], channel_multiplier=1).then_inc(s("const1"), 1)

            def gather_edges(k):
                pool.wait_ge(s("table_stored"), 16 * (k + 1))

                def body(it):
                    for h in range(2):
                        pool.wait_ge(s(f"idx_ready{k}_{h}"), it + 1)
                        pool.sem_inc(s("pool_passed"), 1)
                        if past(it):
                            pool.wait_ge(s(f"turned_in{k}_{h}"), it)
                        pool.sem_inc(s("pool_passed"), 1)
                        for t in range(C):
                            pool.indirect_dma_start(got[:, h, t, :], None, table[k], bass.IndirectOffsetOnAxis(ap=idx[:, h, t:t + 1], axis=0)).then_inc(s(f"got{k}_{h}"), 16)
                steps(pool, body)

            def gather_ends(k):
                for h in range(2):
                    pool.wait_ge(s(f"rows_stored{k}_{h}"), 16 * ITERS)
                pool.wait_ge(s("carry_ready"), TURN[k])
                pool.indirect_dma_start(carried[k], bass.IndirectOffsetOnAxis(ap=cidx[:, :], axis=0), carry[:, :], None).then_inc(s("carry_sent"), 16)
                if k == 0:
                    pool.wait_ge(s("places_ready"), 2)
                    pool.wait_ge(s("zeros_stored"), 16 * ZEROED)
                for j in range(J):
                    pool.indirect_dma_start(ag[:, j, :], None, scans[k], bass.IndirectOffsetOnAxis(ap=last_i[:, j:j + 1], axis=0)).then_inc(s("ends_in"), 16)

            pool.wait_ge(s("zeros_stored"), 16 * ZEROED)
            gather_edges(0)
            gather_ends(0)
            pool.wait_ge(s("table_stored"), 16 * 2)
            pool.indirect_dma_start(head[:, :], None, table[1], bass.IndirectOffsetOnAxis(ap=dst0_i[:, :], axis=0)).then_inc(s("heads_in"), 16)
            for j in range(J):
                pool.indirect_dma_start(spread, bass.IndirectOffsetOnAxis(ap=first_i[:, j:j + 1], axis=0), hn[:, j, :], None).then_inc(s("starts_sent"), 16)

            def add_sums(it):
                for h in range(2):
                    for t in range(C):
                        if t == 0:
                            pool.wait_ge(s(f"targets_ready_{h}"), it + 1)
                            pool.sem_inc(s("pool_passed"), 1)
                        if t % (2 * G) == 0:
                            if past((C // (2 * G)) * it + t // (2 * G) + 1):
                                pool.wait_ge(s(f"sums_ready_{h}"), (C // (2 * G)) * it + t // (2 * G) + 1)
                            pool.sem_inc(s("pool_passed"), 1)
                        if past(((2 * it + h) * (C // TABLES) + t // TABLES) * 16):
                            pool.wait_ge(s(f"added_{t % TABLES}"), ((2 * it + h) * (C // TABLES) + t // TABLES) * 16)
                        pool.sem_inc(s("pool_passed"), 1)
                        pool.indirect_dma_start(part[t % TABLES], bass.IndirectOffsetOnAxis(ap=idx[:, h, t:t + 1], axis=0), sums[:, h, t, :], None,
                                                compute_op=ALU.add, oob_is_err=True).then_inc(s(f"added_{t % TABLES}"), 16)
            steps(pool, add_sums)
            for k in range(TABLES):
                pool.wait_ge(s(f"added_{k}"), 16 * T // TABLES)
            pool.memset(dump_i[:, :], 0).then_inc(s("adds_done"), 1)
            for k in (2, 3):
                gather_edges(k)
                gather_ends(k)

        @block.scalar
        def _(act):
            act.wait_ge(s("zeros_set"), 1)
            for k in (0, 2, 3):
                act.dma_start(scans[k][EP:EP + 1, :], zeros[0:1, 0:F]).then_inc(s("zeros_stored"), 16)
            for view, n in ZERO_RUNS:
                for a in range(0, n, 3328):
                    b = min(n, a + 3328)
                    act.dma_start(view[:, a:b], zeros[:, 0:b - a]).then_inc(s("zeros_stored"), 16)

            def root(k):
                act.wait_ge(s("var"), k + 1)
                nc.scalar.activation(st3[:, :], st2[:, :], ACT.Sqrt).then_inc(s("std"), 1)

            def stage_idx(k, it, h):
                if past(it * (16 * C)):
                    act.wait_ge(s(f"got{k}_{h}"), it * (16 * C))
                nc.scalar.activation(idx[:, h, :], src_i[:, bass.ds(it * (2 * C) + h * C, C)], ACT.Copy).then_inc(s(f"idx_ready{k}_{h}"), 1)
                if k == 2:
                    if past((2 * it + h - 1) * (C // G)):
                        act.wait_ge(s("w_spread"), (2 * it + h - 1) * (C // G))
                    nc.scalar.activation(idxf[:, h, :], wgt[:, bass.ds(it * (2 * C) + h * C, C)], ACT.Copy).then_inc(s(f"w_ready_{h}"), 1)

            def set_keep(k, it, h):
                if past(it):
                    act.wait_ge(s(f"scanned{k}_{h}"), it)
                nc.scalar.activation(keep[:, h, :, 1:W1], same[:, bass.ds(it * (2 * C) + h * C, C)].unsqueeze(1).broadcast_to([P, F, C]),
                                     ACT.Copy).then_inc(s(f"keep_ready{k}_{h}"), 1)

            def turn_in(k, it, h, source, per):
                act.wait_ge(s(f"{source}_{h}"), (it + 1) * per)
                nc.scalar.activation(xT[:, h, :, 1:W1], got[:, h, :, :].rearrange("p t f -> p f t"), ACT.Copy).then_inc(s(f"turned_in{k}_{h}"), 1)

            def turn_out(k, it, h):
                act.wait_ge(s(f"scanned{k}_{h}"), it + 1)
                if past(it * 16):
                    act.wait_ge(s(f"rows_stored{k}_{h}"), it * 16)
                nc.scalar.activation(rows[:, h, :, :], sc[:, h, :, 1:W1].rearrange("p f t -> p t f"), ACT.Copy).then_inc(s(f"rows_ready{k}_{h}"), 1)

            def sum_sources(k):
                stage_idx(k, 0, 0)

                def body(it):
                    for h in range(2):
                        stage_idx(k, it + h, 1 - h)
                        set_keep(k, it, h)
                        turn_in(k, it, h, f"got{k}", 16 * C)
                        turn_out(k, it, h)
                steps(act, body)

            def dense(k, width):
                def body(it):
                    for half in range(2):
                        a = half * (NB // 2)
                        act.wait_ge(s(f"turned_ps{k}"), 2 * it + half + 1)
                        if past(2 * it + half):
                            act.wait_ge(s(f"product{k}"), 2 * it + half)
                        for b in range(2):
                            m = (4, 3)[b]
                            nc.scalar.activation(turned[0:width, b * 4 * P:(b * 4 + m) * P], pr[2 * half + b][0:width, 0:m * P], ACT.Copy).then_inc(s(f"turned_sb{k}"), 1)
                body_steps(act, body)

            root(0)
            act.wait_ge(s("src_in"), 32)
            act.wait_ge(s("same_ready"), 1)
            sum_sources(0)
            dense(0, 2 * F)
            root(1)

            act.wait_ge(s("zeros_stored"), 16 * ZEROED)

            def layer1(it):
                for h in range(2):
                    if past(it):
                        act.wait_ge(s(f"srcf_used_{h}"), it)
                    nc.scalar.activation(idxf[:, h, :], src_i[:, bass.ds(it * (2 * C) + h * C, C)], ACT.Copy).then_inc(s(f"srcf_ready_{h}"), 1)
                    set_keep(1, it, h)
                    turn_in(1, it, h, "spread_in", 16)
                for h in range(2):
                    for q in range(TABLES):
                        if past((2 * it + h - 1) * (16 * C // TABLES)):
                            act.wait_ge(s(f"added_{q}"), (2 * it + h - 1) * (16 * C // TABLES))
                    for g in range(C // (2 * G)):
                        if past((2 * it + h) * (C // G) + 2 * g + 2):
                            act.wait_ge(s("eq_used"), (2 * it + h) * (C // G) + 2 * g + 2)
                        nc.scalar.activation(sums[:, h, g * 2 * G:(g + 1) * 2 * G, :].rearrange("p t f -> p (t f)"),
                                             pm[g % 2][:, 0:2 * G * FM], ACT.Copy).then_inc(s(f"sums_ready_{h}"), 1)
            steps(act, layer1)
            root(2)
            act.wait_ge(s("norm2"), 1)
            nc.scalar.activation(share_b[:, 0:T], share_a[:, 0:T], ACT.Sqrt).then_inc(s("norm"), 1)
            act.wait_ge(s("degree"), 1)
            nc.scalar.activation(isd[:, :], rcnt[:, :], ACT.Sqrt).then_inc(s("degree_root"), 1)

            act.wait_ge(s("weights_in"), 16 * 8)

            act.wait_ge(s("wgt_in"), 32)
            stage_idx(2, 0, 0)

            def pair_sums(it, h, b):
                act.wait_ge(s("pairs_summed"), (2 * it + h) * (C // (2 * G)) + b + 1)
                got_sums = pm[b % 2][:, 0:2 * G * PAIR].rearrange("p (t k u) -> p t k u", k=2, u=MUL)
                a = b * 2 * G
                nc.scalar.activation(xT[:, h, 0:MUL, 1 + a:1 + a + 2 * G].rearrange("p u t -> p t u"), got_sums[:, :, 0, :], ACT.Copy).then_inc(s("pairs_out"), 1)
                nc.scalar.activation(sv[:, h, a:a + 2 * G, :], got_sums[:, :, 1, :], ACT.Copy).then_inc(s("pairs_out"), 1)

            def layer2(it):
                for h in range(2):
                    stage_idx(2, it + h, 1 - h)
                    set_keep(2, it, h)
                    cols = bass.ds(it * (2 * C) + h * C, C)
                    act.wait_ge(s(f"got2_{h}"), (it + 1) * (16 * C))
                    nc.scalar.activation(r5[:, h, :, 0:3], rvec[:, cols, :], ACT.Copy).then_inc(s("factors_in"), 1)
                    nc.scalar.activation(r5[:, h, :, 3:5], rvec[:, cols, 0:2], ACT.Copy).then_inc(s("factors_in"), 1)
                    if past(2 * G * (2 * it + h - 1)):
                        act.wait_ge(s("r_used"), C * (2 * it + h - 1))
                    nc.scalar.activation(d16[:, h, :, 0:MUL], got[:, h, :, 0:MUL], ACT.Copy).then_inc(s("factors_in"), 1)
                    for g in range(C // G):
                        n = (2 * it + h) * (C // G) + g
                        if g >= 4 and g % 2 == 0:
                            pair_sums(it, h, g // 2 - 2)
                        if g == 2:
                            if h == 0 and not isinstance(it, int):
                                pair_sums(it - 1, 1, 3)
                            elif h == 1:
                                pair_sums(it, 0, 3)
                        if g == 6:
                            if h == 0 and not isinstance(it, int):
                                turn_out(2, it - 1, 1)
                            elif h == 1:
                                turn_out(2, it, 0)
                        act.wait_ge(s("w_spread"), n + 1)
                        if past(G * (n - 1)):
                            act.wait_ge(s("r_done"), G * (n - 1))
                        nc.scalar.activation(hid[0:HID, g % 2, :], pbc[g % 2][0:HID, :], ACT.Relu, bias=b1c[:, :], scale=w1c[:, :]).then_inc(s("hid_ready"), 1)
                    pair_sums(it, h, 2)
            steps(act, layer2)
            pair_sums(ITERS - 1, 1, 3)
            turn_out(2, ITERS - 1, 1)
            root(3)
            sum_sources(3)
            dense(3, F)

        @block.tensor
        def _(pe):
            pe.wait_ge(s("const1"), 7)

            def histogram(it):
                for h in range(2):
                    for g in range(C // G):
                        n = (2 * it + h) * (C // G) + g
                        pe.wait_ge(s("onehots"), n + 1)
                        for c in range(G):
                            first = h == 0 and g == 0 and c == 0 and isinstance(it, int)
                            ins = nc.tensor.matmul(hist, one_hi[:, g % 2, c, :], one_lo[:, g % 2, c, :], start=first, stop=True, skip_group_check=True)
                        ins.then_inc(s("counted"), 1)
            steps(pe, histogram)
            pe.wait_ge(s("totals"), 1)
            nc.tensor.matmul(pm[0][:, 0:1], upper[:, :], st1[:, 0:1], start=True, stop=True).then_inc(s("offsets_ps"), 1)
            nc.tensor.matmul(pm[1][:, 0:P], dst_f[:, 0:1].broadcast_to([P, P]), ident[:, :], start=True, stop=True).then_inc(s("firsts_ps"), 1)

            def carry_product(k):
                pe.wait_ge(s("tails"), TURN[k])
                nc.tensor.matmul(pm[0][:, 0:F], joins[:, :], tails[:, :], start=True, stop=True).then_inc(s("carry_ps"), 1)

            def dense(k, width, w):
                def body(it):
                    pe.wait_ge(s(f"staged{k}"), it + 1)
                    for half in range(2):
                        if past(it):
                            pe.wait_ge(s(f"finished{k}"), it)
                        for n in range(NB // 2):
                            bank, at = pr[2 * half + n // 4], n % 4
                            ins = nc.tensor.matmul(bank[0:width, at * P:(at + 1) * P], stage[:, half * (NB // 2) + n, 0:width], ident[:, :], start=True, stop=True)
                        ins.then_inc(s(f"turned_ps{k}"), 1)
                        pe.wait_ge(s(f"turned_sb{k}"), 4 * it + 2 * half + 2)
                        for n in range(NB // 2):
                            a = half * (NB // 2) + n
                            ins = nc.tensor.matmul(pm[0][:, a * F:(a + 1) * F], turned[0:width, n * P:(n + 1) * P], w, start=True, stop=True)
                        ins.then_inc(s(f"product{k}"), 1)
                body_steps(pe, body)

            carry_product(0)
            dense(0, 2 * F, w_sage_s[:, :])

            def layer1(it):
                for h in range(2):
                    pe.wait_ge(s(f"srcf_ready_{h}"), it + 1)

                    def spread_sources(g):
                        n = (2 * it + h) * (C // G) + g
                        if past(n - 1):
                            pe.wait_ge(s("eq_ready"), n - 1)
                        for c in range(G):
                            ins = nc.tensor.matmul(pbc[g % 2][:, c * P:(c + 1) * P], idxf[:, h, g * G + c:g * G + c + 1].broadcast_to([P, P]), ident[:, :], start=True, stop=True)
                        ins.then_inc(s("src_spread"), 1)

                    spread_sources(0)
                    for g in range(C // G):
                        if g + 1 < C // G:
                            spread_sources(g + 1)
                        n = (2 * it + h) * (C // G) + g
                        pe.wait_ge(s("eq_ready"), n + 1)
                        if g == 0:
                            pe.wait_ge(s(f"msg_ready_{h}"), it + 1)
                        b = g // 2
                        if g % 2 == 0:
                            if b >= 2:
                                if past((C // (2 * G)) * it + b - 1):
                                    pe.wait_ge(s(f"sums_ready_{h}"), (C // (2 * G)) * it + b - 1)
                            elif h == 1:
                                if past((C // (2 * G)) * (it + 1) - 1 + b):
                                    pe.wait_ge(s("sums_ready_0"), (C // (2 * G)) * (it + 1) - 1 + b)
                            else:
                                if past((C // (2 * G)) * it - 1 + b):
                                    pe.wait_ge(s("sums_ready_1"), (C // (2 * G)) * it - 1 + b)
                        for c in range(G):
                            t = g * G + c
                            ins = nc.tensor.matmul(pm[b % 2][:, (t % (2 * G)) * FM:(t % (2 * G) + 1) * FM], eq[:, g % 2, c * P:(c + 1) * P], msg[:, h, t, :], start=True, stop=True)
                        ins.then_inc(s("eq_used"), 1)
            steps(pe, layer1)

            def layer2(it):
                for h in range(2):
                    pe.wait_ge(s(f"w_ready_{h}"), it + 1)

                    def spread_weights(g):
                        n = (2 * it + h) * (C // G) + g
                        if past(n - 1):
                            pe.wait_ge(s("hid_ready"), n - 1)
                        for c in range(G):
                            ins = nc.tensor.matmul(pbc[g % 2][0:HID, c * P:(c + 1) * P], idxf[:, h, g * G + c:g * G + c + 1].broadcast_to([P, HID]), ident[:, :], start=True, stop=True)
                        ins.then_inc(s("w_spread"), 1)

                    spread_weights(0)
                    for g in range(C // G):
                        if g + 1 < C // G:
                            spread_weights(g + 1)
                        n = (2 * it + h) * (C // G) + g
                        pe.wait_ge(s("hid_ready"), n + 1)
                        for c in range(G):
                            if past(G * (n - 1) + c + 1):
                                pe.wait_ge(s("r_used"), G * (n - 1) + c + 1)
                            nc.tensor.matmul(pr[c][:, 0:384], hid[:, g % 2, c * P:(c + 1) * P], w2p[:, :], start=True, stop=True).then_inc(s("r_done"), 1)
                        if g >= 2 and g % 2 == 0:
                            sum_pairs(it, h, g // 2 - 1)
                        if g == 0 and h == 1:
                            sum_pairs(it, 0, 3)
                        if g == 0 and h == 0 and not isinstance(it, int):
                            sum_pairs(it - 1, 1, 3)

            def sum_pairs(it, h, b):
                n = (2 * it + h) * (C // (2 * G)) + b
                pe.wait_ge(s("r_used"), (n + 1) * 2 * G)
                if past(2 * (n - 1)):
                    pe.wait_ge(s("pairs_out"), 2 * (n - 1))
                for w in range(PAIR):
                    ins = nc.tensor.matmul(pm[b % 2][:, 0:2 * G * PAIR], ident[:, :], pairs_of[b % 2][:, w, :, :].rearrange("p t q -> p (t q)"),
                                           start=w == 0, stop=w == PAIR - 1)
                ins.then_inc(s("pairs_summed"), 1)
            pe.wait_ge(s("w2_ready"), 1)
            steps(pe, layer2)
            sum_pairs(ITERS - 1, 1, 3)
            carry_product(2)
            carry_product(3)
            dense(3, F, w_gcn_s[:, :])

        @block.vector
        def _(dve):
            V = nc.vector
            ch = Chain(dve, "dve_chain")
            V.memset(dst_i, N).then_inc(s("pads_set"), 1)
            V.memset(src_i[:, :], 0).then_inc(s("pads_set"), 1)
            V.memset(wgt[:, :], 0.0).then_inc(s("pads_set"), 1)
            V.memset(rvec[:, :, :], 1.0).then_inc(s("pads_set"), 1)
            V.memset(xs[:, :, :], 0.0).then_inc(s("pads_set"), 1)
            V.memset(hid[:, :, :], 1.0).then_inc(s("pads_set"), 1)
            V.memset(share_b[:, :], 0.0).then_inc(s("zeros_set"), 1)
            ch.do(V.memset(ones[:, :], 1.0), False)
            ch.do(V.memset(keep[:, :, :, :], 0.0), False)
            ch.do(V.memset(xT[:, :, :, :], 0.0), False)
            ch.do(V.memset(sc[:, :, :, :], 0.0))

            def bc(ap, shape, axis):
                return ap.unsqueeze(axis).broadcast_to(shape)

            NJF = [P, J, F]

            def layernorm(k, scaled=False):
                ch.do(V.tensor_reduce(st1[:, :], xs[:, :, :], AX, ALU.add))
                ch.do(V.tensor_scalar(st1[:, :], st1[:, :], 1.0 / F, None, ALU.mult))
                ch.do(V.tensor_tensor(tmpv, xs[:, :, :], bc(st1[:, :], NJF, 2), ALU.subtract))
                ch.do(V.tensor_tensor(hn[:, :, :], tmpv, tmpv, ALU.mult))
                ch.do(V.tensor_reduce(st2[:, :], hn[:, :, :], AX, ALU.add))
                ch.do(V.tensor_scalar(st2[:, :], st2[:, :], 1.0 / F, EPS, ALU.mult, ALU.add))
                dve.sem_inc(s("var"), 1)
                dve.wait_ge(s("std"), k + 1)
                ch.do(V.reciprocal(st3[:, :], st3[:, :]))
                ch.do(V.tensor_tensor(hn[:, :, :], tmpv, bc(st3[:, :], NJF, 2), ALU.mult))
                ch.do(V.tensor_scalar(hn[:, :, :], hn[:, :, :], 0.0, None, ALU.max))
                if k == 2:
                    ch.do(V.tensor_copy(tmpv, hn[:, :, :]))
                    for c, i in enumerate((2, 0, 1)):
                        ch.do(V.tensor_copy(hn[:, :, MUL * (c + 1):MUL * (c + 2)], tmpv[:, :, MUL + i:F:3]), c == 2)
                if k == 3:
                    ch.do(V.tensor_tensor(hn[:, :, :], hn[:, :, :], bc(isd[:, :], NJF, 2), ALU.mult))
                dve.sem_inc(s("normed"), 1)

            dve.wait_ge(s("x_in"), 32)
            layernorm(0)

            dve.wait_ge(s("dst_in"), 32)
            dve.wait_ge(s("const1"), 7)
            ch.do(V.tensor_copy(ji[:, :], ji_i[:, :]), False)
            ch.do(V.tensor_copy(pif[:, :], pi_i[:, :]), False)
            ch.do(V.tensor_copy(dump[:, :], dump_i[:, :]), False)
            ch.do(V.tensor_copy(sdump[:, :], sdump_i[:, :]), False)
            ch.do(V.tensor_copy(dst0_i[:, :], dst_i[:, 0:1]), False)
            ch.do(V.tensor_copy(dst_f[:, :], dst_i))
            ch.do(V.memset(same[:, 0:1], 0.0), False)
            ch.do(V.tensor_tensor(same[:, 1:T], dst_f[:, 1:T], dst_f[:, 0:T - 1], ALU.is_equal))
            dve.sem_inc(s("same_ready"), 1)
            ch.do(V.tensor_scalar(dst_i, dst_f[:, :], 1.0 / J, None, ALU.mult))
            ch.do(V.tensor_copy(hi, dst_i))
            ch.do(V.scalar_tensor_tensor(lo, hi, -float(J), dst_f[:, :], ALU.mult, ALU.add))
            ch.do(V.tensor_scalar(hi, lo, 0.0, float(J), ALU.is_lt, ALU.mult))
            ch.do(V.tensor_tensor(lo, lo, hi, ALU.add))
            ch.do(V.tensor_scalar(hi, lo, float(J), float(J), ALU.is_ge, ALU.mult))
            ch.do(V.tensor_tensor(lo, lo, hi, ALU.subtract))
            ch.do(V.tensor_tensor(hi, dst_f[:, :], lo, ALU.subtract))

            def scan(chain, k, it, h):
                dve.wait_ge(s(f"keep_ready{k}_{h}"), it + 1)
                chain.do(V.tensor_copy(xT[:, h, :, 0], sc[:, 1 - h, :, C]))
                if k != 1:
                    if past(it):
                        dve.wait_ge(s(f"rows_ready{k}_{h}"), it)
                ins = V.tensor_tensor_scan(sc[:, h, :, :].rearrange("p f t -> p (f t)"), keep[:, h, :, :].rearrange("p f t -> p (f t)"),
                                           xT[:, h, :, :].rearrange("p f t -> p (f t)"), 0.0, ALU.mult, ALU.add)
                ins.then_inc(s(f"scanned{k}_{h}"), 1)
                dve.wait_ge(s(f"scanned{k}_{h}"), it + 1)

            c0 = Chain(dve, "dve_layer0", per_step=2)

            def layer0(it):
                c0.step(it)
                for h in range(2):
                    for g in range(C // G):
                        n = (2 * it + h) * (C // G) + g
                        if past(n - 1):
                            dve.wait_ge(s("counted"), n - 1)
                        cols = bass.ds(it * (2 * C) + h * C + g * G, G)
                        V.tensor_tensor(one_hi[:, g % 2, :, :], bc(hi[:, cols], [P, G, P], 2), bc(pif[:, :], [P, G, P], 1), ALU.is_equal)
                        V.tensor_tensor(one_lo[:, g % 2, :, :], bc(lo[:, cols], [P, G, J], 2), bc(ji[:, :], [P, G, J], 1), ALU.is_equal).then_inc(s("onehots"), 1)
                    dve.wait_ge(s(f"turned_in0_{h}"), it + 1)
                    scan(c0, 0, it, h)
            steps(dve, layer0)

            dve.wait_ge(s("counted"), 2 * ITERS * (C // G))
            ch.do(V.tensor_copy(cnt[:, :], hist))
            ch.do(V.tensor_tensor_scan(run[:, :], ones[:, :], cnt[:, :], 0.0, ALU.mult, ALU.add))
            V.tensor_copy(st1[:, 0:1], run[:, J - 1:J]).then_inc(s("totals"), 1)
            dve.wait_ge(s("offsets_ps"), 1)
            ch.do(V.tensor_copy(offs[:, :], pm[0][:, 0:1]))
            ch.do(V.tensor_scalar(last_f[:, :], run[:, :], offs[:, :], 1.0, ALU.add, ALU.subtract), False)
            ch.do(V.tensor_scalar(nzero[:, :], cnt[:, :], 0.0, None, ALU.is_gt))
            ch.do(V.tensor_tensor(first_f[:, :], last_f[:, :], cnt[:, :], ALU.subtract))
            ch.do(V.tensor_scalar(first_f[:, :], first_f[:, :], 1.0, None, ALU.add))
            ch.do(V.tensor_tensor(first_f[:, :], first_f[:, :], sdump[:, :], ALU.subtract))
            ch.do(V.tensor_scalar(last_f[:, :], last_f[:, :], float(EP), None, ALU.subtract))
            ch.do(V.tensor_tensor(first_f[:, :], first_f[:, :], nzero[:, :], ALU.mult), False)
            ch.do(V.tensor_tensor(last_f[:, :], last_f[:, :], nzero[:, :], ALU.mult))
            ch.do(V.tensor_tensor(first_f[:, :], first_f[:, :], sdump[:, :], ALU.add), False)
            ch.do(V.tensor_scalar(last_f[:, :], last_f[:, :], float(EP), None, ALU.add))
            V.tensor_copy(first_i[:, :], first_f[:, :]).then_inc(s("places_ready"), 1)
            V.tensor_copy(last_i[:, :], last_f[:, :]).then_inc(s("places_ready"), 1)
            dve.wait_ge(s("firsts_ps"), 1)
            ch.do(V.scalar_tensor_tensor(joins[:, :], pm[1][:, 0:P], dst_f[:, T - 1:T], upper[:, :], ALU.is_equal, ALU.mult), False)
            ch.do(V.scalar_tensor_tensor(ends_after[:, :], pm[1][:, 0:P], dst_f[:, 0:1], upper[:, :], ALU.is_equal, ALU.mult))
            ch.do(V.tensor_reduce(cidx_f[:, :], ends_after[:, :], AX, ALU.add))
            ch.do(V.tensor_scalar(cidx_f[:, :], cidx_f[:, :], 0.0, None, ALU.is_equal), False)
            ch.do(V.tensor_tensor(cidx_t[:, :], dst_f[:, 0:1], dump[:, :], ALU.subtract))
            ch.do(V.tensor_tensor(cidx_t[:, :], cidx_t[:, :], cidx_f[:, :], ALU.mult))
            ch.do(V.tensor_tensor(cidx_t[:, :], cidx_t[:, :], dump[:, :], ALU.add))
            ch.do(V.tensor_copy(cidx[:, :], cidx_t[:, :]))

            def finish_sums(k):
                ch.do(V.tensor_copy(tails[:, :], sc[:, 1, :, C]))
                dve.sem_inc(s("tails"), 1)
                dve.wait_ge(s("carry_ps"), TURN[k])
                V.tensor_copy(carry[:, :], pm[0][:, 0:F]).then_inc(s("carry_ready"), 1)
                dve.wait_ge(s("carried_in"), 16 * TURN[k])
                dve.wait_ge(s("ends_in"), 16 * J * TURN[k])
                ch.do(V.tensor_tensor(ag[:, :, :], ag[:, :, :], tmpv, ALU.add))

            def dense(k, finish):
                cd = Chain(dve, f"dve_dense{k}", per_step=3)

                def body(it):
                    cd.step(it)
                    js = bass.ds(it * NB, NB)
                    if k == 0:
                        V.tensor_copy(stage[:, :, 0:F], hn[:, js, :])
                        V.tensor_copy(stage[:, :, F:2 * F], ag[:, js, :]).then_inc(s(f"staged{k}"), 1)
                    else:
                        V.tensor_copy(stage[:, :, 0:F], ag[:, js, :]).then_inc(s(f"staged{k}"), 1)
                    dve.wait_ge(s(f"product{k}"), 2 * it + 2)
                    finish(cd, it, js)
                body_steps(dve, body)

            finish_sums(0)
            ch.do(V.tensor_scalar(rcnt[:, :], cnt[:, :], 1.0, None, ALU.max))
            ch.do(V.reciprocal(rcnt[:, :], rcnt[:, :]))
            ch.do(V.tensor_tensor(ag[:, :, :], ag[:, :, :], bc(rcnt[:, :], NJF, 2), ALU.mult))
            dve.wait_ge(s("weights_in"), 16 * 8)
            BN = [P, NB, F]
            tb = tmp[:, 0:NB * F].rearrange("p (j f) -> p j f", f=F)
            pmv = pm[0][:, 0:NB * F].rearrange("p (j f) -> p j f", f=F)

            def sage(cd, it, js):
                cd.do(V.tensor_tensor(tb, pmv, bc(b_sage_s[:, :], BN, 1), ALU.add))
                cd.do(V.tensor_scalar(tb, tb, 0.0, None, ALU.max))
                cd.do(V.tensor_tensor(xs[:, js, :], xs[:, js, :], tb, ALU.add))
                dve.sem_inc(s("finished0"), 1)
            dense(0, sage)
            layernorm(1)

            dve.wait_ge(s("wgt_in"), 32)
            ch.do(V.memset(sc[:, 1, :, C], 0.0))
            c1 = Chain(dve, "dve_layer1", per_step=0)
            PER1 = 2 * (1 + 2 + (C // G) * 3 + 5)
            c1.per = PER1

            def layer1(it):
                c1.step(it)
                for h in range(2):
                    dve.wait_ge(s(f"turned_in1_{h}"), it + 1)
                    scan(c1, 1, it, h)
                    cols = bass.ds(it * (2 * C) + h * C, C)
                    if past((2 * it + h - 1) * (C // G)):
                        dve.wait_ge(s("eq_used"), (2 * it + h - 1) * (C // G))
                    c1.do(V.tensor_tensor(msg[:, h, :, 0:F], sc[:, h, :, 1:W1].rearrange("p f t -> p t f"), bc(wgt[:, cols], [P, C, F], 2), ALU.mult), False)
                    c1.do(V.tensor_copy(msg[:, h, :, F], wgt[:, cols]))
                    dve.sem_inc(s(f"msg_ready_{h}"), 1)
                    dve.wait_ge(s(f"srcf_ready_{h}"), it + 1)
                    for g in range(C // G):
                        n = (2 * it + h) * (C // G) + g
                        dve.wait_ge(s("src_spread"), n + 1)
                        if past(n - 1):
                            dve.wait_ge(s("eq_used"), n - 1)
                        eqv = eq[:, g % 2, :].rearrange("p (c q) -> p c q", q=P)
                        c1.do(V.tensor_tensor(eqv, pbc[g % 2][:, :].rearrange("p (c q) -> p c q", q=P),
                                              bc(idxf[:, h, g * G:(g + 1) * G], [P, G, P], 2), ALU.is_equal))
                        dve.sem_inc(s("eq_ready"), 1)
                        ev = earlier[:, :].rearrange("p (c q) -> p c q", q=P)
                        c1.do(V.tensor_tensor(ev, eqv, bc(lower[:, :], [P, G, P], 1), ALU.mult))
                        c1.do(V.tensor_reduce(dup[:, g * G:(g + 1) * G], ev, AX, ALU.add), g == C // G - 1)
                    c1.do(V.tensor_scalar(widx_f[:, :], idxf[:, h, :], dump[:, :], None, ALU.subtract), False)
                    c1.do(V.tensor_scalar(dup[:, :], dup[:, :], 0.0, None, ALU.is_equal))
                    c1.do(V.tensor_tensor(widx_f[:, :], widx_f[:, :], dup[:, :], ALU.mult))
                    c1.do(V.tensor_scalar(widx_f[:, :], widx_f[:, :], dump[:, :], None, ALU.add))
                    for q in range(TABLES):
                        if past((2 * it + h - 1) * (16 * C // TABLES)):
                            dve.wait_ge(s(f"added_{q}"), (2 * it + h - 1) * (16 * C // TABLES))
                    c1.do(V.tensor_copy(idx[:, h, :], widx_f[:, :]))
                    dve.sem_inc(s(f"targets_ready_{h}"), 1)
                    dve.sem_inc(s(f"srcf_used_{h}"), 1)
                assert c1.n == PER1, c1.n
            steps(dve, layer1)
            sfm = tmp[:, 0:J * FM].rearrange("p (j f) -> p j f", f=FM)
            ch.do(V.memset(ag[:, :, :], 0.0), False)
            ch.do(V.memset(st1[:, :], 0.0))
            for k in range(TABLES):
                dve.wait_ge(s("part_in"), 16 * (k + 1))
                ch.do(V.tensor_tensor(ag[:, :, :], ag[:, :, :], sfm[:, :, 0:F], ALU.add), False)
                ch.do(V.tensor_tensor(st1[:, :], st1[:, :], sfm[:, :, F], ALU.add))
                dve.sem_inc(s("part_added"), 1)
            ch.do(V.tensor_tensor(hn[:, :, :], hn[:, :, :], bc(st1[:, :], NJF, 2), ALU.mult))
            ch.do(V.tensor_tensor(ag[:, :, :], ag[:, :, :], hn[:, :, :], ALU.subtract))
            ch.do(V.tensor_tensor(xs[:, :, :], xs[:, :, :], ag[:, :, :], ALU.add))
            layernorm(2)

            dve.wait_ge(s("attr_in"), 32)
            rt = share_b[:, 0:T]
            ra = share_a[:, 0:T]
            ch.do(V.tensor_tensor(ra, rvec[:, :, 0], rvec[:, :, 0], ALU.mult), False)
            ch.do(V.tensor_tensor(rt, rvec[:, :, 1], rvec[:, :, 1], ALU.mult))
            ch.do(V.tensor_tensor(ra, ra, rt, ALU.add))
            ch.do(V.tensor_tensor(rt, rvec[:, :, 2], rvec[:, :, 2], ALU.mult))
            ch.do(V.tensor_tensor(ra, ra, rt, ALU.add))
            dve.sem_inc(s("norm2"), 1)
            dve.wait_ge(s("norm"), 1)
            ch.do(V.reciprocal(ra, rt))
            ch.do(V.tensor_tensor(rvec[:, :, :], rvec[:, :, :], bc(ra, [P, T, 3], 2), ALU.mult))
            ch.do(V.tensor_scalar(rcnt[:, :], cnt[:, :], 1.0, 1.0, ALU.add, ALU.max))
            dve.sem_inc(s("degree"), 1)
            dve.wait_ge(s("degree_root"), 1)
            ch.do(V.reciprocal(isd[:, :], isd[:, :]))

            y0, y1 = 0.5 / sqrt(pi), sqrt(3.0 / (4.0 * pi))
            norm0 = sqrt(4.0 * pi) / sqrt(2 * MUL)
            norm1 = sqrt(4.0 * pi) * sqrt(3.0) / sqrt(4 * MUL)
            quad = sqrt(1.0 / (24.0 * pi))
            sq = MUL * MUL

            def uv(ap):
                return ap.rearrange("p (u v) -> p u v", v=MUL)

            def pick(k):
                return w2s[:, 3 * sq:6 * sq].rearrange("p (u v k) -> p u v k", v=MUL, k=3)[:, :, :, k]
            coef = w2p[:, :]
            c_vec, c_cross = uv(coef[:, 0:sq]), uv(coef[:, sq:2 * sq])
            pairs = coef[:, 2 * sq:].rearrange("p (k u s v) -> p k u s v", k=2, u=MUL, s=2)
            ch.do(V.tensor_scalar(pairs[:, 0, :, 0, :], uv(w2s[:, 0:sq]), norm0 * y0, None, ALU.mult), False)
            ch.do(V.tensor_scalar(pairs[:, 0, :, 1, :], uv(w2s[:, sq:2 * sq]), norm0 * y1 / sqrt(3), None, ALU.mult), False)
            ch.do(V.tensor_scalar(pairs[:, 1, :, 0, :], uv(w2s[:, 2 * sq:3 * sq]), norm1 * y1 / sqrt(3), None, ALU.mult), False)
            ch.do(V.tensor_scalar(pairs[:, 1, :, 1, :], pick(2), norm1 * 3 * quad, None, ALU.mult), False)
            ch.do(V.tensor_scalar(c_cross, pick(1), norm1 * y1 / sqrt(6), None, ALU.mult), False)
            ch.do(V.tensor_scalar(c_vec, pick(0), norm1 * y0 / sqrt(3), None, ALU.mult), False)
            ch.do(V.tensor_scalar(fr[0:HID + 1, 0:MUL, 0, :], pick(2), -norm1 * quad, None, ALU.mult))
            ch.do(V.tensor_tensor(c_vec, c_vec, fr[0:HID + 1, 0:MUL, 0, :], ALU.add))
            dve.sem_inc(s("w2_ready"), 1)
            ch.do(V.memset(sc[:, 1, :, C], 0.0))

            CV = [P, C, 3, MUL]
            c2 = Chain(dve, "dve_layer2")
            FINISH, HALF = 9, 3 + C + C // 2
            c2.per = 2 * (HALF + FINISH)

            def finish_messages(it, h):
                va = red[:, h, :, 0:VEC // 2].rearrange("p t (u o) -> p t o u", o=3)
                vc = red[:, h, :, VEC // 2:VEC].rearrange("p t (u o) -> p t o u", o=3)
                r = r5[:, h, :, :]
                c2.do(V.tensor_copy(c5[:, :, 0:3, :], vc), False)
                c2.do(V.tensor_copy(c5[:, :, 3:5, :], vc[:, :, 0:2, :]))
                c2.do(V.tensor_tensor(fr, c5[:, :, 2:5, :], bc(r[:, :, 1:4], CV, 3), ALU.mult), False)
                c2.do(V.tensor_tensor(fr2, c5[:, :, 1:4, :], bc(r[:, :, 2:5], CV, 3), ALU.mult))
                c2.do(V.tensor_tensor(fr, fr, fr2, ALU.subtract))
                dve.wait_ge(s("pairs_out"), (2 * it + h + 1) * (C // G))
                c2.do(V.tensor_tensor(fr2, bc(sv[:, h, :, :], CV, 2), bc(r[:, :, 0:3], CV, 3), ALU.mult), False)
                c2.do(V.tensor_tensor(fr, fr, va, ALU.add))
                m1 = xT[:, h, MUL:F, 1:W1].rearrange("p (o u) t -> p t o u", o=3)
                c2.do(V.tensor_tensor(m1, fr, fr2, ALU.add))
                scan(c2, 2, it, h)

            def layer2(it):
                c2.step(it)
                c2.before = 0 if isinstance(it, int) else -FINISH
                for h in range(2):
                    dve.wait_ge(s(f"got2_{h}"), (it + 1) * (16 * C))
                    f1 = got[:, h, :, MUL:F].rearrange("p t (o v) -> p t o v", v=MUL)
                    dve.wait_ge(s("factors_in"), (2 * it + h) * 3 + 3)
                    c2.do(V.tensor_tensor(fr, f1, bc(r5[:, h, :, 0:3], CV, 3), ALU.mult))
                    c2.do(V.tensor_tensor(d16[:, h, :, MUL:], fr[:, :, 0, :], fr[:, :, 1, :], ALU.add))
                    c2.do(V.tensor_tensor(d16[:, h, :, MUL:], d16[:, h, :, MUL:], fr[:, :, 2, :], ALU.add))
                    reduced = {}
                    for t in range(C + 2):
                        if t == C // 4:
                            if h == 1:
                                finish_messages(it, 0)
                            elif not isinstance(it, int):
                                finish_messages(it - 1, 1)
                        if t < C:
                            n = (2 * it + h) * C + t
                            b = t // (2 * G)
                            dve.wait_ge(s("r_done"), n + 1)
                            if t >= 4 and t % 2 == 0:
                                c2.now(reduced[t - 4])
                            if t % (2 * G) == 0:
                                past_sums = (2 * it + h) * (C // (2 * G)) + b - 1
                                if past(past_sums):
                                    dve.wait_ge(s("pairs_summed"), past_sums)
                            bank = pr[t % 4]
                            c2.do(V.tensor_tensor(prod[:, t % 4, :].rearrange("p (u o v) -> p u o v", o=3, v=MUL),
                                                  bc(bank[:, 0:2 * sq].rearrange("p (u v) -> p u v", v=MUL), [P, 2 * MUL, 3, MUL], 2),
                                                  bc(f1[:, t, :, :], [P, 2 * MUL, 3, MUL], 1), ALU.mult), False)
                            V.tensor_tensor(pairs_of[b % 2][:, :, t % (2 * G), :].rearrange("p w q -> p q w"),
                                            bank[:, 2 * sq:6 * sq].rearrange("p (q w) -> p q w", w=PAIR),
                                            bc(d16[:, h, t, :], [P, PAIR, PAIR], 1), ALU.mult).then_inc(s("r_used"), 1)
                        if t >= 3 and t % 2 == 1 or t == C + 1:
                            a = t - 3
                            dve.wait_ge(s("r_used"), (2 * it + h) * C + a + 2)
                            reduced[a] = c2.do(V.tensor_reduce(red[:, h, a:a + 2, :].rearrange("p t q -> p (t q)"),
                                                               prod[:, a % 4:a % 4 + 2, :].rearrange("p s (q v) -> p (s q) v", v=MUL), AX, ALU.add), t == C + 1)
                    dve.sem_inc(s(f"turned_in2_{h}"), 1)
                assert c2.n == c2.per - (FINISH if isinstance(it, int) else 0), c2.n
            steps(dve, layer2)
            c2.step(ITERS)
            finish_messages(ITERS - 1, 1)
            finish_sums(2)
            ch.do(V.tensor_tensor(xs[:, :, 0:MUL], xs[:, :, 0:MUL], ag[:, :, 0:MUL], ALU.add), False)
            for c, i in enumerate((2, 0, 1)):
                ch.do(V.tensor_tensor(xs[:, :, MUL + i:F:3], xs[:, :, MUL + i:F:3], ag[:, :, MUL * (c + 1):MUL * (c + 2)], ALU.add), c == 2)

            layernorm(3)
            ch.do(V.memset(sc[:, 1, :, C], 0.0))
            c3 = Chain(dve, "dve_layer3", per_step=2)

            def layer3(it):
                c3.step(it)
                for h in range(2):
                    dve.wait_ge(s(f"turned_in3_{h}"), it + 1)
                    scan(c3, 3, it, h)
            steps(dve, layer3)
            finish_sums(3)
            ch.do(V.tensor_tensor(ag[:, :, :], ag[:, :, :], hn[:, :, :], ALU.add))
            ch.do(V.tensor_tensor(ag[:, :, :], ag[:, :, :], bc(isd[:, :], NJF, 2), ALU.mult))

            def gcn(cd, it, js):
                cd.do(V.tensor_tensor(tb, pmv, bc(b_gcn_s[:, :], BN, 1), ALU.add))
                cd.do(V.tensor_scalar(tb, tb, 0.0, None, ALU.max))
                cd.do(V.tensor_tensor(xs[:, js, :], xs[:, js, :], tb, ALU.add))
                dve.sem_inc(s("finished3"), 1)
            dense(3, gcn)
            dve.sem_inc(s("x_done"), 1)


_INS = ["x", "src", "dst", "edge_attr_3", "edge_weight", "L0_gnn_W", "L0_gnn_b", "L2_gnn_w1", "L2_gnn_b1", "L2_gnn_w2", "L2_gnn_b2", "L3_gnn_W", "L3_gnn_bias"]


def kernel(**inputs):
    import numpy as np
    import concourse.bacc as bacc
    from concourse import mybir as mb
    from concourse.bass_utils import run_bass_kernel_spmd

    nc = bacc.Bacc("TRN2", target_bir_lowering=False, num_devices=1)
    arrays, args = {}, []
    for name in _INS:
        a = np.ascontiguousarray(inputs[name])
        arrays[f"in_{name}"] = a
        args.append(nc.dram_tensor(f"in_{name}", a.shape, mb.dt.from_np(a.dtype), kind="ExternalInput").ap())
    args.append(nc.dram_tensor("out_x", (N, F), mb.dt.float32, kind="ExternalOutput").ap())
    gnn_program(nc, *args)
    result = run_bass_kernel_spmd(nc, [arrays], core_ids=[0])
    return result.results[0]["out_x"]
```

```python
import concourse.bass as bass
from concourse import mybir
from contextlib import ExitStack
from math import pi, sqrt

fp32 = mybir.dt.float32
bf16 = mybir.dt.bfloat16
i32 = mybir.dt.int32
ALU = mybir.AluOpType
ACT = mybir.ActivationFunctionType
AX = mybir.AxisListType.X

P = 128
N, F = 12500, 32
E = 212500
J = -(-N // P)
NP = P * J
C = 32
ITERS = -(-E // (P * C * 2))
T = ITERS * 2 * C
EP = P * T
W1 = C + 1
FM = F + 1
TABLES = 4
REC = 6
PARTS = 4
G = 4
HID = 64
MUL = 8
NB = 14
BLOCKS = J // NB
TURN = {0: 1, 2: 2, 3: 3}
OLD = {k: (TURN[k] - 1) * ITERS for k in TURN}
EPS = 1e-5


def gnn_program(nc, x, src, dst, attr, weight, w_sage, b_sage, w1, b1, w2, b2, w_gcn, b_gcn, out):
    ctx = ExitStack()

    def sb(name, shape, dt=fp32):
        return ctx.enter_context(nc.sbuf_tensor(name, shape, dt))

    def pb(name):
        return ctx.enter_context(nc.psum_tensor(name, [P, 512], fp32))

    def sem(name):
        return ctx.enter_context(nc.semaphore(name))

    def dram(name, shape, dt=fp32):
        return nc.dram_tensor(name, shape, dt, kind="Internal").ap()

    with ctx:
        table = [dram(f"node_table{k}", (NP, F)) for k in range(4)]
        scans = {k: dram(f"edge_scans{k}", (EP + 1, F)) for k in (0, 2, 3)}
        spread = dram("edge_spread", (EP + NP, F))
        carried = {k: dram(f"carried{k}", (NP + P, F)) for k in (0, 2, 3)}
        cursor = dram("cursor", (NP + P, 1))
        records = dram("records", (EP, REC))
        part = [dram(f"source_sums{k}", (NP + P, FM)) for k in range(TABLES)]

        src_i = sb("src_i", [P, T + C], i32)
        wgt = sb("wgt", [P, T + C])
        dst_f = sb("dst_f", [P, T])
        same = sb("same", [P, T])
        rvec = sb("rvec", [P, T, 3])
        share_a = sb("share_a", [P, 2 * T])
        lo, hi = share_a[:, 0:T], share_a[:, T:2 * T]
        share_b = sb("share_b", [P, 3328])
        zeros = share_b[:, :]
        xs = sb("xs", [P, J, F])
        hn = sb("hn", [P, J, F])
        ag = sb("ag", [P, J, F])
        tmp = sb("tmp", [P, J * FM])
        tmpv = tmp[:, 0:J * F].rearrange("p (j f) -> p j f", f=F)
        got = sb("got", [P, 2, C, F])
        xT = sb("xT", [P, 2, F, W1])
        keep = sb("keep", [P, 2, F, W1])
        sc = sb("sc", [P, 2, F, W1])
        rows = sb("rows", [P, 2, C, F])
        dst_i = rows[:, :, :, :].rearrange("p h t f -> p (h t f)").bitcast(i32)[:, 0:T]
        idx = sb("idx", [P, 2, C], i32)
        idxf = sb("idxf", [P, 2, C])
        msg = share_a[:, 0:2 * C * FM].rearrange("p (h t f) -> p h t f", h=2, f=FM)
        sums = share_b[:, 0:2 * C * FM].rearrange("p (h t f) -> p h t f", h=2, f=FM)
        share_c = sb("share_c", [P, 15 * C * MUL])
        part_in = [tmp, share_a, share_b, share_c]
        eq = share_c[:, 0:2 * G * P].rearrange("p (h q) -> p h q", h=2)
        earlier = share_c[:, 2 * G * P:3 * G * P]
        dup = sb("dup", [P, C])
        widx_f = sb("widx_f", [P, C])
        VEC, PAIR = 6 * MUL, 2 * MUL
        red = share_a[:, 0:2 * C * VEC].rearrange("p (h t q) -> p h t q", h=2, q=VEC)
        prod = share_b[:, 0:4 * VEC * MUL].rearrange("p (s q) -> p s q", q=VEC * MUL)
        pairs_of = [tile.rearrange("p (w t q) -> p w t q", w=PAIR, q=PAIR)
                    for tile in (tmp[:, 0:2 * G * PAIR * PAIR],
                                 ag[:, :, :].rearrange("p j f -> p (j f)")[:, 0:2 * G * PAIR * PAIR])]
        CM = C * MUL
        d16 = share_c[:, 0:4 * CM].rearrange("p (h t v) -> p h t v", h=2, t=C)
        fr = share_c[:, 4 * CM:7 * CM].rearrange("p (t o v) -> p t o v", t=C, o=3)
        fr2 = share_c[:, 7 * CM:10 * CM].rearrange("p (t o v) -> p t o v", t=C, o=3)
        c5 = share_c[:, 10 * CM:15 * CM].rearrange("p (t o v) -> p t o v", t=C, o=5)
        r5 = sb("r5", [P, 2, C, 5])
        sv = sb("sv", [P, 2, C, MUL])
        hid = sb("hid", [HID + 1, 2, G * P])
        w2s = sb("w2s", [HID + 1, 384])
        w2p = sb("w2p", [HID + 1, 384])
        w1c = sb("w1c", [HID, 1])
        b1c = sb("b1c", [HID, 1])
        one_lo = sb("one_lo", [P, 2, G, J], bf16)
        one_hi = sb("one_hi", [P, 2, G, P], bf16)
        ident = sb("ident", [P, P])
        upper = sb("upper", [P, P])
        lower = sb("lower", [P, P])
        joins = sb("joins", [P, P])
        ends_after = sb("ends_after", [P, P])
        ji_i = sb("ji_i", [P, J], i32)
        ji = sb("ji", [P, J])
        pi_i = sb("pi_i", [P, P], i32)
        pif = sb("pif", [P, P])
        dump_i = sb("dump_i", [P, 1], i32)
        dump = sb("dump", [P, 1])
        cnt = sb("cnt", [P, J])
        run = sb("run", [P, J])
        first_f = sb("first_f", [P, J])
        last_f = sb("last_f", [P, J])
        nzero = sb("nzero", [P, J])
        sdump_i = sb("sdump_i", [P, J], i32)
        sdump = sb("sdump", [P, J])
        first_i = sb("first_i", [P, J], i32)
        last_i = sb("last_i", [P, J], i32)
        rcnt = sb("rcnt", [P, J])
        isd = sb("isd", [P, J])
        st1 = sb("st1", [P, J])
        st2 = sb("st2", [P, J])
        st3 = sb("st3", [P, J])
        ones = sb("ones", [P, J])
        offs = sb("offs", [P, 1])
        cidx_f = sb("cidx_f", [P, 1])
        cidx_t = sb("cidx_t", [P, 1])
        cidx = sb("cidx", [P, 1], i32)
        dst0_i = sb("dst0_i", [P, 1], i32)
        tails = sb("tails", [P, F])
        disorder = sb("disorder", [P, 3])
        unsorted = sb("unsorted", [1, 1], i32)
        rec = sb("rec", [P, REC])
        node_i = sb("node_i", [P, 1], i32)
        place = sb("place", [P, 1])
        place_i = sb("place_i", [P, 1], i32)
        next_place = sb("next_place", [P, 1])
        rank = sb("rank", [P, 2])
        target = sb("target", [P, 1])
        target_i = sb("target_i", [P, 1], i32)
        carry = sb("carry", [P, F])
        head = sb("head", [P, F])
        stage = share_c[:, 0:NB * 2 * F].rearrange("p (j f) -> p j f", j=NB)
        turned = share_c[0:2 * F, NB * 2 * F:NB * (2 * F + P // 2)]
        w_sage_s = sb("w_sage_s", [2 * F, F])
        w_gcn_s = sb("w_gcn_s", [F, F])
        b_sage_s = sb("b_sage_s", [P, F])
        b_gcn_s = sb("b_gcn_s", [P, F])

        pbc = [pb(f"pbc{k}") for k in range(2)]
        pr = [pb(f"pr{k}") for k in range(4)]
        pm = [pb(f"pm{k}") for k in range(2)]
        hist = pr[0][:, 0:J]

        S = {}

        def s(name):
            if name not in S:
                S[name] = sem(name)
            return S[name]

        def past(value):
            return not isinstance(value, int) or value > 0

        def steps(eng, body):
            body(0)
            with eng.Fori(1, ITERS) as it:
                body(it)

        class Chain:

            def __init__(self, eng, name, per_step=0, before=0):
                self.eng, self.name, self.per, self.n, self.before, self.it = eng, name, per_step, 0, before, 0

            def step(self, it):
                self.it, self.n = it, 0

            def do(self, ins, wait_now=True):
                self.n += 1
                ins.then_inc(s(self.name), 1)
                if wait_now:
                    self.now()
                return self.n

            def now(self, n=None):
                self.eng.wait_ge(s(self.name), self.it * self.per + (self.n if n is None else n) + self.before)

        def node_rows(t):
            return t.rearrange("(p j) f -> p (j f)", p=P)

        ZERO_RUNS = [(spread[0:EP, :].rearrange("(p t) f -> p (t f)", p=P), T * F)]
        for k in range(TABLES):
            ZERO_RUNS.append((part[k].rearrange("(p j) f -> p (j f)", p=P), (NP + P) // P * FM))
        for k in (0, 2, 3):
            ZERO_RUNS.append((carried[k].rearrange("(p j) f -> p (j f)", p=P), (NP + P) // P * F))
        ZEROED = sum(-(-n // 3328) for _, n in ZERO_RUNS) + 3

        block = ctx.enter_context(nc.Block())

        @block.sync
        def _(sp):
            sp.wait_ge(s("pads_set"), 6)
            def load_padded(name, tile, src_ap, width):
                full, rest = src_ap.shape[0] // width, src_ap.shape[0] % width
                most = full // 16 * 16
                for a, b in ((0, most), (most, full)):
                    sp.dma_start(tile[a:b, 0:width], src_ap[a * width:b * width].rearrange("(p t) -> p t", t=width)).then_inc(s(name), 16)
                sp.dma_start(tile[full:full + 1, 0:rest], src_ap[full * width:].rearrange("(p t) -> p t", p=1)).then_inc(s(name), 16)

            nfull, nrest = N // J, N % J
            xv = xs[:, :, :].rearrange("p j f -> p (j f)")
            load_padded("x_in", xv, x.rearrange("n f -> (n f)"), J * F)
            load_padded("dst_in", dst_i, dst, T)
            load_padded("src_in", src_i, src, T)
            load_padded("wgt_in", wgt, weight, T)
            load_padded("attr_in", rvec[:, :, :].rearrange("p t c -> p (t c)"), attr.rearrange("e c -> (e c)"), 3 * T)
            sp.dma_start(w_sage_s[:, :], w_sage).then_inc(s("weights_in"), 16)
            sp.dma_start(w_gcn_s[:, :], w_gcn.rearrange("o i -> i o"), allow_slow_non_contiguous=True).then_inc(s("weights_in"), 16)
            sp.dma_start(b_sage_s[:, :], b_sage.rearrange("(a f) -> a f", a=1).broadcast_to([P, F])).then_inc(s("weights_in"), 16)
            sp.dma_start(b_gcn_s[:, :], b_gcn.rearrange("(a f) -> a f", a=1).broadcast_to([P, F])).then_inc(s("weights_in"), 16)
            sp.dma_start(w1c[:, :], w1.rearrange("a (h c) -> (a h) c", c=1)).then_inc(s("weights_in"), 16)
            sp.dma_start(b1c[:, :], b1.rearrange("(h a) -> h a", a=1)).then_inc(s("weights_in"), 16)
            sp.dma_start(w2s[0:HID, :], w2).then_inc(s("weights_in"), 16)
            sp.dma_start(w2s[HID:HID + 1, :], b2.rearrange("(a f) -> a f", a=1)).then_inc(s("weights_in"), 16)

            sp.wait_ge(s("order_known"), 1)
            with sp.If(sp.value_load(unsorted[0:1, 0:1], min_val=0, max_val=1)):
                sp.wait_ge(s("sort_cursors"), 1)
                sp.dma_start(cursor[0:NP, :].rearrange("(p j) c -> p (j c)", p=P), first_f[:, :]).then_inc(s("sort_cursors_stored"), 16)
                sp.wait_ge(s("sort_moved"), 32 * T)
                for q in range(PARTS):
                    if q >= 1:
                        sp.wait_ge(s("sort_unpacked"), q)
                    n = T // PARTS
                    sp.dma_start(share_a[:, 0:n * REC], records.rearrange("(p t) c -> p (t c)", p=P)[:, q * n * REC:(q + 1) * n * REC]).then_inc(s("sort_back"), 16)

            def store_scans(k):
                view = scans[k][0:EP, :].rearrange("(p t) f -> p t f", t=T)

                def body(it):
                    for h in range(2):
                        sp.wait_ge(s(f"rows_ready_{h}"), OLD[k] + it + 1)
                        sp.dma_start(view[:, bass.ds(it * (2 * C) + h * C, C), :], rows[:, h, :, :]).then_inc(s(f"rows_stored_{h}"), 16)
                steps(sp, body)

            def load_carried(k):
                sp.wait_ge(s("carry_sent"), 16 * TURN[k])
                sp.dma_start(tmp[:, 0:J * F], node_rows(carried[k][0:NP, :])).then_inc(s("carried_in"), 16)

            def store_table(k):
                for b in range(BLOCKS):
                    sp.wait_ge(s("normed"), BLOCKS * k + b + 1)
                    sp.dma_start(table[k].rearrange("(p j) f -> p j f", p=P)[:, b * NB:(b + 1) * NB, :], hn[:, b * NB:(b + 1) * NB, :]).then_inc(s("table_stored"), 16)

            store_table(0)
            store_scans(0)
            load_carried(0)
            store_table(1)

            sp.wait_ge(s("starts_sent"), 16 * J)
            sp.wait_ge(s("heads_in"), 16)
            sp.dma_start(spread[0:EP, :].rearrange("(p t) f -> p t f", t=T)[:, 0, :], head[:, :]).then_inc(s("heads_stored"), 16)
            sp.wait_ge(s("heads_stored"), 16)
            view = spread[0:EP, :].rearrange("(p t) f -> p t f", t=T)

            def load_spread(it):
                for h in range(2):
                    sp.wait_ge(s(f"turned_in_{h}"), ITERS + it)
                    sp.dma_start(got[:, h, :, :], view[:, bass.ds(it * (2 * C) + h * C, C), :]).then_inc(s(f"spread_in_{h}"), 16)
            steps(sp, load_spread)
            sp.wait_ge(s("adds_done"), 1)
            for k in range(TABLES):
                sp.dma_start(part_in[k][:, 0:J * FM], node_rows(part[k][0:NP, :])).then_inc(s(f"part_in{k}"), 16)
            store_table(2)
            store_scans(2)
            load_carried(2)
            store_table(3)
            store_scans(3)
            load_carried(3)
            for b in range(BLOCKS):
                lo_c, hi_c = b * NB * F, (b + 1) * NB * F
                sp.wait_ge(s("x_done"), b + 1)
                sp.dma_start(out[0:nfull * J, :].rearrange("(p j) f -> p (j f)", j=J)[:, lo_c:hi_c], xv[0:nfull, lo_c:hi_c]).then_inc(s("out_stored"), 16)
                if lo_c < nrest * F:
                    top = min(hi_c, nrest * F)
                    sp.dma_start(out[nfull * J:N, :].rearrange("(p j) f -> p (j f)", p=1)[:, lo_c:top], xv[nfull:nfull + 1, lo_c:top]).then_inc(s("out_stored"), 16)
            sp.wait_ge(s("out_stored"), 16 * (BLOCKS + -(-nrest // NB)))

        @block.gpsimd
        def _(pool):
            pool.memset(ident[:, :], 0.0).then_inc(s("const0"), 1)
            pool.memset(upper[:, :], 1.0).then_inc(s("const0"), 1)
            pool.memset(lower[:, :], 1.0).then_inc(s("const0"), 1)
            pool.iota(ji_i[:, :], pattern=[[1, J]], base=0, channel_multiplier=0).then_inc(s("const1"), 1)
            pool.iota(pi_i[:, :], pattern=[[J, P]], base=0, channel_multiplier=0).then_inc(s("const1"), 1)
            pool.iota(dump_i[:, :], pattern=[[0, 1]], base=NP, channel_multiplier=1).then_inc(s("const1"), 1)
            pool.iota(sdump_i[:, :], pattern=[[1, J]], base=EP, channel_multiplier=J).then_inc(s("const1"), 1)
            pool.wait_ge(s("const0"), 3)
            pool.affine_select(out=ident[:, :], in_=ident[:, :], compare_op=ALU.not_equal, fill=1.0, base=0,
                               pattern=[[-1, P]], channel_multiplier=1).then_inc(s("const1"), 1)
            pool.affine_select(out=upper[:, :], in_=upper[:, :], compare_op=ALU.is_gt, fill=0.0, base=0,
                               pattern=[[1, P]], channel_multiplier=-1).then_inc(s("const1"), 1)
            pool.affine_select(out=lower[:, :], in_=lower[:, :], compare_op=ALU.is_gt, fill=0.0, base=0,
                               pattern=[[-1, P]], channel_multiplier=1).then_inc(s("const1"), 1)

            pool.wait_ge(s("order_known"), 1)
            with pool.If(pool.value_load(unsorted[0:1, 0:1], min_val=0, max_val=1)):
                pool.wait_ge(s("sort_cursors_stored"), 16)
                with pool.Fori(0, T) as t:
                    pool.wait_ge(s("sort_staged"), t + 1)
                    pool.sem_inc(s("pool_passed"), 1)
                    pool.indirect_dma_start(place[:, :], None, cursor[0:NP, :], bass.IndirectOffsetOnAxis(ap=node_i[:, :], axis=0)).then_inc(s("sort_cursor_in"), 16)
                    pool.wait_ge(s("sort_placed"), t + 1)
                    pool.sem_inc(s("pool_passed"), 1)
                    pool.indirect_dma_start(records, bass.IndirectOffsetOnAxis(ap=place_i[:, :], axis=0), rec[:, :], None).then_inc(s("sort_moved"), 16)
                    pool.indirect_dma_start(cursor, bass.IndirectOffsetOnAxis(ap=target_i[:, :], axis=0), next_place[:, :], None).then_inc(s("sort_moved"), 16)
                    pool.wait_ge(s("sort_moved"), 32 * (t + 1))
                    pool.sem_inc(s("pool_passed"), 1)

            def gather_edges(k):
                pool.wait_ge(s("table_stored"), 16 * BLOCKS * (k + 1))

                def body(it):
                    for h in range(2):
                        pool.wait_ge(s(f"idx_ready{k}_{h}"), it + 1)
                        pool.sem_inc(s("pool_passed"), 1)
                        if past(k * ITERS + it):
                            pool.wait_ge(s(f"turned_in_{h}"), k * ITERS + it)
                        pool.sem_inc(s("pool_passed"), 1)
                        for t in range(C):
                            pool.indirect_dma_start(got[:, h, t, :], None, table[k], bass.IndirectOffsetOnAxis(ap=idx[:, h, t:t + 1], axis=0)).then_inc(s(f"got{k}_{h}"), 16)
                steps(pool, body)

            def gather_ends(k):
                for h in range(2):
                    pool.wait_ge(s(f"rows_stored_{h}"), 16 * (OLD[k] + ITERS))
                pool.wait_ge(s("carry_ready"), TURN[k])
                if k == 0:
                    pool.wait_ge(s("places_ready"), 2)
                    pool.wait_ge(s("zeros_stored"), 16 * ZEROED)
                pool.indirect_dma_start(carried[k], bass.IndirectOffsetOnAxis(ap=cidx[:, :], axis=0), carry[:, :], None).then_inc(s("carry_sent"), 16)
                for j in range(J):
                    pool.indirect_dma_start(ag[:, j, :], None, scans[k], bass.IndirectOffsetOnAxis(ap=last_i[:, j:j + 1], axis=0)).then_inc(s(f"ends_in_{j // NB}"), 16)

            gather_edges(0)
            gather_ends(0)
            for j in range(J):
                if j % NB == 0:
                    pool.wait_ge(s("normed"), BLOCKS + j // NB + 1)
                if j == J - NB:
                    pool.wait_ge(s("table_stored"), 16 * BLOCKS * 2)
                    pool.indirect_dma_start(head[:, :], None, table[1], bass.IndirectOffsetOnAxis(ap=dst0_i[:, :], axis=0)).then_inc(s("heads_in"), 16)
                pool.indirect_dma_start(spread, bass.IndirectOffsetOnAxis(ap=first_i[:, j:j + 1], axis=0), hn[:, j, :], None).then_inc(s("starts_sent"), 16)

            def add_sums(it):
                for h in range(2):
                    for t in range(C):
                        if t == 0:
                            pool.wait_ge(s(f"targets_ready_{h}"), it + 1)
                            pool.sem_inc(s("pool_passed"), 1)
                        if t % (2 * G) == 0:
                            if past((C // (2 * G)) * it + t // (2 * G) + 1):
                                pool.wait_ge(s(f"sums_ready_{h}"), (C // (2 * G)) * it + t // (2 * G) + 1)
                            pool.sem_inc(s("pool_passed"), 1)
                        if past(((2 * it + h) * (C // TABLES) + t // TABLES) * 16):
                            pool.wait_ge(s(f"added_{t % TABLES}"), ((2 * it + h) * (C // TABLES) + t // TABLES) * 16)
                        pool.sem_inc(s("pool_passed"), 1)
                        pool.indirect_dma_start(part[t % TABLES], bass.IndirectOffsetOnAxis(ap=idx[:, h, t:t + 1], axis=0), sums[:, h, t, :], None,
                                                compute_op=ALU.add, oob_is_err=True).then_inc(s(f"added_{t % TABLES}"), 16)
            steps(pool, add_sums)
            for k in range(TABLES):
                pool.wait_ge(s(f"added_{k}"), 16 * T // TABLES)
            pool.memset(dump_i[:, :], 0).then_inc(s("adds_done"), 1)
            for k in (2, 3):
                gather_edges(k)
                gather_ends(k)

        @block.scalar
        def _(act):
            def store_zeros():
                act.wait_ge(s("zeros_set"), 1)
                for k in (0, 2, 3):
                    act.dma_start(scans[k][EP:EP + 1, :], zeros[0:1, 0:F]).then_inc(s("zeros_stored"), 16)
                for view, n in ZERO_RUNS:
                    for a in range(0, n, 3328):
                        b = min(n, a + 3328)
                        act.dma_start(view[:, a:b], zeros[:, 0:b - a]).then_inc(s("zeros_stored"), 16)

            def root(k, b):
                js = slice(b * NB, (b + 1) * NB)
                act.wait_ge(s("var"), BLOCKS * k + b + 1)
                nc.scalar.activation(st3[:, js], st2[:, js], ACT.Sqrt).then_inc(s("std"), 1)

            def stage_idx(k, it, h):
                if past(it * (16 * C)):
                    act.wait_ge(s(f"got{k}_{h}"), it * (16 * C))
                nc.scalar.activation(idx[:, h, :], src_i[:, bass.ds(it * (2 * C) + h * C, C)], ACT.Copy).then_inc(s(f"idx_ready{k}_{h}"), 1)
                if k == 2:
                    if past((2 * it + h - 1) * (C // G)):
                        act.wait_ge(s("w_spread"), (2 * it + h - 1) * (C // G))
                    nc.scalar.activation(idxf[:, h, :], wgt[:, bass.ds(it * (2 * C) + h * C, C)], ACT.Copy).then_inc(s(f"w_ready_{h}"), 1)

            def set_keep(k, it, h):
                if past(k * ITERS + it):
                    act.wait_ge(s(f"scanned_{h}"), k * ITERS + it)
                nc.scalar.activation(keep[:, h, :, 1:W1], same[:, bass.ds(it * (2 * C) + h * C, C)].unsqueeze(1).broadcast_to([P, F, C]),
                                     ACT.Copy).then_inc(s(f"keep_ready_{h}"), 1)

            def turn_in(k, it, h, source, per):
                act.wait_ge(s(f"{source}_{h}"), (it + 1) * per)
                nc.scalar.activation(xT[:, h, :, 1:W1], got[:, h, :, :].rearrange("p t f -> p f t"), ACT.Copy).then_inc(s(f"turned_in_{h}"), 1)

            def turn_out(k, it, h):
                act.wait_ge(s(f"scanned_{h}"), k * ITERS + it + 1)
                if past(OLD[k] + it):
                    act.wait_ge(s(f"rows_stored_{h}"), (OLD[k] + it) * 16)
                nc.scalar.activation(rows[:, h, :, :], sc[:, h, :, 1:W1].rearrange("p f t -> p t f"), ACT.Copy).then_inc(s(f"rows_ready_{h}"), 1)

            def sum_sources(k):
                stage_idx(k, 0, 0)
                if k == 0:
                    store_zeros()

                def body(it):
                    for h in range(2):
                        stage_idx(k, it + h, 1 - h)
                        set_keep(k, it, h)
                        turn_in(k, it, h, f"got{k}", 16 * C)
                        turn_out(k, it, h)
                steps(act, body)

            def dense(k, width):
                for it in range(BLOCKS):
                    for half in range(2):
                        act.wait_ge(s(f"turned_ps{k}"), 2 * it + half + 1)
                        if past(2 * it + half):
                            act.wait_ge(s(f"product{k}"), 2 * it + half)
                        for b in range(2):
                            m = (4, 3)[b]
                            nc.scalar.activation(turned[0:width, b * 4 * P:(b * 4 + m) * P], pr[2 * half + b][0:width, 0:m * P], ACT.Copy).then_inc(s(f"turned_sb{k}"), 1)
                    if k == 0:
                        root(1, it)

            for b in range(BLOCKS):
                root(0, b)
            act.wait_ge(s("src_in"), 48)
            act.wait_ge(s("same_ready"), 1)
            sum_sources(0)
            dense(0, 2 * F)
            act.wait_ge(s("zeros_stored"), 16 * ZEROED)
            act.wait_ge(s("norm2"), 1)
            nc.scalar.activation(share_b[:, 0:T], share_a[:, 0:T], ACT.Sqrt).then_inc(s("norm"), 1)
            act.wait_ge(s("degree"), 1)
            nc.scalar.activation(isd[:, :], rcnt[:, :], ACT.Sqrt).then_inc(s("degree_root"), 1)


            def layer1(it):
                for h in range(2):
                    if past(it):
                        act.wait_ge(s(f"srcf_used_{h}"), it)
                    nc.scalar.activation(idxf[:, h, :], src_i[:, bass.ds(it * (2 * C) + h * C, C)], ACT.Copy).then_inc(s(f"srcf_ready_{h}"), 1)
                    set_keep(1, it, h)
                    turn_in(1, it, h, "spread_in", 16)
                for h in range(2):
                    for q in range(TABLES):
                        if past((2 * it + h - 1) * (16 * C // TABLES)):
                            act.wait_ge(s(f"added_{q}"), (2 * it + h - 1) * (16 * C // TABLES))
                    for g in range(C // (2 * G)):
                        if past((2 * it + h) * (C // G) + 2 * g + 2):
                            act.wait_ge(s("eq_used"), (2 * it + h) * (C // G) + 2 * g + 2)
                        nc.scalar.activation(sums[:, h, g * 2 * G:(g + 1) * 2 * G, :].rearrange("p t f -> p (t f)"),
                                             pm[g % 2][:, 0:2 * G * FM], ACT.Copy).then_inc(s(f"sums_ready_{h}"), 1)
            steps(act, layer1)
            for b in range(BLOCKS):
                root(2, b)
            act.wait_ge(s("weights_in"), 16 * 8)

            act.wait_ge(s("wgt_in"), 48)
            stage_idx(2, 0, 0)

            def pair_sums(it, h, b):
                act.wait_ge(s("pairs_summed"), (2 * it + h) * (C // (2 * G)) + b + 1)
                got_sums = pm[b % 2][:, 0:2 * G * PAIR].rearrange("p (t k u) -> p t k u", k=2, u=MUL)
                a = b * 2 * G
                nc.scalar.activation(xT[:, h, 0:MUL, 1 + a:1 + a + 2 * G].rearrange("p u t -> p t u"), got_sums[:, :, 0, :], ACT.Copy).then_inc(s("pairs_out"), 1)
                nc.scalar.activation(sv[:, h, a:a + 2 * G, :], got_sums[:, :, 1, :], ACT.Copy).then_inc(s("pairs_out"), 1)

            def layer2(it):
                for h in range(2):
                    stage_idx(2, it + h, 1 - h)
                    set_keep(2, it, h)
                    cols = bass.ds(it * (2 * C) + h * C, C)
                    act.wait_ge(s(f"got2_{h}"), (it + 1) * (16 * C))
                    nc.scalar.activation(r5[:, h, :, 0:3], rvec[:, cols, :], ACT.Copy).then_inc(s("factors_in"), 1)
                    nc.scalar.activation(r5[:, h, :, 3:5], rvec[:, cols, 0:2], ACT.Copy).then_inc(s("factors_in"), 1)
                    if past(2 * G * (2 * it + h - 1)):
                        act.wait_ge(s("r_used"), C * (2 * it + h - 1))
                    nc.scalar.activation(d16[:, h, :, 0:MUL], got[:, h, :, 0:MUL], ACT.Copy).then_inc(s("factors_in"), 1)
                    for g in range(C // G):
                        n = (2 * it + h) * (C // G) + g
                        if g >= 4 and g % 2 == 0:
                            pair_sums(it, h, g // 2 - 2)
                        if g == 2:
                            if h == 0 and not isinstance(it, int):
                                pair_sums(it - 1, 1, 3)
                            elif h == 1:
                                pair_sums(it, 0, 3)
                        if g == 7:
                            if h == 0 and not isinstance(it, int):
                                turn_out(2, it - 1, 1)
                            elif h == 1:
                                turn_out(2, it, 0)
                        act.wait_ge(s("w_spread"), n + 1)
                        if past(G * (n - 1)):
                            act.wait_ge(s("r_done"), G * (n - 1))
                        nc.scalar.activation(hid[0:HID, g % 2, :], pbc[g % 2][0:HID, :], ACT.Relu, bias=b1c[:, :], scale=w1c[:, :]).then_inc(s("hid_ready"), 1)
                    pair_sums(it, h, 2)
            steps(act, layer2)
            pair_sums(ITERS - 1, 1, 3)
            turn_out(2, ITERS - 1, 1)
            for b in range(BLOCKS):
                root(3, b)
            sum_sources(3)
            dense(3, F)

        @block.tensor
        def _(pe):
            pe.wait_ge(s("const1"), 7)
            pe.wait_ge(s("firsts_ready"), 1)
            nc.tensor.matmul(pm[1][:, 0:P], dst_f[:, 0:1].broadcast_to([P, P]), ident[:, :], start=True, stop=True).then_inc(s("order_firsts"), 1)
            pe.wait_ge(s("disorder"), 1)
            nc.tensor.matmul(pm[0][0:J, 0:1], ones[:, :], disorder[:, 2:3], start=True, stop=True).then_inc(s("disorder_summed"), 1)
            pe.wait_ge(s("order_known"), 1)
            with pe.If(pe.value_load(unsorted[0:1, 0:1], min_val=0, max_val=1)):
                def count(n):
                    pe.wait_ge(s("sort_onehots"), n + 1)
                    for c in range(G):
                        ins = nc.tensor.matmul(hist, one_hi[:, 0, c, :], one_lo[:, 0, c, :], start=isinstance(n, int) and c == 0, stop=True, skip_group_check=True)
                    ins.then_inc(s("sort_counted"), 1)
                count(0)
                with pe.Fori(1, T // G) as n:
                    count(n)
                pe.wait_ge(s("sort_totals"), 1)
                nc.tensor.matmul(pm[0][:, 0:1], upper[:, :], st1[:, 0:1], start=True, stop=True).then_inc(s("sort_offsets"), 1)
                with pe.Fori(0, T) as t:
                    pe.wait_ge(s("sort_staged"), t + 1)
                    nc.tensor.matmul(pm[1][:, 0:P], rec[:, 0:1].broadcast_to([P, P]), ident[:, :], start=True, stop=True).then_inc(s("sort_spread"), 1)

            def histogram(it):
                for h in range(2):
                    for g in range(C // G):
                        n = (2 * it + h) * (C // G) + g
                        pe.wait_ge(s("onehots"), n + 1)
                        for c in range(G):
                            first = h == 0 and g == 0 and c == 0 and isinstance(it, int)
                            ins = nc.tensor.matmul(hist, one_hi[:, g % 2, c, :], one_lo[:, g % 2, c, :], start=first, stop=True, skip_group_check=True)
                        ins.then_inc(s("counted"), 1)
            steps(pe, histogram)
            pe.wait_ge(s("totals"), 1)
            nc.tensor.matmul(pm[0][:, 0:1], upper[:, :], st1[:, 0:1], start=True, stop=True).then_inc(s("offsets_ps"), 1)
            nc.tensor.matmul(pm[1][:, 0:P], dst_f[:, 0:1].broadcast_to([P, P]), ident[:, :], start=True, stop=True).then_inc(s("firsts_ps"), 1)

            def carry_product(k):
                pe.wait_ge(s("tails"), TURN[k])
                nc.tensor.matmul(pm[0][:, 0:F], joins[:, :], tails[:, :], start=True, stop=True).then_inc(s("carry_ps"), 1)

            def dense(k, width, w):
                for it in range(BLOCKS):
                    pe.wait_ge(s(f"staged{k}"), it + 1)
                    for half in range(2):
                        if past(it):
                            pe.wait_ge(s(f"finished{k}"), it)
                        for n in range(NB // 2):
                            bank, at = pr[2 * half + n // 4], n % 4
                            ins = nc.tensor.matmul(bank[0:width, at * P:(at + 1) * P], stage[:, half * (NB // 2) + n, 0:width], ident[:, :], start=True, stop=True)
                        ins.then_inc(s(f"turned_ps{k}"), 1)
                        pe.wait_ge(s(f"turned_sb{k}"), 4 * it + 2 * half + 2)
                        for n in range(NB // 2):
                            a = half * (NB // 2) + n
                            ins = nc.tensor.matmul(pm[0][:, a * F:(a + 1) * F], turned[0:width, n * P:(n + 1) * P], w, start=True, stop=True)
                        ins.then_inc(s(f"product{k}"), 1)

            carry_product(0)
            dense(0, 2 * F, w_sage_s[:, :])

            def layer1(it):
                for h in range(2):
                    pe.wait_ge(s(f"srcf_ready_{h}"), it + 1)

                    def spread_sources(g):
                        n = (2 * it + h) * (C // G) + g
                        if past(n - 1):
                            pe.wait_ge(s("eq_ready"), n - 1)
                        for c in range(G):
                            ins = nc.tensor.matmul(pbc[g % 2][:, c * P:(c + 1) * P], idxf[:, h, g * G + c:g * G + c + 1].broadcast_to([P, P]), ident[:, :], start=True, stop=True)
                        ins.then_inc(s("src_spread"), 1)

                    spread_sources(0)
                    for g in range(C // G):
                        if g + 1 < C // G:
                            spread_sources(g + 1)
                        n = (2 * it + h) * (C // G) + g
                        pe.wait_ge(s("eq_ready"), n + 1)
                        if g == 0:
                            pe.wait_ge(s(f"msg_ready_{h}"), it + 1)
                        b = g // 2
                        if g % 2 == 0:
                            if b >= 2:
                                if past((C // (2 * G)) * it + b - 1):
                                    pe.wait_ge(s(f"sums_ready_{h}"), (C // (2 * G)) * it + b - 1)
                            elif h == 1:
                                if past((C // (2 * G)) * (it + 1) - 1 + b):
                                    pe.wait_ge(s("sums_ready_0"), (C // (2 * G)) * (it + 1) - 1 + b)
                            else:
                                if past((C // (2 * G)) * it - 1 + b):
                                    pe.wait_ge(s("sums_ready_1"), (C // (2 * G)) * it - 1 + b)
                        for c in range(G):
                            t = g * G + c
                            ins = nc.tensor.matmul(pm[b % 2][:, (t % (2 * G)) * FM:(t % (2 * G) + 1) * FM], eq[:, g % 2, c * P:(c + 1) * P], msg[:, h, t, :], start=True, stop=True)
                        ins.then_inc(s("eq_used"), 1)
            steps(pe, layer1)

            def layer2(it):
                for h in range(2):
                    pe.wait_ge(s(f"w_ready_{h}"), it + 1)

                    def spread_weights(g):
                        n = (2 * it + h) * (C // G) + g
                        if past(n - 1):
                            pe.wait_ge(s("hid_ready"), n - 1)
                        for c in range(G):
                            ins = nc.tensor.matmul(pbc[g % 2][0:HID, c * P:(c + 1) * P], idxf[:, h, g * G + c:g * G + c + 1].broadcast_to([P, HID]), ident[:, :], start=True, stop=True)
                        ins.then_inc(s("w_spread"), 1)

                    spread_weights(0)
                    for g in range(C // G):
                        if g + 1 < C // G:
                            spread_weights(g + 1)
                        n = (2 * it + h) * (C // G) + g
                        pe.wait_ge(s("hid_ready"), n + 1)
                        for c in range(G):
                            if past(G * (n - 1) + c + 1):
                                pe.wait_ge(s("r_used"), G * (n - 1) + c + 1)
                            nc.tensor.matmul(pr[c][:, 0:384], hid[:, g % 2, c * P:(c + 1) * P], w2p[:, :], start=True, stop=True).then_inc(s("r_done"), 1)
                        if g >= 2 and g % 2 == 0:
                            sum_pairs(it, h, g // 2 - 1)
                        if g == 0 and h == 1:
                            sum_pairs(it, 0, 3)
                        if g == 0 and h == 0 and not isinstance(it, int):
                            sum_pairs(it - 1, 1, 3)

            def sum_pairs(it, h, b):
                n = (2 * it + h) * (C // (2 * G)) + b
                pe.wait_ge(s("r_used"), (n + 1) * 2 * G)
                if past(2 * (n - 1)):
                    pe.wait_ge(s("pairs_out"), 2 * (n - 1))
                for w in range(PAIR):
                    ins = nc.tensor.matmul(pm[b % 2][:, 0:2 * G * PAIR], ident[:, :], pairs_of[b % 2][:, w, :, :].rearrange("p t q -> p (t q)"),
                                           start=w == 0, stop=w == PAIR - 1)
                ins.then_inc(s("pairs_summed"), 1)
            pe.wait_ge(s("w2_ready"), 1)
            steps(pe, layer2)
            sum_pairs(ITERS - 1, 1, 3)
            carry_product(2)
            carry_product(3)
            dense(3, F, w_gcn_s[:, :])

        @block.vector
        def _(dve):
            V = nc.vector
            ch = Chain(dve, "dve_chain")
            V.memset(dst_i, N).then_inc(s("pads_set"), 1)
            V.memset(src_i[:, :], 0).then_inc(s("pads_set"), 1)
            V.memset(wgt[:, :], 0.0).then_inc(s("pads_set"), 1)
            V.memset(rvec[:, :, :], 1.0).then_inc(s("pads_set"), 1)
            V.memset(xs[:, :, :], 0.0).then_inc(s("pads_set"), 1)
            V.memset(hid[:, :, :], 1.0).then_inc(s("pads_set"), 1)
            V.memset(share_b[:, :], 0.0).then_inc(s("zeros_set"), 1)
            ch.do(V.memset(ones[:, :], 1.0), False)
            ch.do(V.memset(keep[:, :, :, :], 0.0), False)
            ch.do(V.memset(xT[:, :, :, :], 0.0), False)
            ch.do(V.memset(sc[:, :, :, :], 0.0))

            def bc(ap, shape, axis):
                return ap.unsqueeze(axis).broadcast_to(shape)

            NJF, BN = [P, J, F], [P, NB, F]

            def layernorm(k, b):
                js = slice(b * NB, (b + 1) * NB)
                ch.do(V.tensor_reduce(st1[:, js], xs[:, js, :], AX, ALU.add))
                ch.do(V.tensor_scalar(st1[:, js], st1[:, js], 1.0 / F, None, ALU.mult))
                ch.do(V.tensor_tensor(tmpv[:, js, :], xs[:, js, :], bc(st1[:, js], BN, 2), ALU.subtract))
                ch.do(V.tensor_tensor(hn[:, js, :], tmpv[:, js, :], tmpv[:, js, :], ALU.mult))
                ch.do(V.tensor_reduce(st2[:, js], hn[:, js, :], AX, ALU.add))
                ch.do(V.tensor_scalar(st2[:, js], st2[:, js], 1.0 / F, EPS, ALU.mult, ALU.add))
                dve.sem_inc(s("var"), 1)
                dve.wait_ge(s("std"), BLOCKS * k + b + 1)
                ch.do(V.reciprocal(st3[:, js], st3[:, js]))
                if k == 3:
                    ch.do(V.tensor_tensor(st3[:, js], st3[:, js], isd[:, js], ALU.mult))
                if k == 2:
                    BM = [P, NB, MUL]
                    ch.do(V.scalar_tensor_tensor(hn[:, js, 0:MUL], tmpv[:, js, 0:MUL], 0.0, bc(st3[:, js], BM, 2), ALU.max, ALU.mult), False)
                    for c, i in enumerate((2, 0, 1)):
                        ch.do(V.scalar_tensor_tensor(hn[:, js, MUL * (c + 1):MUL * (c + 2)], tmpv[:, js, MUL + i:F:3], 0.0, bc(st3[:, js], BM, 2), ALU.max, ALU.mult), c == 2)
                else:
                    ch.do(V.scalar_tensor_tensor(hn[:, js, :], tmpv[:, js, :], 0.0, bc(st3[:, js], BN, 2), ALU.max, ALU.mult))
                dve.sem_inc(s("normed"), 1)

            dve.wait_ge(s("x_in"), 48)
            for b in range(BLOCKS):
                layernorm(0, b)

            dve.wait_ge(s("dst_in"), 48)
            dve.wait_ge(s("const1"), 7)
            ch.do(V.tensor_copy(ji[:, :], ji_i[:, :]), False)
            ch.do(V.tensor_copy(pif[:, :], pi_i[:, :]), False)
            ch.do(V.tensor_copy(dump[:, :], dump_i[:, :]), False)
            ch.do(V.tensor_copy(sdump[:, :], sdump_i[:, :]), False)
            ch.do(V.tensor_copy(dst_f[:, :], dst_i))

            def split(quotient):
                ch.do(V.tensor_scalar(quotient, dst_f[:, :], 1.0 / J, None, ALU.mult))
                ch.do(V.tensor_copy(hi, quotient))
                ch.do(V.scalar_tensor_tensor(lo, hi, -float(J), dst_f[:, :], ALU.mult, ALU.add))
                ch.do(V.tensor_scalar(hi, lo, 0.0, float(J), ALU.is_lt, ALU.mult))
                ch.do(V.tensor_tensor(lo, lo, hi, ALU.add))
                ch.do(V.tensor_scalar(hi, lo, float(J), float(J), ALU.is_ge, ALU.mult))
                ch.do(V.tensor_tensor(lo, lo, hi, ALU.subtract))
                ch.do(V.tensor_tensor(hi, dst_f[:, :], lo, ALU.subtract))

            dve.sem_inc(s("firsts_ready"), 1)
            ch.do(V.tensor_tensor(lo[:, 1:T], dst_f[:, 1:T], dst_f[:, 0:T - 1], ALU.is_lt))
            ch.do(V.tensor_reduce(disorder[:, 0:1], lo[:, 1:T], AX, ALU.add))
            dve.wait_ge(s("order_firsts"), 1)
            ch.do(V.scalar_tensor_tensor(ends_after[:, :], pm[1][:, 0:P], dst_f[:, T - 1:T], upper[:, :], ALU.is_lt, ALU.mult))
            ch.do(V.tensor_reduce(disorder[:, 1:2], ends_after[:, :], AX, ALU.add))
            ch.do(V.tensor_tensor(disorder[:, 2:3], disorder[:, 0:1], disorder[:, 1:2], ALU.add))
            dve.sem_inc(s("disorder"), 1)
            dve.wait_ge(s("disorder_summed"), 1)
            V.tensor_scalar(unsorted[:, :], pm[0][0:1, 0:1], 0.0, None, ALU.is_gt).then_inc(s("order_known"), 1)
            dve.wait_ge(s("order_known"), 1)
            before_sort = ch.n
            with dve.If(dve.value_load(unsorted[0:1, 0:1], min_val=0, max_val=1)):
                cs = Chain(dve, "dve_sort")
                main, ch = ch, cs
                dve.wait_ge(s("src_in"), 48)
                dve.wait_ge(s("wgt_in"), 48)
                dve.wait_ge(s("attr_in"), 48)
                split(dst_i)

                def count(n):
                    cols = bass.ds(n * G, G)
                    V.tensor_tensor(one_hi[:, 0, :, :], bc(hi[:, cols], [P, G, P], 2), bc(pif[:, :], [P, G, P], 1), ALU.is_equal)
                    V.tensor_tensor(one_lo[:, 0, :, :], bc(lo[:, cols], [P, G, J], 2), bc(ji[:, :], [P, G, J], 1), ALU.is_equal).then_inc(s("sort_onehots"), 1)
                    dve.wait_ge(s("sort_counted"), n + 1)
                count(0)
                with dve.Fori(1, T // G) as n:
                    count(n)
                ch.do(V.tensor_copy(cnt[:, :], hist))
                ch.do(V.tensor_tensor_scan(run[:, :], ones[:, :], cnt[:, :], 0.0, ALU.mult, ALU.add))
                V.tensor_copy(st1[:, 0:1], run[:, J - 1:J]).then_inc(s("sort_totals"), 1)
                dve.wait_ge(s("sort_offsets"), 1)
                ch.do(V.tensor_copy(offs[:, :], pm[0][:, 0:1]))
                ch.do(V.tensor_scalar(first_f[:, :], run[:, :], offs[:, :], None, ALU.add))
                ch.do(V.tensor_tensor(first_f[:, :], first_f[:, :], cnt[:, :], ALU.subtract))
                dve.sem_inc(s("sort_cursors"), 1)
                ct = Chain(dve, "dve_sort_columns", per_step=17)
                with dve.Fori(0, T) as t:
                    ct.step(t)
                    col = bass.ds(t, 1)
                    ct.do(V.tensor_copy(rec[:, 0:1], dst_f[:, col]), False)
                    ct.do(V.tensor_copy(rec[:, 1:2], src_i[:, col]), False)
                    ct.do(V.tensor_copy(rec[:, 2:3], wgt[:, col]), False)
                    ct.do(V.tensor_copy(rec[:, 3:6], rvec[:, col, :]), False)
                    ct.do(V.tensor_copy(node_i[:, :], dst_f[:, col]))
                    dve.sem_inc(s("sort_staged"), 1)
                    dve.wait_ge(s("sort_spread"), t + 1)
                    ct.do(V.scalar_tensor_tensor(ends_after[:, :], pm[1][:, 0:P], rec[:, 0:1], lower[:, :], ALU.is_equal, ALU.mult), False)
                    ct.do(V.scalar_tensor_tensor(joins[:, :], pm[1][:, 0:P], rec[:, 0:1], upper[:, :], ALU.is_equal, ALU.mult))
                    ct.do(V.tensor_reduce(rank[:, 0:1], ends_after[:, :], AX, ALU.add), False)
                    ct.do(V.tensor_reduce(rank[:, 1:2], joins[:, :], AX, ALU.add))
                    ct.do(V.tensor_scalar(rank[:, 1:2], rank[:, 1:2], 0.0, None, ALU.is_equal), False)
                    ct.do(V.tensor_tensor(target[:, :], rec[:, 0:1], dump[:, :], ALU.subtract))
                    ct.do(V.tensor_tensor(target[:, :], target[:, :], rank[:, 1:2], ALU.mult))
                    ct.do(V.tensor_tensor(target[:, :], target[:, :], dump[:, :], ALU.add))
                    ct.do(V.tensor_copy(target_i[:, :], target[:, :]))
                    dve.wait_ge(s("sort_cursor_in"), 16 * (t + 1))
                    ct.do(V.tensor_tensor(place[:, :], place[:, :], rank[:, 0:1], ALU.add))
                    ct.do(V.tensor_copy(place_i[:, :], place[:, :]), False)
                    ct.do(V.tensor_scalar(next_place[:, :], place[:, :], 1.0, None, ALU.add))
                    assert ct.n == ct.per, ct.n
                    dve.sem_inc(s("sort_placed"), 1)
                    dve.wait_ge(s("sort_moved"), 32 * (t + 1))
                for q in range(PARTS):
                    n = T // PARTS
                    back = share_a[:, 0:n * REC].rearrange("p (t c) -> p t c", c=REC)
                    dve.wait_ge(s("sort_back"), 16 * (q + 1))
                    ch.do(V.tensor_copy(dst_f[:, q * n:(q + 1) * n], back[:, :, 0]), False)
                    ch.do(V.tensor_copy(src_i[:, q * n:(q + 1) * n], back[:, :, 1]), False)
                    ch.do(V.tensor_copy(wgt[:, q * n:(q + 1) * n], back[:, :, 2]), False)
                    ch.do(V.tensor_copy(rvec[:, q * n:(q + 1) * n, :], back[:, :, 3:6]))
                    dve.sem_inc(s("sort_unpacked"), 1)
                ch = main
            assert ch.n == before_sort

            ch.do(V.tensor_copy(dst0_i[:, :], dst_f[:, 0:1]), False)
            ch.do(V.memset(same[:, 0:1], 0.0), False)
            ch.do(V.tensor_tensor(same[:, 1:T], dst_f[:, 1:T], dst_f[:, 0:T - 1], ALU.is_equal))
            dve.sem_inc(s("same_ready"), 1)
            split(dst_i)

            def scan(chain, k, it, h):
                dve.wait_ge(s(f"keep_ready_{h}"), k * ITERS + it + 1)
                chain.do(V.tensor_copy(xT[:, h, :, 0], sc[:, 1 - h, :, C]))
                if k != 1:
                    if past(OLD[k] + it):
                        dve.wait_ge(s(f"rows_ready_{h}"), OLD[k] + it)
                ins = V.tensor_tensor_scan(sc[:, h, :, :].rearrange("p f t -> p (f t)"), keep[:, h, :, :].rearrange("p f t -> p (f t)"),
                                           xT[:, h, :, :].rearrange("p f t -> p (f t)"), 0.0, ALU.mult, ALU.add)
                ins.then_inc(s(f"scanned_{h}"), 1)
                dve.wait_ge(s(f"scanned_{h}"), k * ITERS + it + 1)

            c0 = Chain(dve, "dve_layer0", per_step=2)

            def layer0(it):
                c0.step(it)
                for h in range(2):
                    for g in range(C // G):
                        n = (2 * it + h) * (C // G) + g
                        if past(n - 1):
                            dve.wait_ge(s("counted"), n - 1)
                        cols = bass.ds(it * (2 * C) + h * C + g * G, G)
                        V.tensor_tensor(one_hi[:, g % 2, :, :], bc(hi[:, cols], [P, G, P], 2), bc(pif[:, :], [P, G, P], 1), ALU.is_equal)
                        V.tensor_tensor(one_lo[:, g % 2, :, :], bc(lo[:, cols], [P, G, J], 2), bc(ji[:, :], [P, G, J], 1), ALU.is_equal).then_inc(s("onehots"), 1)
                    dve.wait_ge(s(f"turned_in_{h}"), it + 1)
                    scan(c0, 0, it, h)
            steps(dve, layer0)

            dve.wait_ge(s("counted"), 2 * ITERS * (C // G))
            ch.do(V.tensor_copy(cnt[:, :], hist))
            ch.do(V.tensor_tensor_scan(run[:, :], ones[:, :], cnt[:, :], 0.0, ALU.mult, ALU.add))
            V.tensor_copy(st1[:, 0:1], run[:, J - 1:J]).then_inc(s("totals"), 1)
            dve.wait_ge(s("offsets_ps"), 1)
            ch.do(V.tensor_copy(offs[:, :], pm[0][:, 0:1]))
            ch.do(V.tensor_scalar(last_f[:, :], run[:, :], offs[:, :], 1.0, ALU.add, ALU.subtract), False)
            ch.do(V.tensor_scalar(nzero[:, :], cnt[:, :], 0.0, None, ALU.is_gt))
            ch.do(V.tensor_tensor(first_f[:, :], last_f[:, :], cnt[:, :], ALU.subtract))
            ch.do(V.tensor_scalar(first_f[:, :], first_f[:, :], 1.0, None, ALU.add))
            ch.do(V.tensor_tensor(first_f[:, :], first_f[:, :], sdump[:, :], ALU.subtract))
            ch.do(V.tensor_scalar(last_f[:, :], last_f[:, :], float(EP), None, ALU.subtract))
            ch.do(V.tensor_tensor(first_f[:, :], first_f[:, :], nzero[:, :], ALU.mult), False)
            ch.do(V.tensor_tensor(last_f[:, :], last_f[:, :], nzero[:, :], ALU.mult))
            ch.do(V.tensor_tensor(first_f[:, :], first_f[:, :], sdump[:, :], ALU.add), False)
            ch.do(V.tensor_scalar(last_f[:, :], last_f[:, :], float(EP), None, ALU.add))
            V.tensor_copy(first_i[:, :], first_f[:, :]).then_inc(s("places_ready"), 1)
            V.tensor_copy(last_i[:, :], last_f[:, :]).then_inc(s("places_ready"), 1)
            dve.wait_ge(s("firsts_ps"), 1)
            ch.do(V.scalar_tensor_tensor(joins[:, :], pm[1][:, 0:P], dst_f[:, T - 1:T], upper[:, :], ALU.is_equal, ALU.mult), False)
            ch.do(V.scalar_tensor_tensor(ends_after[:, :], pm[1][:, 0:P], dst_f[:, 0:1], upper[:, :], ALU.is_equal, ALU.mult))
            ch.do(V.tensor_reduce(cidx_f[:, :], ends_after[:, :], AX, ALU.add))
            ch.do(V.tensor_scalar(cidx_f[:, :], cidx_f[:, :], 0.0, None, ALU.is_equal), False)
            ch.do(V.tensor_tensor(cidx_t[:, :], dst_f[:, 0:1], dump[:, :], ALU.subtract))
            ch.do(V.tensor_tensor(cidx_t[:, :], cidx_t[:, :], cidx_f[:, :], ALU.mult))
            ch.do(V.tensor_tensor(cidx_t[:, :], cidx_t[:, :], dump[:, :], ALU.add))
            ch.do(V.tensor_copy(cidx[:, :], cidx_t[:, :]))

            def send_carries():
                ch.do(V.tensor_copy(tails[:, :], sc[:, 1, :, C]))
                dve.sem_inc(s("tails"), 1)

            def finish_carries(k):
                dve.wait_ge(s("carry_ps"), TURN[k])
                V.tensor_copy(carry[:, :], pm[0][:, 0:F]).then_inc(s("carry_ready"), 1)
                dve.wait_ge(s("carried_in"), 16 * TURN[k])

            def node_sums(k, b):
                js = slice(b * NB, (b + 1) * NB)
                dve.wait_ge(s(f"ends_in_{b}"), 16 * NB * TURN[k])
                ch.do(V.tensor_tensor(ag[:, js, :], ag[:, js, :], tmpv[:, js, :], ALU.add))
                return js

            tb = share_c[:, NB * 4 * F:NB * 5 * F].rearrange("p (j f) -> p j f", f=F)
            pmv = pm[0][:, 0:NB * F].rearrange("p (j f) -> p j f", f=F)

            def relu_dense(k, b, js, bias):
                dve.wait_ge(s(f"product{k}"), 2 * b + 2)
                ch.do(V.tensor_tensor(tb, pmv, bc(bias[:, :], BN, 1), ALU.add))
                ch.do(V.scalar_tensor_tensor(xs[:, js, :], tb, 0.0, xs[:, js, :], ALU.max, ALU.add))
                dve.sem_inc(s(f"finished{k}"), 1)

            send_carries()
            finish_carries(0)
            ch.do(V.tensor_scalar(rcnt[:, :], cnt[:, :], 1.0, None, ALU.max))
            ch.do(V.reciprocal(rcnt[:, :], rcnt[:, :]))
            dve.wait_ge(s("weights_in"), 16 * 8)
            for b in range(BLOCKS):
                js = node_sums(0, b)
                V.tensor_copy(stage[:, :, 0:F], hn[:, js, :])
                V.tensor_tensor(stage[:, :, F:2 * F], ag[:, js, :], bc(rcnt[:, js], BN, 2), ALU.mult).then_inc(s("staged0"), 1)
                relu_dense(0, b, js, b_sage_s)
                layernorm(1, b)

            dve.wait_ge(s("attr_in"), 48)
            rt = share_b[:, 0:T]
            ra = share_a[:, 0:T]
            ch.do(V.tensor_tensor(ra, rvec[:, :, 0], rvec[:, :, 0], ALU.mult), False)
            ch.do(V.tensor_tensor(rt, rvec[:, :, 1], rvec[:, :, 1], ALU.mult))
            ch.do(V.tensor_tensor(ra, ra, rt, ALU.add))
            ch.do(V.tensor_tensor(rt, rvec[:, :, 2], rvec[:, :, 2], ALU.mult))
            ch.do(V.tensor_tensor(ra, ra, rt, ALU.add))
            dve.sem_inc(s("norm2"), 1)
            dve.wait_ge(s("norm"), 1)
            ch.do(V.reciprocal(ra, rt))
            ch.do(V.tensor_tensor(rvec[:, :, :], rvec[:, :, :], bc(ra, [P, T, 3], 2), ALU.mult))
            ch.do(V.tensor_scalar(rcnt[:, :], cnt[:, :], 1.0, 1.0, ALU.add, ALU.max))
            dve.sem_inc(s("degree"), 1)
            dve.wait_ge(s("degree_root"), 1)
            ch.do(V.reciprocal(isd[:, :], isd[:, :]))

            y0, y1 = 0.5 / sqrt(pi), sqrt(3.0 / (4.0 * pi))
            norm0 = sqrt(4.0 * pi) / sqrt(2 * MUL)
            norm1 = sqrt(4.0 * pi) * sqrt(3.0) / sqrt(4 * MUL)
            quad = sqrt(1.0 / (24.0 * pi))
            sq = MUL * MUL

            def uv(ap):
                return ap.rearrange("p (u v) -> p u v", v=MUL)

            def pick(k):
                return w2s[:, 3 * sq:6 * sq].rearrange("p (u v k) -> p u v k", v=MUL, k=3)[:, :, :, k]
            coef = w2p[:, :]
            c_vec, c_cross = uv(coef[:, 0:sq]), uv(coef[:, sq:2 * sq])
            pairs = coef[:, 2 * sq:].rearrange("p (k u s v) -> p k u s v", k=2, u=MUL, s=2)
            ch.do(V.tensor_scalar(pairs[:, 0, :, 0, :], uv(w2s[:, 0:sq]), norm0 * y0, None, ALU.mult), False)
            ch.do(V.tensor_scalar(pairs[:, 0, :, 1, :], uv(w2s[:, sq:2 * sq]), norm0 * y1 / sqrt(3), None, ALU.mult), False)
            ch.do(V.tensor_scalar(pairs[:, 1, :, 0, :], uv(w2s[:, 2 * sq:3 * sq]), norm1 * y1 / sqrt(3), None, ALU.mult), False)
            ch.do(V.tensor_scalar(pairs[:, 1, :, 1, :], pick(2), norm1 * 3 * quad, None, ALU.mult), False)
            ch.do(V.tensor_scalar(c_cross, pick(1), norm1 * y1 / sqrt(6), None, ALU.mult), False)
            ch.do(V.tensor_scalar(c_vec, pick(0), norm1 * y0 / sqrt(3), None, ALU.mult), False)
            ch.do(V.tensor_scalar(fr[0:HID + 1, 0:MUL, 0, :], pick(2), -norm1 * quad, None, ALU.mult))
            ch.do(V.tensor_tensor(c_vec, c_vec, fr[0:HID + 1, 0:MUL, 0, :], ALU.add))
            dve.sem_inc(s("w2_ready"), 1)

            dve.wait_ge(s("wgt_in"), 48)
            ch.do(V.memset(sc[:, 1, :, C], 0.0))
            c1 = Chain(dve, "dve_layer1", per_step=0)
            PER1 = 2 * (1 + 2 + (C // G) * 3 + 5)
            c1.per = PER1

            def layer1(it):
                c1.step(it)
                for h in range(2):
                    dve.wait_ge(s(f"turned_in_{h}"), ITERS + it + 1)
                    scan(c1, 1, it, h)
                    cols = bass.ds(it * (2 * C) + h * C, C)
                    if past((2 * it + h - 1) * (C // G)):
                        dve.wait_ge(s("eq_used"), (2 * it + h - 1) * (C // G))
                    c1.do(V.tensor_tensor(msg[:, h, :, 0:F], sc[:, h, :, 1:W1].rearrange("p f t -> p t f"), bc(wgt[:, cols], [P, C, F], 2), ALU.mult), False)
                    c1.do(V.tensor_copy(msg[:, h, :, F], wgt[:, cols]))
                    dve.sem_inc(s(f"msg_ready_{h}"), 1)
                    dve.wait_ge(s(f"srcf_ready_{h}"), it + 1)
                    for g in range(C // G):
                        n = (2 * it + h) * (C // G) + g
                        dve.wait_ge(s("src_spread"), n + 1)
                        if past(n - 1):
                            dve.wait_ge(s("eq_used"), n - 1)
                        eqv = eq[:, g % 2, :].rearrange("p (c q) -> p c q", q=P)
                        c1.do(V.tensor_tensor(eqv, pbc[g % 2][:, :].rearrange("p (c q) -> p c q", q=P),
                                              bc(idxf[:, h, g * G:(g + 1) * G], [P, G, P], 2), ALU.is_equal))
                        dve.sem_inc(s("eq_ready"), 1)
                        ev = earlier[:, :].rearrange("p (c q) -> p c q", q=P)
                        c1.do(V.tensor_tensor(ev, eqv, bc(lower[:, :], [P, G, P], 1), ALU.mult))
                        c1.do(V.tensor_reduce(dup[:, g * G:(g + 1) * G], ev, AX, ALU.add), g == C // G - 1)
                    c1.do(V.tensor_scalar(widx_f[:, :], idxf[:, h, :], dump[:, :], None, ALU.subtract), False)
                    c1.do(V.tensor_scalar(dup[:, :], dup[:, :], 0.0, None, ALU.is_equal))
                    c1.do(V.tensor_tensor(widx_f[:, :], widx_f[:, :], dup[:, :], ALU.mult))
                    c1.do(V.tensor_scalar(widx_f[:, :], widx_f[:, :], dump[:, :], None, ALU.add))
                    for q in range(TABLES):
                        if past((2 * it + h - 1) * (16 * C // TABLES)):
                            dve.wait_ge(s(f"added_{q}"), (2 * it + h - 1) * (16 * C // TABLES))
                    c1.do(V.tensor_copy(idx[:, h, :], widx_f[:, :]))
                    dve.sem_inc(s(f"targets_ready_{h}"), 1)
                    dve.sem_inc(s(f"srcf_used_{h}"), 1)
                assert c1.n == PER1, c1.n
            steps(dve, layer1)
            part_0 = part_in[0][:, 0:J * FM].rearrange("p (j f) -> p j f", f=FM)
            for k in range(TABLES):
                sfm = part_in[k][:, 0:J * FM].rearrange("p (j f) -> p j f", f=FM)
                dve.wait_ge(s(f"part_in{k}"), 16)
                if k == 0:
                    continue
                if k == 1:
                    ch.do(V.tensor_tensor(ag[:, :, :], part_0[:, :, 0:F], sfm[:, :, 0:F], ALU.add), False)
                    ch.do(V.tensor_tensor(st1[:, :], part_0[:, :, F], sfm[:, :, F], ALU.add))
                else:
                    ch.do(V.tensor_tensor(ag[:, :, :], ag[:, :, :], sfm[:, :, 0:F], ALU.add), False)
                    ch.do(V.tensor_tensor(st1[:, :], st1[:, :], sfm[:, :, F], ALU.add))
            ch.do(V.tensor_tensor(hn[:, :, :], hn[:, :, :], bc(st1[:, :], NJF, 2), ALU.mult))
            ch.do(V.tensor_tensor(ag[:, :, :], ag[:, :, :], hn[:, :, :], ALU.subtract))
            ch.do(V.tensor_tensor(xs[:, :, :], xs[:, :, :], ag[:, :, :], ALU.add))
            for b in range(BLOCKS):
                layernorm(2, b)

            ch.do(V.memset(sc[:, 1, :, C], 0.0))

            CV = [P, C, 3, MUL]
            c2 = Chain(dve, "dve_layer2")
            FINISH, HALF, FINISH_AT = 9, 3 + C + C // 2, 4
            c2.per = 2 * (HALF + FINISH)

            def finish_messages(it, h):
                va = red[:, h, :, 0:VEC // 2].rearrange("p t (u o) -> p t o u", o=3)
                vc = red[:, h, :, VEC // 2:VEC].rearrange("p t (u o) -> p t o u", o=3)
                m1 = xT[:, h, MUL:F, 1:W1].rearrange("p (o u) t -> p t o u", o=3)
                r = r5[:, h, :, :]
                c2.do(V.tensor_copy(c5[:, :, 0:3, :], vc), False)
                yield
                c_in = c2.do(V.tensor_copy(c5[:, :, 3:5, :], vc[:, :, 0:2, :]), False)
                yield
                c2.now(c_in)
                c2.do(V.tensor_tensor(fr, c5[:, :, 2:5, :], bc(r[:, :, 1:4], CV, 3), ALU.mult), False)
                yield
                crossed = c2.do(V.tensor_tensor(fr2, c5[:, :, 1:4, :], bc(r[:, :, 2:5], CV, 3), ALU.mult), False)
                yield
                c2.now(crossed)
                crossed = c2.do(V.tensor_tensor(fr, fr, fr2, ALU.subtract), False)
                yield
                dve.wait_ge(s("pairs_out"), (2 * it + h + 1) * (C // G))
                c2.now(crossed)
                c2.do(V.tensor_tensor(fr2, bc(sv[:, h, :, :], CV, 2), bc(r[:, :, 0:3], CV, 3), ALU.mult), False)
                yield
                added = c2.do(V.tensor_tensor(fr, fr, va, ALU.add), False)
                yield
                c2.now(added)
                c2.do(V.tensor_tensor(m1, fr, fr2, ALU.add), False)
                yield
                dve.wait_ge(s(f"keep_ready_{h}"), 2 * ITERS + it + 1)
                whole = c2.do(V.tensor_copy(xT[:, h, :, 0], sc[:, 1 - h, :, C]), False)
                yield
                if past(OLD[2] + it):
                    dve.wait_ge(s(f"rows_ready_{h}"), OLD[2] + it)
                c2.now(whole)
                V.tensor_tensor_scan(sc[:, h, :, :].rearrange("p f t -> p (f t)"), keep[:, h, :, :].rearrange("p f t -> p (f t)"),
                                     xT[:, h, :, :].rearrange("p f t -> p (f t)"), 0.0, ALU.mult, ALU.add).then_inc(s(f"scanned_{h}"), 1)
                yield
                dve.wait_ge(s(f"scanned_{h}"), 2 * ITERS + it + 1)
                yield

            def layer2(it):
                c2.step(it)
                c2.before = 0 if isinstance(it, int) else -FINISH
                for h in range(2):
                    dve.wait_ge(s(f"got2_{h}"), (it + 1) * (16 * C))
                    f1 = got[:, h, :, MUL:F].rearrange("p t (o v) -> p t o v", v=MUL)
                    dve.wait_ge(s("factors_in"), (2 * it + h) * 3 + 3)
                    c2.do(V.tensor_tensor(fr, f1, bc(r5[:, h, :, 0:3], CV, 3), ALU.mult))
                    c2.do(V.tensor_tensor(d16[:, h, :, MUL:], fr[:, :, 0, :], fr[:, :, 1, :], ALU.add))
                    c2.do(V.tensor_tensor(d16[:, h, :, MUL:], d16[:, h, :, MUL:], fr[:, :, 2, :], ALU.add))
                    reduced = {}
                    if h == 1:
                        last_chunk = finish_messages(it, 0)
                    else:
                        last_chunk = iter(()) if isinstance(it, int) else finish_messages(it - 1, 1)
                    for t in range(C + 2):
                        if t >= FINISH_AT:
                            next(last_chunk, None)
                        if t < C:
                            n = (2 * it + h) * C + t
                            b = t // (2 * G)
                            dve.wait_ge(s("r_done"), n + 1)
                            if t >= 4 and t % 2 == 0:
                                c2.now(reduced[t - 4])
                            if t % (2 * G) == 0:
                                past_sums = (2 * it + h) * (C // (2 * G)) + b - 1
                                if past(past_sums):
                                    dve.wait_ge(s("pairs_summed"), past_sums)
                            bank = pr[t % 4]
                            c2.do(V.tensor_tensor(prod[:, t % 4, :].rearrange("p (u o v) -> p u o v", o=3, v=MUL),
                                                  bc(bank[:, 0:2 * sq].rearrange("p (u v) -> p u v", v=MUL), [P, 2 * MUL, 3, MUL], 2),
                                                  bc(f1[:, t, :, :], [P, 2 * MUL, 3, MUL], 1), ALU.mult), False)
                            V.tensor_tensor(pairs_of[b % 2][:, :, t % (2 * G), :].rearrange("p w q -> p q w"),
                                            bank[:, 2 * sq:6 * sq].rearrange("p (q w) -> p q w", w=PAIR),
                                            bc(d16[:, h, t, :], [P, PAIR, PAIR], 1), ALU.mult).then_inc(s("r_used"), 1)
                        if t >= 3 and t % 2 == 1 or t == C + 1:
                            a = t - 3
                            dve.wait_ge(s("r_used"), (2 * it + h) * C + a + 2)
                            reduced[a] = c2.do(V.tensor_reduce(red[:, h, a:a + 2, :].rearrange("p t q -> p (t q)"),
                                                               prod[:, a % 4:a % 4 + 2, :].rearrange("p s (q v) -> p (s q) v", v=MUL), AX, ALU.add), t == C + 1)
                    dve.sem_inc(s(f"turned_in_{h}"), 1)
                assert c2.n == c2.per - (FINISH if isinstance(it, int) else 0), c2.n
            steps(dve, layer2)
            c2.step(ITERS)
            for _ in finish_messages(ITERS - 1, 1):
                pass
            send_carries()
            finish_carries(2)
            for b in range(BLOCKS):
                js = node_sums(2, b)
                ch.do(V.tensor_tensor(xs[:, js, 0:MUL], xs[:, js, 0:MUL], ag[:, js, 0:MUL], ALU.add), False)
                for c, i in enumerate((2, 0, 1)):
                    ch.do(V.tensor_tensor(xs[:, js, MUL + i:F:3], xs[:, js, MUL + i:F:3], ag[:, js, MUL * (c + 1):MUL * (c + 2)], ALU.add), c == 2)
                layernorm(3, b)

            ch.do(V.memset(sc[:, 1, :, C], 0.0))
            c3 = Chain(dve, "dve_layer3", per_step=2)

            def layer3(it):
                c3.step(it)
                for h in range(2):
                    dve.wait_ge(s(f"turned_in_{h}"), 3 * ITERS + it + 1)
                    scan(c3, 3, it, h)
            steps(dve, layer3)
            send_carries()
            finish_carries(3)
            for b in range(BLOCKS):
                js = node_sums(3, b)
                ch.do(V.tensor_tensor(ag[:, js, :], ag[:, js, :], hn[:, js, :], ALU.add))
                V.tensor_tensor(stage[:, :, 0:F], ag[:, js, :], bc(isd[:, js], BN, 2), ALU.mult).then_inc(s("staged3"), 1)
                relu_dense(3, b, js, b_gcn_s)
                dve.sem_inc(s("x_done"), 1)


_INS = ["x", "src", "dst", "edge_attr_3", "edge_weight", "L0_gnn_W", "L0_gnn_b", "L2_gnn_w1", "L2_gnn_b1", "L2_gnn_w2", "L2_gnn_b2", "L3_gnn_W", "L3_gnn_bias"]


def kernel(**inputs):
    import numpy as np
    import concourse.bacc as bacc
    from concourse import mybir as mb
    from concourse.bass_utils import run_bass_kernel_spmd

    nc = bacc.Bacc("TRN2", target_bir_lowering=False, num_devices=1)
    arrays, args = {}, []
    for name in _INS:
        a = np.ascontiguousarray(inputs[name])
        arrays[f"in_{name}"] = a
        args.append(nc.dram_tensor(f"in_{name}", a.shape, mb.dt.from_np(a.dtype), kind="ExternalInput").ap())
    args.append(nc.dram_tensor("out_x", (N, F), mb.dt.float32, kind="ExternalOutput").ap())
    gnn_program(nc, *args)
    result = run_bass_kernel_spmd(nc, [arrays], core_ids=[0])
    return result.results[0]["out_x"]
```

```python
import concourse.bass as bass
from concourse import mybir
from contextlib import ExitStack
from math import pi, sqrt

fp32 = mybir.dt.float32
bf16 = mybir.dt.bfloat16
i32 = mybir.dt.int32
ALU = mybir.AluOpType
ACT = mybir.ActivationFunctionType
AX = mybir.AxisListType.X

P = 128
N, F = 12500, 32
E = 212500
J = -(-N // P)
NP = P * J
C = 32
ITERS = -(-E // (P * C * 2))
T = ITERS * 2 * C
EP = P * T
W1 = C + 1
FM = F + 1
TABLES = 4
REC = 6
PARTS = 4
G = 4
HID = 64
WSLOTS = 4
MUL = 8
NB = 14
BLOCKS = J // NB
TURN = {0: 1, 2: 2, 3: 3}
OLD = {k: (TURN[k] - 1) * ITERS for k in TURN}
EPS = 1e-5


def gnn_program(nc, x, src, dst, attr, weight, w_sage, b_sage, w1, b1, w2, b2, w_gcn, b_gcn, out):
    ctx = ExitStack()

    def sb(name, shape, dt=fp32):
        return ctx.enter_context(nc.sbuf_tensor(name, shape, dt))

    def pb(name):
        return ctx.enter_context(nc.psum_tensor(name, [P, 512], fp32))

    def sem(name):
        return ctx.enter_context(nc.semaphore(name))

    def dram(name, shape, dt=fp32):
        return nc.dram_tensor(name, shape, dt, kind="Internal").ap()

    with ctx:
        table = [dram(f"node_table{k}", (NP, F)) for k in range(4)]
        scans = {k: dram(f"edge_scans{k}", (EP + 1, F)) for k in (0, 2, 3)}
        spread = dram("edge_spread", (EP + NP, F))
        carried = {k: dram(f"carried{k}", (NP + P, F)) for k in (0, 2, 3)}
        cursor = dram("cursor", (NP + P, 1))
        records = dram("records", (EP, REC))
        w_columns = dram("weights_by_column", (T, P))
        part = [dram(f"source_sums{k}", (NP + P, FM)) for k in range(TABLES)]

        src_i = sb("src_i", [P, T + C], i32)
        wgt = sb("wgt", [P, T + C])
        dst_f = sb("dst_f", [P, T])
        same = sb("same", [P, T])
        rvec = sb("rvec", [P, T, 3])
        share_a = sb("share_a", [P, 2 * T])
        lo, hi = share_a[:, 0:T], share_a[:, T:2 * T]
        share_b = sb("share_b", [P, 3328])
        zeros = share_b[:, :]
        xs = sb("xs", [P, J, F])
        hn = sb("hn", [P, J, F])
        ag = sb("ag", [P, J, F])
        tmp = sb("tmp", [P, J * FM])
        tmpv = tmp[:, 0:J * F].rearrange("p (j f) -> p j f", f=F)
        got = sb("got", [P, 2, C, F])
        xT = sb("xT", [P, 2, F, W1])
        keep = sb("keep", [P, 2, F, W1])
        sc = sb("sc", [P, 2, F, W1])
        rows = sb("rows", [P, 2, C, F])
        dst_i = rows[:, :, :, :].rearrange("p h t f -> p (h t f)").bitcast(i32)[:, 0:T]
        idx = sb("idx", [P, 2, C], i32)
        idxf = sb("idxf", [P, 2, C])
        msg = share_a[:, 0:2 * C * FM].rearrange("p (h t f) -> p h t f", h=2, f=FM)
        sums = share_b[:, 0:2 * C * FM].rearrange("p (h t f) -> p h t f", h=2, f=FM)
        share_c = sb("share_c", [P, 19 * C * MUL])
        part_in = [tmp, share_a, share_b, share_c]
        eq = share_c[:, 0:2 * G * P].rearrange("p (h q) -> p h q", h=2)
        earlier = share_c[:, 2 * G * P:3 * G * P]
        dup = sb("dup", [P, C])
        widx_f = sb("widx_f", [P, C])
        VEC, PAIR = 3 * MUL, 2 * MUL
        CM = C * MUL
        red = share_a[:, 0:2 * C * VEC].rearrange("p (h t q) -> p h t q", h=2, q=VEC)
        prod = share_b[:, 0:2 * (G - 1) * VEC * PAIR].rearrange("p (s q) -> p s q", q=VEC * PAIR)
        SUMMED = 2 * G * PAIR + 2 * VEC
        to_sum = [tile[:, 0:PAIR * SUMMED].rearrange("p (w n) -> p w n", w=PAIR)
                  for tile in (tmp, ag[:, :, :].rearrange("p j f -> p (j f)"))]
        d16 = share_c[:, 0:4 * CM].rearrange("p (h t v) -> p h t v", h=2, t=C)
        fr = share_c[:, 4 * CM:7 * CM].rearrange("p (t o v) -> p t o v", t=C, o=3)
        fr2 = share_c[:, 7 * CM:10 * CM].rearrange("p (t o v) -> p t o v", t=C, o=3)
        fr3 = share_c[:, 10 * CM:13 * CM].rearrange("p (t o v) -> p t o v", t=C, o=3)
        fx = [share_c[:, 13 * CM:19 * CM].rearrange("p (t o w) -> p t o w", t=C, o=3),
              share_a[:, 6 * CM:12 * CM].rearrange("p (t o w) -> p t o w", t=C, o=3)]
        f5 = dst_f[:, 0:5 * CM].rearrange("p (t o v) -> p t o v", t=C, o=5)
        r5 = sb("r5", [P, 2, C, 5])
        sv = sb("sv", [P, 2, C, MUL])
        turned_w = dst_f[:, :]
        w_rows = [hn[:, :, :].rearrange("p j f -> p (j f)")[0:HID, k * G * P:(k + 1) * G * P] for k in range(WSLOTS)]
        hid = sb("hid", [HID + 1, 2, G * P])
        w2s = sb("w2s", [HID + 1, 384])
        w2p = sb("w2p", [HID + 1, 384])
        w1c = sb("w1c", [HID, 1])
        b1c = sb("b1c", [HID, 1])
        one_lo = sb("one_lo", [P, 2, G, J], bf16)
        one_hi = sb("one_hi", [P, 2, G, P], bf16)
        ident = sb("ident", [P, P])
        upper = sb("upper", [P, P])
        lower = sb("lower", [P, P])
        joins = sb("joins", [P, P])
        ends_after = sb("ends_after", [P, P])
        ji_i = sb("ji_i", [P, J], i32)
        ji = sb("ji", [P, J])
        pi_i = sb("pi_i", [P, P], i32)
        pif = sb("pif", [P, P])
        dump_i = sb("dump_i", [P, 1], i32)
        dump = sb("dump", [P, 1])
        cnt = sb("cnt", [P, J])
        run = sb("run", [P, J])
        first_f = sb("first_f", [P, J])
        last_f = sb("last_f", [P, J])
        nzero = sb("nzero", [P, J])
        sdump_i = sb("sdump_i", [P, J], i32)
        sdump = sb("sdump", [P, J])
        first_i = sb("first_i", [P, J], i32)
        last_i = sb("last_i", [P, J], i32)
        rcnt = sb("rcnt", [P, J])
        isd = sb("isd", [P, J])
        st1 = sb("st1", [P, J])
        st2 = sb("st2", [P, J])
        st3 = sb("st3", [P, J])
        ones = sb("ones", [P, J])
        offs = sb("offs", [P, 1])
        cidx_f = sb("cidx_f", [P, 1])
        cidx_t = sb("cidx_t", [P, 1])
        cidx = sb("cidx", [P, 1], i32)
        dst0_i = sb("dst0_i", [P, 1], i32)
        tails = sb("tails", [P, F])
        disorder = sb("disorder", [P, 3])
        unsorted = sb("unsorted", [1, 1], i32)
        rec = sb("rec", [P, REC])
        node_i = sb("node_i", [P, 1], i32)
        place = sb("place", [P, 1])
        place_i = sb("place_i", [P, 1], i32)
        next_place = sb("next_place", [P, 1])
        rank = sb("rank", [P, 2])
        target = sb("target", [P, 1])
        target_i = sb("target_i", [P, 1], i32)
        carry = sb("carry", [P, F])
        head = sb("head", [P, F])
        stage = share_c[:, 0:NB * 2 * F].rearrange("p (j f) -> p j f", j=NB)
        turned = share_c[0:2 * F, NB * 2 * F:NB * (2 * F + P // 2)]
        w_sage_s = sb("w_sage_s", [2 * F, F])
        w_gcn_s = sb("w_gcn_s", [F, F])
        b_sage_s = sb("b_sage_s", [P, F])
        b_gcn_s = sb("b_gcn_s", [P, F])

        r_set = [ctx.enter_context(nc.psum_tensor(f"r_set{k}", [P, 3 * 512], fp32)) for k in range(2)]
        pr = [r_set[k // 3][:, k % 3 * 512:(k % 3 + 1) * 512] for k in range(4)]
        pbc = [r_set[1][:, k * 512:(k + 1) * 512] for k in (1, 2)]
        pm = [pb(f"pm{k}") for k in range(2)]
        hist = pr[0][:, 0:J]

        S = {}

        def s(name):
            if name not in S:
                S[name] = sem(name)
            return S[name]

        def past(value):
            return not isinstance(value, int) or value > 0

        def steps(eng, body):
            body(0)
            with eng.Fori(1, ITERS) as it:
                body(it)

        class Chain:

            def __init__(self, eng, name, per_step=0, before=0):
                self.eng, self.name, self.per, self.n, self.before, self.it = eng, name, per_step, 0, before, 0

            def step(self, it):
                self.it, self.n = it, 0

            def do(self, ins, wait_now=True):
                self.n += 1
                ins.then_inc(s(self.name), 1)
                if wait_now:
                    self.now()
                return self.n

            def now(self, n=None):
                self.eng.wait_ge(s(self.name), self.it * self.per + (self.n if n is None else n) + self.before)

        def node_rows(t):
            return t.rearrange("(p j) f -> p (j f)", p=P)

        SPREAD_PART = T * F // ITERS
        spread_runs = spread[0:EP, :].rearrange("(p t) f -> p (t f)", p=P)
        ZEROED = ITERS + TABLES + 3 + 3

        block = ctx.enter_context(nc.Block())

        @block.sync
        def _(sp):
            sp.wait_ge(s("pads_set"), 6)
            def load_padded(name, tile, src_ap, width):
                full, rest = src_ap.shape[0] // width, src_ap.shape[0] % width
                most = full // 16 * 16
                for a, b in ((0, most), (most, full)):
                    sp.dma_start(tile[a:b, 0:width], src_ap[a * width:b * width].rearrange("(p t) -> p t", t=width)).then_inc(s(name), 16)
                sp.dma_start(tile[full:full + 1, 0:rest], src_ap[full * width:].rearrange("(p t) -> p t", p=1)).then_inc(s(name), 16)

            nfull, nrest = N // J, N % J
            xv = xs[:, :, :].rearrange("p j f -> p (j f)")
            load_padded("x_in", xv, x.rearrange("n f -> (n f)"), J * F)
            load_padded("dst_in", dst_i, dst, T)
            load_padded("src_in", src_i, src, T)
            load_padded("wgt_in", wgt, weight, T)
            load_padded("attr_in", rvec[:, :, :].rearrange("p t c -> p (t c)"), attr.rearrange("e c -> (e c)"), 3 * T)
            sp.dma_start(w_sage_s[:, :], w_sage).then_inc(s("weights_in"), 16)
            sp.dma_start(w_gcn_s[:, :], w_gcn.rearrange("o i -> i o"), allow_slow_non_contiguous=True).then_inc(s("weights_in"), 16)
            sp.dma_start(b_sage_s[:, :], b_sage.rearrange("(a f) -> a f", a=1).broadcast_to([P, F])).then_inc(s("weights_in"), 16)
            sp.dma_start(b_gcn_s[:, :], b_gcn.rearrange("(a f) -> a f", a=1).broadcast_to([P, F])).then_inc(s("weights_in"), 16)
            sp.dma_start(w1c[:, :], w1.rearrange("a (h c) -> (a h) c", c=1)).then_inc(s("weights_in"), 16)
            sp.dma_start(b1c[:, :], b1.rearrange("(h a) -> h a", a=1)).then_inc(s("weights_in"), 16)
            sp.dma_start(w2s[0:HID, :], w2).then_inc(s("weights_in"), 16)
            sp.dma_start(w2s[HID:HID + 1, :], b2.rearrange("(a f) -> a f", a=1)).then_inc(s("weights_in"), 16)

            sp.wait_ge(s("order_known"), 1)
            with sp.If(sp.value_load(unsorted[0:1, 0:1], min_val=0, max_val=1)):
                sp.wait_ge(s("sort_cursors"), 1)
                sp.dma_start(cursor[0:NP, :].rearrange("(p j) c -> p (j c)", p=P), first_f[:, :]).then_inc(s("sort_cursors_stored"), 16)
                sp.wait_ge(s("sort_moved"), 32 * T)
                for q in range(PARTS):
                    if q >= 1:
                        sp.wait_ge(s("sort_unpacked"), q)
                    n = T // PARTS
                    sp.dma_start(share_a[:, 0:n * REC], records.rearrange("(p t) c -> p (t c)", p=P)[:, q * n * REC:(q + 1) * n * REC]).then_inc(s("sort_back"), 16)

            def store_scans(k):
                view = scans[k][0:EP, :].rearrange("(p t) f -> p t f", t=T)

                def body(it):
                    for h in range(2):
                        sp.wait_ge(s(f"rows_ready_{h}"), OLD[k] + it + 1)
                        sp.dma_start(view[:, bass.ds(it * (2 * C) + h * C, C), :], rows[:, h, :, :]).then_inc(s(f"rows_stored_{h}"), 16)
                steps(sp, body)

            def load_carried(k):
                sp.wait_ge(s("carry_sent"), 16 * TURN[k])
                sp.dma_start(tmp[:, 0:J * F], node_rows(carried[k][0:NP, :])).then_inc(s("carried_in"), 16)

            def store_table(k):
                for b in range(BLOCKS):
                    sp.wait_ge(s("normed"), BLOCKS * k + b + 1)
                    sp.dma_start(table[k].rearrange("(p j) f -> p j f", p=P)[:, b * NB:(b + 1) * NB, :], hn[:, b * NB:(b + 1) * NB, :]).then_inc(s("table_stored"), 16)

            store_table(0)
            store_scans(0)
            load_carried(0)
            store_table(1)
            sp.wait_ge(s("turned_weights"), 4)
            sp.dma_start(w_columns.rearrange("(b q) p -> q b p", q=P), turned_w.rearrange("q (b p) -> q b p", p=P)).then_inc(s("weights_stored"), 16)

            sp.wait_ge(s("starts_sent"), 16 * J)
            sp.wait_ge(s("heads_in"), 16)
            sp.dma_start(spread[0:EP, :].rearrange("(p t) f -> p t f", t=T)[:, 0, :], head[:, :]).then_inc(s("heads_stored"), 16)
            sp.wait_ge(s("heads_stored"), 16)
            view = spread[0:EP, :].rearrange("(p t) f -> p t f", t=T)

            def load_spread(it):
                for h in range(2):
                    sp.wait_ge(s(f"turned_in_{h}"), ITERS + it)
                    sp.dma_start(got[:, h, :, :], view[:, bass.ds(it * (2 * C) + h * C, C), :]).then_inc(s(f"spread_in_{h}"), 16)
            steps(sp, load_spread)
            sp.wait_ge(s("adds_done"), 1)
            sp.wait_ge(s("weights_stored"), 16)
            for k in range(TABLES):
                sp.dma_start(part_in[k][:, 0:J * FM], node_rows(part[k][0:NP, :])).then_inc(s(f"part_in{k}"), 16)
            store_table(2)
            sp.wait_ge(s("table_stored"), 16 * BLOCKS * 3)
            by_four = w_columns.rearrange("(n c) p -> n (c p)", c=G)
            scans_2 = scans[2][0:EP, :].rearrange("(p t) f -> p t f", t=T)

            def layer2(it):
                for h in range(2):
                    for g in range(C // G):
                        n = (2 * it + h) * (C // G) + g
                        if past(n - WSLOTS + 1):
                            sp.wait_ge(s("hid_ready"), n - WSLOTS + 1)
                        sp.dma_start(w_rows[g % WSLOTS], by_four[bass.ds(n, 1), :].broadcast_to([HID, G * P])).then_inc(s(f"w_rows_in_{g % WSLOTS}"), 16)
                        if g == C // G // 2 and not (isinstance(it, int) and it == 0):
                            sp.wait_ge(s(f"rows_ready_{h}"), OLD[2] + it)
                            sp.dma_start(scans_2[:, bass.ds((it - 1) * (2 * C) + h * C, C), :], rows[:, h, :, :]).then_inc(s(f"rows_stored_{h}"), 16)
            steps(sp, layer2)
            for h in range(2):
                sp.wait_ge(s(f"rows_ready_{h}"), OLD[2] + ITERS)
                sp.dma_start(scans_2[:, T - (2 - h) * C:T - (1 - h) * C, :], rows[:, h, :, :]).then_inc(s(f"rows_stored_{h}"), 16)
            load_carried(2)
            store_table(3)
            store_scans(3)
            load_carried(3)
            for b in range(BLOCKS):
                lo_c, hi_c = b * NB * F, (b + 1) * NB * F
                sp.wait_ge(s("x_done"), b + 1)
                sp.dma_start(out[0:nfull * J, :].rearrange("(p j) f -> p (j f)", j=J)[:, lo_c:hi_c], xv[0:nfull, lo_c:hi_c]).then_inc(s("out_stored"), 16)
                if lo_c < nrest * F:
                    top = min(hi_c, nrest * F)
                    sp.dma_start(out[nfull * J:N, :].rearrange("(p j) f -> p (j f)", p=1)[:, lo_c:top], xv[nfull:nfull + 1, lo_c:top]).then_inc(s("out_stored"), 16)
            sp.wait_ge(s("out_stored"), 16 * (BLOCKS + -(-nrest // NB)))

        @block.gpsimd
        def _(pool):
            pool.memset(ident[:, :], 0.0).then_inc(s("const0"), 1)
            pool.memset(upper[:, :], 1.0).then_inc(s("const0"), 1)
            pool.memset(lower[:, :], 1.0).then_inc(s("const0"), 1)
            pool.iota(ji_i[:, :], pattern=[[1, J]], base=0, channel_multiplier=0).then_inc(s("const1"), 1)
            pool.iota(pi_i[:, :], pattern=[[J, P]], base=0, channel_multiplier=0).then_inc(s("const1"), 1)
            pool.iota(dump_i[:, :], pattern=[[0, 1]], base=NP, channel_multiplier=1).then_inc(s("const1"), 1)
            pool.iota(sdump_i[:, :], pattern=[[1, J]], base=EP, channel_multiplier=J).then_inc(s("const1"), 1)
            pool.wait_ge(s("const0"), 3)
            pool.affine_select(out=ident[:, :], in_=ident[:, :], compare_op=ALU.not_equal, fill=1.0, base=0,
                               pattern=[[-1, P]], channel_multiplier=1).then_inc(s("const1"), 1)
            pool.affine_select(out=upper[:, :], in_=upper[:, :], compare_op=ALU.is_gt, fill=0.0, base=0,
                               pattern=[[1, P]], channel_multiplier=-1).then_inc(s("const1"), 1)
            pool.affine_select(out=lower[:, :], in_=lower[:, :], compare_op=ALU.is_gt, fill=0.0, base=0,
                               pattern=[[-1, P]], channel_multiplier=1).then_inc(s("const1"), 1)

            pool.wait_ge(s("order_known"), 1)
            with pool.If(pool.value_load(unsorted[0:1, 0:1], min_val=0, max_val=1)):
                pool.wait_ge(s("sort_cursors_stored"), 16)
                with pool.Fori(0, T) as t:
                    pool.wait_ge(s("sort_staged"), t + 1)
                    pool.sem_inc(s("pool_passed"), 1)
                    pool.indirect_dma_start(place[:, :], None, cursor[0:NP, :], bass.IndirectOffsetOnAxis(ap=node_i[:, :], axis=0)).then_inc(s("sort_cursor_in"), 16)
                    pool.wait_ge(s("sort_placed"), t + 1)
                    pool.sem_inc(s("pool_passed"), 1)
                    pool.indirect_dma_start(records, bass.IndirectOffsetOnAxis(ap=place_i[:, :], axis=0), rec[:, :], None).then_inc(s("sort_moved"), 16)
                    pool.indirect_dma_start(cursor, bass.IndirectOffsetOnAxis(ap=target_i[:, :], axis=0), next_place[:, :], None).then_inc(s("sort_moved"), 16)
                    pool.wait_ge(s("sort_moved"), 32 * (t + 1))
                    pool.sem_inc(s("pool_passed"), 1)

            def cross(it, h):
                r = r5[:, h, :, :]
                shape = [P, C, 3, MUL]
                if past(2 * it + h):
                    pool.wait_ge(s("crossed"), 2 * it + h)
                nc.gpsimd.tensor_tensor(fr, f5[:, :, 2:5, :], r[:, :, 1:4].unsqueeze(3).broadcast_to(shape), ALU.mult).then_inc(s("cross_terms"), 1)
                nc.gpsimd.tensor_tensor(fr2, f5[:, :, 1:4, :], r[:, :, 2:5].unsqueeze(3).broadcast_to(shape), ALU.mult).then_inc(s("cross_terms"), 1)
                pool.wait_ge(s("cross_terms"), 2 * (2 * it + h + 1))
                nc.gpsimd.tensor_tensor(fx[h][:, :, :, MUL:], fr, fr2, ALU.subtract).then_inc(s("crossed"), 1)

            def gather_edges(k):
                pool.wait_ge(s("table_stored"), 16 * BLOCKS * (k + 1))

                def body(it):
                    for h in range(2):
                        pool.wait_ge(s(f"idx_ready{k}_{h}"), it + 1)
                        pool.sem_inc(s("pool_passed"), 1)
                        if past(k * ITERS + it):
                            pool.wait_ge(s(f"turned_in_{h}"), k * ITERS + it)
                        pool.sem_inc(s("pool_passed"), 1)
                        if k == 2 and not (isinstance(it, int) and it == 0):
                            cross(it - 1, h)
                        for t in range(C):
                            pool.indirect_dma_start(got[:, h, t, :], None, table[k], bass.IndirectOffsetOnAxis(ap=idx[:, h, t:t + 1], axis=0)).then_inc(s(f"got{k}_{h}"), 16)
                steps(pool, body)
                if k == 2:
                    for h in range(2):
                        pool.wait_ge(s(f"turned_in_{h}"), 3 * ITERS)
                        cross(ITERS - 1, h)

            def gather_ends(k):
                for h in range(2):
                    pool.wait_ge(s(f"rows_stored_{h}"), 16 * (OLD[k] + ITERS))
                pool.wait_ge(s("carry_ready"), TURN[k])
                if k == 0:
                    pool.wait_ge(s("places_ready"), 2)
                    pool.wait_ge(s("zeros_stored"), 16 * ZEROED)
                pool.indirect_dma_start(carried[k], bass.IndirectOffsetOnAxis(ap=cidx[:, :], axis=0), carry[:, :], None).then_inc(s("carry_sent"), 16)
                for j in range(J):
                    pool.indirect_dma_start(ag[:, j, :], None, scans[k], bass.IndirectOffsetOnAxis(ap=last_i[:, j:j + 1], axis=0)).then_inc(s(f"ends_in_{j // NB}"), 16)

            gather_edges(0)
            gather_ends(0)
            for j in range(J):
                if j % NB == 0:
                    pool.wait_ge(s("normed"), BLOCKS + j // NB + 1)
                if j == J - NB:
                    pool.wait_ge(s("table_stored"), 16 * BLOCKS * 2)
                    pool.indirect_dma_start(head[:, :], None, table[1], bass.IndirectOffsetOnAxis(ap=dst0_i[:, :], axis=0)).then_inc(s("heads_in"), 16)
                pool.indirect_dma_start(spread, bass.IndirectOffsetOnAxis(ap=first_i[:, j:j + 1], axis=0), hn[:, j, :], None).then_inc(s("starts_sent"), 16)

            def add_sums(it):
                for h in range(2):
                    for t in range(C):
                        if t == 0:
                            pool.wait_ge(s(f"targets_ready_{h}"), it + 1)
                            pool.sem_inc(s("pool_passed"), 1)
                        if t % (2 * G) == 0:
                            if past((C // (2 * G)) * it + t // (2 * G) + 1):
                                pool.wait_ge(s(f"sums_ready_{h}"), (C // (2 * G)) * it + t // (2 * G) + 1)
                            pool.sem_inc(s("pool_passed"), 1)
                        if past(((2 * it + h) * (C // TABLES) + t // TABLES) * 16):
                            pool.wait_ge(s(f"added_{t % TABLES}"), ((2 * it + h) * (C // TABLES) + t // TABLES) * 16)
                        pool.sem_inc(s("pool_passed"), 1)
                        pool.indirect_dma_start(part[t % TABLES], bass.IndirectOffsetOnAxis(ap=idx[:, h, t:t + 1], axis=0), sums[:, h, t, :], None,
                                                compute_op=ALU.add, oob_is_err=True).then_inc(s(f"added_{t % TABLES}"), 16)
            steps(pool, add_sums)
            for k in range(TABLES):
                pool.wait_ge(s(f"added_{k}"), 16 * T // TABLES)
            pool.memset(dump_i[:, :], 0).then_inc(s("adds_done"), 1)
            for k in (2, 3):
                gather_edges(k)
                gather_ends(k)

        @block.scalar
        def _(act):
            def store_zeros(tables, width):
                for view in tables:
                    act.dma_start(view.rearrange("(p j) f -> p (j f)", p=P), zeros[:, 0:(NP + P) // P * width]).then_inc(s("zeros_stored"), 16)

            def root(k, b):
                js = slice(b * NB, (b + 1) * NB)
                act.wait_ge(s("var"), BLOCKS * k + b + 1)
                nc.scalar.activation(st3[:, js], st2[:, js], ACT.Sqrt).then_inc(s("std"), 1)

            def stage_idx(k, it, h):
                if past(it * (16 * C)):
                    act.wait_ge(s(f"got{k}_{h}"), it * (16 * C))
                nc.scalar.activation(idx[:, h, :], src_i[:, bass.ds(it * (2 * C) + h * C, C)], ACT.Copy).then_inc(s(f"idx_ready{k}_{h}"), 1)

            def set_keep(k, it, h):
                if past(k * ITERS + it):
                    act.wait_ge(s(f"scanned_{h}"), k * ITERS + it)
                nc.scalar.activation(keep[:, h, :, 1:W1], same[:, bass.ds(it * (2 * C) + h * C, C)].unsqueeze(1).broadcast_to([P, F, C]),
                                     ACT.Copy).then_inc(s(f"keep_ready_{h}"), 1)

            def turn_in(k, it, h, source, per):
                act.wait_ge(s(f"{source}_{h}"), (it + 1) * per)
                nc.scalar.activation(xT[:, h, :, 1:W1], got[:, h, :, :].rearrange("p t f -> p f t"), ACT.Copy).then_inc(s(f"turned_in_{h}"), 1)

            def turn_out(k, it, h):
                act.wait_ge(s(f"scanned_{h}"), k * ITERS + it + 1)
                if past(OLD[k] + it):
                    act.wait_ge(s(f"rows_stored_{h}"), (OLD[k] + it) * 16)
                nc.scalar.activation(rows[:, h, :, :], sc[:, h, :, 1:W1].rearrange("p f t -> p t f"), ACT.Copy).then_inc(s(f"rows_ready_{h}"), 1)

            def sum_sources(k):
                stage_idx(k, 0, 0)
                if k == 0:
                    act.wait_ge(s("zeros_set"), 1)
                    for q in (0, 2, 3):
                        act.dma_start(scans[q][EP:EP + 1, :], zeros[0:1, 0:F]).then_inc(s("zeros_stored"), 16)

                def body(it):
                    for h in range(2):
                        stage_idx(k, it + h, 1 - h)
                        set_keep(k, it, h)
                        turn_in(k, it, h, f"got{k}", 16 * C)
                        turn_out(k, it, h)
                    if k == 0:
                        act.dma_start(spread_runs[:, bass.ds(it * SPREAD_PART, SPREAD_PART)], zeros[:, 0:SPREAD_PART]).then_inc(s("zeros_stored"), 16)
                        if isinstance(it, int):
                            store_zeros([carried[q] for q in carried], F)
                            store_zeros(part, FM)
                steps(act, body)

            def dense(k, width):
                for it in range(BLOCKS):
                    for half in range(2):
                        act.wait_ge(s(f"turned_ps{k}"), 2 * it + half + 1)
                        if past(2 * it + half):
                            act.wait_ge(s(f"product{k}"), 2 * it + half)
                        for b in range(2):
                            m = (4, 3)[b]
                            nc.scalar.activation(turned[0:width, b * 4 * P:(b * 4 + m) * P], pr[2 * half + b][0:width, 0:m * P], ACT.Copy).then_inc(s(f"turned_sb{k}"), 1)
                    if k == 0:
                        root(1, it)

            for b in range(BLOCKS):
                root(0, b)
            act.wait_ge(s("src_in"), 48)
            act.wait_ge(s("same_ready"), 1)
            sum_sources(0)
            dense(0, 2 * F)
            act.wait_ge(s("zeros_stored"), 16 * ZEROED)
            act.wait_ge(s("norm2"), 1)
            nc.scalar.activation(share_b[:, 0:T], share_a[:, 0:T], ACT.Sqrt).then_inc(s("norm"), 1)
            act.wait_ge(s("degree"), 1)
            nc.scalar.activation(isd[:, :], rcnt[:, :], ACT.Sqrt).then_inc(s("degree_root"), 1)
            act.wait_ge(s("weights_ps"), 1)
            for b in range(4):
                wide = min(4 * P, T - b * 4 * P)
                nc.scalar.activation(turned_w[:, b * 4 * P:b * 4 * P + wide], pr[b][:, 0:wide], ACT.Copy).then_inc(s("turned_weights"), 1)


            def layer1(it):
                for h in range(2):
                    if past(it):
                        act.wait_ge(s(f"srcf_used_{h}"), it)
                    nc.scalar.activation(idxf[:, h, :], src_i[:, bass.ds(it * (2 * C) + h * C, C)], ACT.Copy).then_inc(s(f"srcf_ready_{h}"), 1)
                    set_keep(1, it, h)
                    turn_in(1, it, h, "spread_in", 16)
                for h in range(2):
                    for q in range(TABLES):
                        if past((2 * it + h - 1) * (16 * C // TABLES)):
                            act.wait_ge(s(f"added_{q}"), (2 * it + h - 1) * (16 * C // TABLES))
                    for g in range(C // (2 * G)):
                        if past((2 * it + h) * (C // G) + 2 * g + 2):
                            act.wait_ge(s("eq_used"), (2 * it + h) * (C // G) + 2 * g + 2)
                        nc.scalar.activation(sums[:, h, g * 2 * G:(g + 1) * 2 * G, :].rearrange("p t f -> p (t f)"),
                                             pm[g % 2][:, 0:2 * G * FM], ACT.Copy).then_inc(s(f"sums_ready_{h}"), 1)
            steps(act, layer1)
            for b in range(BLOCKS):
                root(2, b)
            act.wait_ge(s("weights_in"), 16 * 8)

            act.wait_ge(s("wgt_in"), 48)
            for h in range(2):
                stage_idx(2, 0, h)

            def pair_sums(it, h, b):
                act.wait_ge(s("pairs_summed"), (2 * it + h) * (C // (2 * G)) + b + 1)
                bank = pm[b % 2]
                got_sums = bank[:, 0:2 * G * PAIR].rearrange("p (t k u) -> p t k u", k=2, u=MUL)
                a = b * 2 * G
                nc.scalar.activation(xT[:, h, 0:MUL, 1 + a:1 + a + 2 * G].rearrange("p u t -> p t u"), got_sums[:, :, 0, :], ACT.Copy).then_inc(s("pairs_out"), 1)
                nc.scalar.activation(sv[:, h, a:a + 2 * G, :], got_sums[:, :, 1, :], ACT.Copy).then_inc(s("pairs_out"), 1)
                nc.scalar.activation(red[:, h, a + G - 1:a + 2 * G:G, :], bank[:, 2 * G * PAIR:SUMMED].rearrange("p (t q) -> p t q", q=VEC), ACT.Copy).then_inc(s("pairs_out"), 1)

            def lay_out(it, h, more=True):
                cols = bass.ds(it * (2 * C) + h * C, C)
                act.wait_ge(s(f"got2_{h}"), (it + 1) * (16 * C))
                if past((C // G) * (2 * it + h - 1) + 1):
                    act.wait_ge(s("r_used"), (C // G) * (2 * it + h - 1) + 1)
                nc.scalar.activation(r5[:, h, :, 0:3], rvec[:, cols, :], ACT.Copy).then_inc(s("factors_in"), 1)
                nc.scalar.activation(r5[:, h, :, 3:5], rvec[:, cols, 0:2], ACT.Copy).then_inc(s("factors_in"), 1)
                f1 = got[:, h, :, MUL:F].rearrange("p t (o v) -> p t o v", v=MUL)
                nc.scalar.activation(f5[:, :, 0:3, :], f1, ACT.Copy).then_inc(s("factors_in"), 1)
                nc.scalar.activation(f5[:, :, 3:5, :], f1[:, :, 0:2, :], ACT.Copy).then_inc(s("factors_in"), 1)
                nc.scalar.activation(fx[h][:, :, :, 0:MUL], f1, ACT.Copy).then_inc(s("factors_in"), 1)
                nc.scalar.activation(d16[:, h, :, 0:MUL], got[:, h, :, 0:MUL], ACT.Copy).then_inc(s("factors_in"), 1)
                act.wait_ge(s("factors_in"), (2 * it + h + 1) * 6)
                act.sem_inc(s(f"turned_in_{h}"), 1)
                if more:
                    stage_idx(2, it + 1, h)

            def layer2(it):
                last = isinstance(it, int) and it == ITERS - 1
                for h in range(2):
                    for g in range(C // G):
                        n = (2 * it + h) * (C // G) + g
                        act.wait_ge(s(f"w_rows_in_{g % WSLOTS}"), 16 * ((2 * it + h) * (C // G // WSLOTS) + g // WSLOTS + 1))
                        if past(n - 1):
                            act.wait_ge(s("r_done"), n - 1)
                        nc.scalar.activation(hid[0:HID, g % 2, :], w_rows[g % WSLOTS], ACT.Relu, bias=b1c[:, :], scale=w1c[:, :]).then_inc(s("hid_ready"), 1)
                        if g in (0, 2, 4):
                            if h == 1:
                                pair_sums(it, 0, 1 + g // 2)
                            elif not (isinstance(it, int) and it == 0):
                                pair_sums(it - 1, 1, 1 + g // 2)
                        if g == 6:
                            pair_sums(it, h, 0)
                        if g == 2:
                            if h == 0:
                                lay_out(it, 1, not last)
                            elif not last:
                                lay_out(it + 1, 0)
                        if g == 0:
                            if not (isinstance(it, int) and it == 0):
                                turn_out(2, it - 1, h)
                            set_keep(2, it, h)

            act.wait_ge(s("weights_stored"), 16)
            lay_out(0, 0)
            layer2(0)
            with act.Fori(1, ITERS - 1) as step:
                layer2(step)
            layer2(ITERS - 1)
            for b in (1, 2, 3):
                pair_sums(ITERS - 1, 1, b)
            for h in range(2):
                turn_out(2, ITERS - 1, h)
            for b in range(BLOCKS):
                root(3, b)
            sum_sources(3)
            dense(3, F)

        @block.tensor
        def _(pe):
            pe.wait_ge(s("const1"), 7)
            pe.wait_ge(s("firsts_ready"), 1)
            nc.tensor.matmul(pm[1][:, 0:P], dst_f[:, 0:1].broadcast_to([P, P]), ident[:, :], start=True, stop=True).then_inc(s("order_firsts"), 1)
            pe.wait_ge(s("disorder"), 1)
            nc.tensor.matmul(pm[0][0:J, 0:1], ones[:, :], disorder[:, 2:3], start=True, stop=True).then_inc(s("disorder_summed"), 1)
            pe.wait_ge(s("order_known"), 1)
            with pe.If(pe.value_load(unsorted[0:1, 0:1], min_val=0, max_val=1)):
                def count(n):
                    pe.wait_ge(s("sort_onehots"), n + 1)
                    for c in range(G):
                        ins = nc.tensor.matmul(hist, one_hi[:, 0, c, :], one_lo[:, 0, c, :], start=isinstance(n, int) and c == 0, stop=True, skip_group_check=True)
                    ins.then_inc(s("sort_counted"), 1)
                count(0)
                with pe.Fori(1, T // G) as n:
                    count(n)
                pe.wait_ge(s("sort_totals"), 1)
                nc.tensor.matmul(pm[0][:, 0:1], upper[:, :], st1[:, 0:1], start=True, stop=True).then_inc(s("sort_offsets"), 1)
                with pe.Fori(0, T) as t:
                    pe.wait_ge(s("sort_staged"), t + 1)
                    nc.tensor.matmul(pm[1][:, 0:P], rec[:, 0:1].broadcast_to([P, P]), ident[:, :], start=True, stop=True).then_inc(s("sort_spread"), 1)

            def histogram(it):
                for h in range(2):
                    for g in range(C // G):
                        n = (2 * it + h) * (C // G) + g
                        pe.wait_ge(s("onehots"), n + 1)
                        for c in range(G):
                            first = h == 0 and g == 0 and c == 0 and isinstance(it, int)
                            ins = nc.tensor.matmul(hist, one_hi[:, g % 2, c, :], one_lo[:, g % 2, c, :], start=first, stop=True, skip_group_check=True)
                        ins.then_inc(s("counted"), 1)
            steps(pe, histogram)
            pe.wait_ge(s("totals"), 1)
            nc.tensor.matmul(pm[0][:, 0:1], upper[:, :], st1[:, 0:1], start=True, stop=True).then_inc(s("offsets_ps"), 1)
            nc.tensor.matmul(pm[1][:, 0:P], dst_f[:, 0:1].broadcast_to([P, P]), ident[:, :], start=True, stop=True).then_inc(s("firsts_ps"), 1)

            def carry_product(k):
                pe.wait_ge(s("tails"), TURN[k])
                nc.tensor.matmul(pm[0][:, 0:F], joins[:, :], tails[:, :], start=True, stop=True).then_inc(s("carry_ps"), 1)

            def dense(k, width, w):
                for it in range(BLOCKS):
                    pe.wait_ge(s(f"staged{k}"), it + 1)
                    for half in range(2):
                        if past(it):
                            pe.wait_ge(s(f"finished{k}"), it)
                        for n in range(NB // 2):
                            bank, at = pr[2 * half + n // 4], n % 4
                            ins = nc.tensor.matmul(bank[0:width, at * P:(at + 1) * P], stage[:, half * (NB // 2) + n, 0:width], ident[:, :], start=True, stop=True)
                        ins.then_inc(s(f"turned_ps{k}"), 1)
                        pe.wait_ge(s(f"turned_sb{k}"), 4 * it + 2 * half + 2)
                        for n in range(NB // 2):
                            a = half * (NB // 2) + n
                            ins = nc.tensor.matmul(pm[0][:, a * F:(a + 1) * F], turned[0:width, n * P:(n + 1) * P], w, start=True, stop=True)
                        ins.then_inc(s(f"product{k}"), 1)

            carry_product(0)
            dense(0, 2 * F, w_sage_s[:, :])

            pe.wait_ge(s("wgt_in"), 48)
            for b in range(T // P):
                ins = nc.tensor.matmul(pr[b // 4][:, b % 4 * P:(b % 4 + 1) * P], wgt[:, b * P:(b + 1) * P], ident[:, :], start=True, stop=True)
            ins.then_inc(s("weights_ps"), 1)

            def layer1(it):
                for h in range(2):
                    pe.wait_ge(s(f"srcf_ready_{h}"), it + 1)

                    def spread_sources(g):
                        n = (2 * it + h) * (C // G) + g
                        if past(n - 1):
                            pe.wait_ge(s("eq_ready"), n - 1)
                        for c in range(G):
                            ins = nc.tensor.matmul(pbc[g % 2][:, c * P:(c + 1) * P], idxf[:, h, g * G + c:g * G + c + 1].broadcast_to([P, P]), ident[:, :], start=True, stop=True)
                        ins.then_inc(s("src_spread"), 1)

                    spread_sources(0)
                    for g in range(C // G):
                        if g + 1 < C // G:
                            spread_sources(g + 1)
                        n = (2 * it + h) * (C // G) + g
                        pe.wait_ge(s("eq_ready"), n + 1)
                        if g == 0:
                            pe.wait_ge(s(f"msg_ready_{h}"), it + 1)
                        b = g // 2
                        if g % 2 == 0:
                            if b >= 2:
                                if past((C // (2 * G)) * it + b - 1):
                                    pe.wait_ge(s(f"sums_ready_{h}"), (C // (2 * G)) * it + b - 1)
                            elif h == 1:
                                if past((C // (2 * G)) * (it + 1) - 1 + b):
                                    pe.wait_ge(s("sums_ready_0"), (C // (2 * G)) * (it + 1) - 1 + b)
                            else:
                                if past((C // (2 * G)) * it - 1 + b):
                                    pe.wait_ge(s("sums_ready_1"), (C // (2 * G)) * it - 1 + b)
                        for c in range(G):
                            t = g * G + c
                            ins = nc.tensor.matmul(pm[b % 2][:, (t % (2 * G)) * FM:(t % (2 * G) + 1) * FM], eq[:, g % 2, c * P:(c + 1) * P], msg[:, h, t, :], start=True, stop=True)
                        ins.then_inc(s("eq_used"), 1)
            steps(pe, layer1)

            def layer2(it):
                for h in range(2):
                    for g in range(C // G):
                        n = (2 * it + h) * (C // G) + g
                        for quarter in ((0, 1), (2, 3))[g % 2]:
                            if g >= 4:
                                sum_pairs(it, h, g // 2 - 2, quarter)
                            elif h == 1:
                                sum_pairs(it, 0, 2 + g // 2, quarter)
                            elif not isinstance(it, int):
                                sum_pairs(it - 1, 1, 2 + g // 2, quarter)
                        pe.wait_ge(s("hid_ready"), n + 1)
                        if past(n - 1):
                            pe.wait_ge(s("r_used"), n - 1)
                        for c in range(G):
                            units = hid[:, g % 2, c * P:(c + 1) * P]
                            nc.tensor.matmul(r_set[g % 2][:, c * P:(c + 1) * P], units, w2p[:, 0:P], start=True, stop=True)
                            ins = nc.tensor.matmul(r_set[g % 2][:, 512 + c * 2 * P:512 + (c + 1) * 2 * P], units, w2p[:, P:3 * P], start=True, stop=True)
                        ins.then_inc(s("r_done"), 1)

            def sum_pairs(it, h, b, quarter):
                n = (2 * it + h) * (C // (2 * G)) + b
                if quarter == 0:
                    pe.wait_ge(s("r_used"), (n + 1) * 2)
                    if past(3 * (n - 1)):
                        pe.wait_ge(s("pairs_out"), 3 * (n - 1))
                for w in range(quarter * (PAIR // 4), (quarter + 1) * (PAIR // 4)):
                    ins = nc.tensor.matmul(pm[b % 2][:, 0:SUMMED], ident[:, :], to_sum[b % 2][:, w, :],
                                           start=w == 0, stop=w == PAIR - 1)
                if quarter == 3:
                    ins.then_inc(s("pairs_summed"), 1)
            pe.wait_ge(s("w2_ready"), 1)
            steps(pe, layer2)
            for b in (2, 3):
                for quarter in range(4):
                    sum_pairs(ITERS - 1, 1, b, quarter)
            carry_product(2)
            carry_product(3)
            dense(3, F, w_gcn_s[:, :])

        @block.vector
        def _(dve):
            V = nc.vector
            ch = Chain(dve, "dve_chain")
            V.memset(dst_i, N).then_inc(s("pads_set"), 1)
            V.memset(src_i[:, :], 0).then_inc(s("pads_set"), 1)
            V.memset(wgt[:, :], 0.0).then_inc(s("pads_set"), 1)
            V.memset(rvec[:, :, :], 1.0).then_inc(s("pads_set"), 1)
            V.memset(xs[:, :, :], 0.0).then_inc(s("pads_set"), 1)
            V.memset(hid[:, :, :], 1.0).then_inc(s("pads_set"), 1)
            V.memset(share_b[:, :], 0.0).then_inc(s("zeros_set"), 1)
            ch.do(V.memset(ones[:, :], 1.0), False)
            ch.do(V.memset(keep[:, :, :, :], 0.0), False)
            ch.do(V.memset(xT[:, :, :, :], 0.0), False)
            ch.do(V.memset(sc[:, :, :, :], 0.0))

            def bc(ap, shape, axis):
                return ap.unsqueeze(axis).broadcast_to(shape)

            NJF, BN = [P, J, F], [P, NB, F]

            def layernorm(k, b):
                js = slice(b * NB, (b + 1) * NB)
                ch.do(V.tensor_reduce(st1[:, js], xs[:, js, :], AX, ALU.add))
                ch.do(V.tensor_scalar(st1[:, js], st1[:, js], 1.0 / F, None, ALU.mult))
                ch.do(V.tensor_tensor(tmpv[:, js, :], xs[:, js, :], bc(st1[:, js], BN, 2), ALU.subtract))
                ch.do(V.tensor_tensor(hn[:, js, :], tmpv[:, js, :], tmpv[:, js, :], ALU.mult))
                ch.do(V.tensor_reduce(st2[:, js], hn[:, js, :], AX, ALU.add))
                ch.do(V.tensor_scalar(st2[:, js], st2[:, js], 1.0 / F, EPS, ALU.mult, ALU.add))
                dve.sem_inc(s("var"), 1)
                dve.wait_ge(s("std"), BLOCKS * k + b + 1)
                ch.do(V.reciprocal(st3[:, js], st3[:, js]))
                if k == 3:
                    ch.do(V.tensor_tensor(st3[:, js], st3[:, js], isd[:, js], ALU.mult))
                if k == 2:
                    BM = [P, NB, MUL]
                    ch.do(V.scalar_tensor_tensor(hn[:, js, 0:MUL], tmpv[:, js, 0:MUL], 0.0, bc(st3[:, js], BM, 2), ALU.max, ALU.mult), False)
                    for c, i in enumerate((2, 0, 1)):
                        ch.do(V.scalar_tensor_tensor(hn[:, js, MUL * (c + 1):MUL * (c + 2)], tmpv[:, js, MUL + i:F:3], 0.0, bc(st3[:, js], BM, 2), ALU.max, ALU.mult), c == 2)
                else:
                    ch.do(V.scalar_tensor_tensor(hn[:, js, :], tmpv[:, js, :], 0.0, bc(st3[:, js], BN, 2), ALU.max, ALU.mult))
                dve.sem_inc(s("normed"), 1)

            dve.wait_ge(s("x_in"), 48)
            for b in range(BLOCKS):
                layernorm(0, b)

            dve.wait_ge(s("dst_in"), 48)
            dve.wait_ge(s("const1"), 7)
            ch.do(V.tensor_copy(ji[:, :], ji_i[:, :]), False)
            ch.do(V.tensor_copy(pif[:, :], pi_i[:, :]), False)
            ch.do(V.tensor_copy(dump[:, :], dump_i[:, :]), False)
            ch.do(V.tensor_copy(sdump[:, :], sdump_i[:, :]), False)
            ch.do(V.tensor_copy(dst_f[:, :], dst_i))

            def split(quotient):
                ch.do(V.tensor_scalar(quotient, dst_f[:, :], 1.0 / J, None, ALU.mult))
                ch.do(V.tensor_copy(hi, quotient))
                ch.do(V.scalar_tensor_tensor(lo, hi, -float(J), dst_f[:, :], ALU.mult, ALU.add))
                ch.do(V.tensor_scalar(hi, lo, 0.0, float(J), ALU.is_lt, ALU.mult))
                ch.do(V.tensor_tensor(lo, lo, hi, ALU.add))
                ch.do(V.tensor_scalar(hi, lo, float(J), float(J), ALU.is_ge, ALU.mult))
                ch.do(V.tensor_tensor(lo, lo, hi, ALU.subtract))
                ch.do(V.tensor_tensor(hi, dst_f[:, :], lo, ALU.subtract))

            dve.sem_inc(s("firsts_ready"), 1)
            ch.do(V.tensor_tensor(lo[:, 1:T], dst_f[:, 1:T], dst_f[:, 0:T - 1], ALU.is_lt))
            ch.do(V.tensor_reduce(disorder[:, 0:1], lo[:, 1:T], AX, ALU.add))
            dve.wait_ge(s("order_firsts"), 1)
            ch.do(V.scalar_tensor_tensor(ends_after[:, :], pm[1][:, 0:P], dst_f[:, T - 1:T], upper[:, :], ALU.is_lt, ALU.mult))
            ch.do(V.tensor_reduce(disorder[:, 1:2], ends_after[:, :], AX, ALU.add))
            ch.do(V.tensor_tensor(disorder[:, 2:3], disorder[:, 0:1], disorder[:, 1:2], ALU.add))
            dve.sem_inc(s("disorder"), 1)
            dve.wait_ge(s("disorder_summed"), 1)
            V.tensor_scalar(unsorted[:, :], pm[0][0:1, 0:1], 0.0, None, ALU.is_gt).then_inc(s("order_known"), 1)
            dve.wait_ge(s("order_known"), 1)
            before_sort = ch.n
            with dve.If(dve.value_load(unsorted[0:1, 0:1], min_val=0, max_val=1)):
                cs = Chain(dve, "dve_sort")
                main, ch = ch, cs
                dve.wait_ge(s("src_in"), 48)
                dve.wait_ge(s("wgt_in"), 48)
                dve.wait_ge(s("attr_in"), 48)
                split(dst_i)

                def count(n):
                    cols = bass.ds(n * G, G)
                    V.tensor_tensor(one_hi[:, 0, :, :], bc(hi[:, cols], [P, G, P], 2), bc(pif[:, :], [P, G, P], 1), ALU.is_equal)
                    V.tensor_tensor(one_lo[:, 0, :, :], bc(lo[:, cols], [P, G, J], 2), bc(ji[:, :], [P, G, J], 1), ALU.is_equal).then_inc(s("sort_onehots"), 1)
                    dve.wait_ge(s("sort_counted"), n + 1)
                count(0)
                with dve.Fori(1, T // G) as n:
                    count(n)
                ch.do(V.tensor_copy(cnt[:, :], hist))
                ch.do(V.tensor_tensor_scan(run[:, :], ones[:, :], cnt[:, :], 0.0, ALU.mult, ALU.add))
                V.tensor_copy(st1[:, 0:1], run[:, J - 1:J]).then_inc(s("sort_totals"), 1)
                dve.wait_ge(s("sort_offsets"), 1)
                ch.do(V.tensor_copy(offs[:, :], pm[0][:, 0:1]))
                ch.do(V.tensor_scalar(first_f[:, :], run[:, :], offs[:, :], None, ALU.add))
                ch.do(V.tensor_tensor(first_f[:, :], first_f[:, :], cnt[:, :], ALU.subtract))
                dve.sem_inc(s("sort_cursors"), 1)
                ct = Chain(dve, "dve_sort_columns", per_step=17)
                with dve.Fori(0, T) as t:
                    ct.step(t)
                    col = bass.ds(t, 1)
                    ct.do(V.tensor_copy(rec[:, 0:1], dst_f[:, col]), False)
                    ct.do(V.tensor_copy(rec[:, 1:2], src_i[:, col]), False)
                    ct.do(V.tensor_copy(rec[:, 2:3], wgt[:, col]), False)
                    ct.do(V.tensor_copy(rec[:, 3:6], rvec[:, col, :]), False)
                    ct.do(V.tensor_copy(node_i[:, :], dst_f[:, col]))
                    dve.sem_inc(s("sort_staged"), 1)
                    dve.wait_ge(s("sort_spread"), t + 1)
                    ct.do(V.scalar_tensor_tensor(ends_after[:, :], pm[1][:, 0:P], rec[:, 0:1], lower[:, :], ALU.is_equal, ALU.mult), False)
                    ct.do(V.scalar_tensor_tensor(joins[:, :], pm[1][:, 0:P], rec[:, 0:1], upper[:, :], ALU.is_equal, ALU.mult))
                    ct.do(V.tensor_reduce(rank[:, 0:1], ends_after[:, :], AX, ALU.add), False)
                    ct.do(V.tensor_reduce(rank[:, 1:2], joins[:, :], AX, ALU.add))
                    ct.do(V.tensor_scalar(rank[:, 1:2], rank[:, 1:2], 0.0, None, ALU.is_equal), False)
                    ct.do(V.tensor_tensor(target[:, :], rec[:, 0:1], dump[:, :], ALU.subtract))
                    ct.do(V.tensor_tensor(target[:, :], target[:, :], rank[:, 1:2], ALU.mult))
                    ct.do(V.tensor_tensor(target[:, :], target[:, :], dump[:, :], ALU.add))
                    ct.do(V.tensor_copy(target_i[:, :], target[:, :]))
                    dve.wait_ge(s("sort_cursor_in"), 16 * (t + 1))
                    ct.do(V.tensor_tensor(place[:, :], place[:, :], rank[:, 0:1], ALU.add))
                    ct.do(V.tensor_copy(place_i[:, :], place[:, :]), False)
                    ct.do(V.tensor_scalar(next_place[:, :], place[:, :], 1.0, None, ALU.add))
                    assert ct.n == ct.per, ct.n
                    dve.sem_inc(s("sort_placed"), 1)
                    dve.wait_ge(s("sort_moved"), 32 * (t + 1))
                for q in range(PARTS):
                    n = T // PARTS
                    back = share_a[:, 0:n * REC].rearrange("p (t c) -> p t c", c=REC)
                    dve.wait_ge(s("sort_back"), 16 * (q + 1))
                    ch.do(V.tensor_copy(dst_f[:, q * n:(q + 1) * n], back[:, :, 0]), False)
                    ch.do(V.tensor_copy(src_i[:, q * n:(q + 1) * n], back[:, :, 1]), False)
                    ch.do(V.tensor_copy(wgt[:, q * n:(q + 1) * n], back[:, :, 2]), False)
                    ch.do(V.tensor_copy(rvec[:, q * n:(q + 1) * n, :], back[:, :, 3:6]))
                    dve.sem_inc(s("sort_unpacked"), 1)
                ch = main
            assert ch.n == before_sort

            ch.do(V.tensor_copy(dst0_i[:, :], dst_f[:, 0:1]), False)
            ch.do(V.memset(same[:, 0:1], 0.0), False)
            ch.do(V.tensor_tensor(same[:, 1:T], dst_f[:, 1:T], dst_f[:, 0:T - 1], ALU.is_equal))
            dve.sem_inc(s("same_ready"), 1)
            split(dst_i)

            def scan(chain, k, it, h):
                dve.wait_ge(s(f"keep_ready_{h}"), k * ITERS + it + 1)
                chain.do(V.tensor_copy(xT[:, h, :, 0], sc[:, 1 - h, :, C]))
                if k != 1:
                    if past(OLD[k] + it):
                        dve.wait_ge(s(f"rows_ready_{h}"), OLD[k] + it)
                ins = V.tensor_tensor_scan(sc[:, h, :, :].rearrange("p f t -> p (f t)"), keep[:, h, :, :].rearrange("p f t -> p (f t)"),
                                           xT[:, h, :, :].rearrange("p f t -> p (f t)"), 0.0, ALU.mult, ALU.add)
                ins.then_inc(s(f"scanned_{h}"), 1)
                dve.wait_ge(s(f"scanned_{h}"), k * ITERS + it + 1)

            c0 = Chain(dve, "dve_layer0", per_step=2)

            def layer0(it):
                c0.step(it)
                for h in range(2):
                    for g in range(C // G):
                        n = (2 * it + h) * (C // G) + g
                        if past(n - 1):
                            dve.wait_ge(s("counted"), n - 1)
                        cols = bass.ds(it * (2 * C) + h * C + g * G, G)
                        V.tensor_tensor(one_hi[:, g % 2, :, :], bc(hi[:, cols], [P, G, P], 2), bc(pif[:, :], [P, G, P], 1), ALU.is_equal)
                        V.tensor_tensor(one_lo[:, g % 2, :, :], bc(lo[:, cols], [P, G, J], 2), bc(ji[:, :], [P, G, J], 1), ALU.is_equal).then_inc(s("onehots"), 1)
                    dve.wait_ge(s(f"turned_in_{h}"), it + 1)
                    scan(c0, 0, it, h)
            steps(dve, layer0)

            dve.wait_ge(s("counted"), 2 * ITERS * (C // G))
            ch.do(V.tensor_copy(cnt[:, :], hist))
            ch.do(V.tensor_tensor_scan(run[:, :], ones[:, :], cnt[:, :], 0.0, ALU.mult, ALU.add))
            V.tensor_copy(st1[:, 0:1], run[:, J - 1:J]).then_inc(s("totals"), 1)
            dve.wait_ge(s("offsets_ps"), 1)
            ch.do(V.tensor_copy(offs[:, :], pm[0][:, 0:1]))
            ch.do(V.tensor_scalar(last_f[:, :], run[:, :], offs[:, :], 1.0, ALU.add, ALU.subtract), False)
            ch.do(V.tensor_scalar(nzero[:, :], cnt[:, :], 0.0, None, ALU.is_gt))
            ch.do(V.tensor_tensor(first_f[:, :], last_f[:, :], cnt[:, :], ALU.subtract))
            ch.do(V.tensor_scalar(first_f[:, :], first_f[:, :], 1.0, None, ALU.add))
            ch.do(V.tensor_tensor(first_f[:, :], first_f[:, :], sdump[:, :], ALU.subtract))
            ch.do(V.tensor_scalar(last_f[:, :], last_f[:, :], float(EP), None, ALU.subtract))
            ch.do(V.tensor_tensor(first_f[:, :], first_f[:, :], nzero[:, :], ALU.mult), False)
            ch.do(V.tensor_tensor(last_f[:, :], last_f[:, :], nzero[:, :], ALU.mult))
            ch.do(V.tensor_tensor(first_f[:, :], first_f[:, :], sdump[:, :], ALU.add), False)
            ch.do(V.tensor_scalar(last_f[:, :], last_f[:, :], float(EP), None, ALU.add))
            V.tensor_copy(first_i[:, :], first_f[:, :]).then_inc(s("places_ready"), 1)
            V.tensor_copy(last_i[:, :], last_f[:, :]).then_inc(s("places_ready"), 1)
            dve.wait_ge(s("firsts_ps"), 1)
            ch.do(V.scalar_tensor_tensor(joins[:, :], pm[1][:, 0:P], dst_f[:, T - 1:T], upper[:, :], ALU.is_equal, ALU.mult), False)
            ch.do(V.scalar_tensor_tensor(ends_after[:, :], pm[1][:, 0:P], dst_f[:, 0:1], upper[:, :], ALU.is_equal, ALU.mult))
            ch.do(V.tensor_reduce(cidx_f[:, :], ends_after[:, :], AX, ALU.add))
            ch.do(V.tensor_scalar(cidx_f[:, :], cidx_f[:, :], 0.0, None, ALU.is_equal), False)
            ch.do(V.tensor_tensor(cidx_t[:, :], dst_f[:, 0:1], dump[:, :], ALU.subtract))
            ch.do(V.tensor_tensor(cidx_t[:, :], cidx_t[:, :], cidx_f[:, :], ALU.mult))
            ch.do(V.tensor_tensor(cidx_t[:, :], cidx_t[:, :], dump[:, :], ALU.add))
            ch.do(V.tensor_copy(cidx[:, :], cidx_t[:, :]))

            def send_carries():
                ch.do(V.tensor_copy(tails[:, :], sc[:, 1, :, C]))
                dve.sem_inc(s("tails"), 1)

            def finish_carries(k):
                dve.wait_ge(s("carry_ps"), TURN[k])
                V.tensor_copy(carry[:, :], pm[0][:, 0:F]).then_inc(s("carry_ready"), 1)
                dve.wait_ge(s("carried_in"), 16 * TURN[k])

            def node_sums(k, b):
                js = slice(b * NB, (b + 1) * NB)
                dve.wait_ge(s(f"ends_in_{b}"), 16 * NB * TURN[k])
                ch.do(V.tensor_tensor(ag[:, js, :], ag[:, js, :], tmpv[:, js, :], ALU.add))
                return js

            tb = share_c[:, NB * 4 * F:NB * 5 * F].rearrange("p (j f) -> p j f", f=F)
            pmv = pm[0][:, 0:NB * F].rearrange("p (j f) -> p j f", f=F)

            def relu_dense(k, b, js, bias):
                dve.wait_ge(s(f"product{k}"), 2 * b + 2)
                ch.do(V.tensor_tensor(tb, pmv, bc(bias[:, :], BN, 1), ALU.add))
                ch.do(V.scalar_tensor_tensor(xs[:, js, :], tb, 0.0, xs[:, js, :], ALU.max, ALU.add))
                dve.sem_inc(s(f"finished{k}"), 1)

            send_carries()
            finish_carries(0)
            ch.do(V.tensor_scalar(rcnt[:, :], cnt[:, :], 1.0, None, ALU.max))
            ch.do(V.reciprocal(rcnt[:, :], rcnt[:, :]))
            dve.wait_ge(s("weights_in"), 16 * 8)
            for b in range(BLOCKS):
                js = node_sums(0, b)
                V.tensor_copy(stage[:, :, 0:F], hn[:, js, :])
                V.tensor_tensor(stage[:, :, F:2 * F], ag[:, js, :], bc(rcnt[:, js], BN, 2), ALU.mult).then_inc(s("staged0"), 1)
                relu_dense(0, b, js, b_sage_s)
                layernorm(1, b)

            dve.wait_ge(s("attr_in"), 48)
            rt = share_b[:, 0:T]
            ra = share_a[:, 0:T]
            ch.do(V.tensor_tensor(ra, rvec[:, :, 0], rvec[:, :, 0], ALU.mult), False)
            ch.do(V.tensor_tensor(rt, rvec[:, :, 1], rvec[:, :, 1], ALU.mult))
            ch.do(V.tensor_tensor(ra, ra, rt, ALU.add))
            ch.do(V.tensor_tensor(rt, rvec[:, :, 2], rvec[:, :, 2], ALU.mult))
            ch.do(V.tensor_tensor(ra, ra, rt, ALU.add))
            dve.sem_inc(s("norm2"), 1)
            dve.wait_ge(s("norm"), 1)
            ch.do(V.reciprocal(ra, rt))
            ch.do(V.tensor_tensor(rvec[:, :, :], rvec[:, :, :], bc(ra, [P, T, 3], 2), ALU.mult))
            ch.do(V.tensor_scalar(rcnt[:, :], cnt[:, :], 1.0, 1.0, ALU.add, ALU.max))
            dve.sem_inc(s("degree"), 1)
            dve.wait_ge(s("degree_root"), 1)
            ch.do(V.reciprocal(isd[:, :], isd[:, :]))

            y0, y1 = 0.5 / sqrt(pi), sqrt(3.0 / (4.0 * pi))
            norm0 = sqrt(4.0 * pi) / sqrt(2 * MUL)
            norm1 = sqrt(4.0 * pi) * sqrt(3.0) / sqrt(4 * MUL)
            quad = sqrt(1.0 / (24.0 * pi))
            sq = MUL * MUL

            def uv(ap):
                return ap.rearrange("p (u v) -> p u v", v=MUL)

            def pick(k):
                return w2s[:, 3 * sq:6 * sq].rearrange("p (u v k) -> p u v k", v=MUL, k=3)[:, :, :, k]
            coef = w2p[:, :]
            c_vec, c_cross = (coef[:, 0:2 * sq].rearrange("p (u s v) -> p u s v", s=2, v=MUL)[:, :, k, :] for k in range(2))
            pairs = coef[:, 2 * sq:].rearrange("p (k u s v) -> p k u s v", k=2, u=MUL, s=2)
            ch.do(V.tensor_scalar(pairs[:, 0, :, 0, :], uv(w2s[:, 0:sq]), norm0 * y0, None, ALU.mult), False)
            ch.do(V.tensor_scalar(pairs[:, 0, :, 1, :], uv(w2s[:, sq:2 * sq]), norm0 * y1 / sqrt(3), None, ALU.mult), False)
            ch.do(V.tensor_scalar(pairs[:, 1, :, 0, :], uv(w2s[:, 2 * sq:3 * sq]), norm1 * y1 / sqrt(3), None, ALU.mult), False)
            ch.do(V.tensor_scalar(pairs[:, 1, :, 1, :], pick(2), norm1 * 3 * quad, None, ALU.mult), False)
            ch.do(V.tensor_scalar(c_cross, pick(1), norm1 * y1 / sqrt(6), None, ALU.mult), False)
            ch.do(V.tensor_scalar(c_vec, pick(0), norm1 * y0 / sqrt(3), None, ALU.mult), False)
            ch.do(V.tensor_scalar(fr[0:HID + 1, 0:MUL, 0, :], pick(2), -norm1 * quad, None, ALU.mult))
            ch.do(V.tensor_tensor(c_vec, c_vec, fr[0:HID + 1, 0:MUL, 0, :], ALU.add))
            dve.sem_inc(s("w2_ready"), 1)

            dve.wait_ge(s("wgt_in"), 48)
            ch.do(V.memset(sc[:, 1, :, C], 0.0))
            c1 = Chain(dve, "dve_layer1", per_step=0)
            PER1 = 2 * (1 + 2 + (C // G) * 3 + 5)
            c1.per = PER1

            def layer1(it):
                c1.step(it)
                for h in range(2):
                    dve.wait_ge(s(f"turned_in_{h}"), ITERS + it + 1)
                    scan(c1, 1, it, h)
                    cols = bass.ds(it * (2 * C) + h * C, C)
                    if past((2 * it + h - 1) * (C // G)):
                        dve.wait_ge(s("eq_used"), (2 * it + h - 1) * (C // G))
                    c1.do(V.tensor_tensor(msg[:, h, :, 0:F], sc[:, h, :, 1:W1].rearrange("p f t -> p t f"), bc(wgt[:, cols], [P, C, F], 2), ALU.mult), False)
                    c1.do(V.tensor_copy(msg[:, h, :, F], wgt[:, cols]))
                    dve.sem_inc(s(f"msg_ready_{h}"), 1)
                    dve.wait_ge(s(f"srcf_ready_{h}"), it + 1)
                    for g in range(C // G):
                        n = (2 * it + h) * (C // G) + g
                        dve.wait_ge(s("src_spread"), n + 1)
                        if past(n - 1):
                            dve.wait_ge(s("eq_used"), n - 1)
                        eqv = eq[:, g % 2, :].rearrange("p (c q) -> p c q", q=P)
                        c1.do(V.tensor_tensor(eqv, pbc[g % 2][:, :].rearrange("p (c q) -> p c q", q=P),
                                              bc(idxf[:, h, g * G:(g + 1) * G], [P, G, P], 2), ALU.is_equal))
                        dve.sem_inc(s("eq_ready"), 1)
                        ev = earlier[:, :].rearrange("p (c q) -> p c q", q=P)
                        c1.do(V.tensor_tensor(ev, eqv, bc(lower[:, :], [P, G, P], 1), ALU.mult))
                        c1.do(V.tensor_reduce(dup[:, g * G:(g + 1) * G], ev, AX, ALU.add), g == C // G - 1)
                    c1.do(V.tensor_scalar(widx_f[:, :], idxf[:, h, :], dump[:, :], None, ALU.subtract), False)
                    c1.do(V.tensor_scalar(dup[:, :], dup[:, :], 0.0, None, ALU.is_equal))
                    c1.do(V.tensor_tensor(widx_f[:, :], widx_f[:, :], dup[:, :], ALU.mult))
                    c1.do(V.tensor_scalar(widx_f[:, :], widx_f[:, :], dump[:, :], None, ALU.add))
                    for q in range(TABLES):
                        if past((2 * it + h - 1) * (16 * C // TABLES)):
                            dve.wait_ge(s(f"added_{q}"), (2 * it + h - 1) * (16 * C // TABLES))
                    c1.do(V.tensor_copy(idx[:, h, :], widx_f[:, :]))
                    dve.sem_inc(s(f"targets_ready_{h}"), 1)
                    dve.sem_inc(s(f"srcf_used_{h}"), 1)
                assert c1.n == PER1, c1.n
            steps(dve, layer1)
            part_0 = part_in[0][:, 0:J * FM].rearrange("p (j f) -> p j f", f=FM)
            for k in range(TABLES):
                sfm = part_in[k][:, 0:J * FM].rearrange("p (j f) -> p j f", f=FM)
                dve.wait_ge(s(f"part_in{k}"), 16)
                if k == 0:
                    continue
                if k == 1:
                    ch.do(V.tensor_tensor(ag[:, :, :], part_0[:, :, 0:F], sfm[:, :, 0:F], ALU.add), False)
                    ch.do(V.tensor_tensor(st1[:, :], part_0[:, :, F], sfm[:, :, F], ALU.add))
                else:
                    ch.do(V.tensor_tensor(ag[:, :, :], ag[:, :, :], sfm[:, :, 0:F], ALU.add), False)
                    ch.do(V.tensor_tensor(st1[:, :], st1[:, :], sfm[:, :, F], ALU.add))
            ch.do(V.tensor_tensor(hn[:, :, :], hn[:, :, :], bc(st1[:, :], NJF, 2), ALU.mult))
            ch.do(V.tensor_tensor(ag[:, :, :], ag[:, :, :], hn[:, :, :], ALU.subtract))
            ch.do(V.tensor_tensor(xs[:, :, :], xs[:, :, :], ag[:, :, :], ALU.add))
            for b in range(BLOCKS):
                layernorm(2, b)

            ch.do(V.memset(sc[:, 1, :, C], 0.0))

            CV = [P, C, 3, MUL]
            c2 = Chain(dve, "dve_layer2")
            PREPARE, SUM, FINISH = 3, C + C // G, 3
            c2.per = 2 * (PREPARE + SUM + FINISH)

            def prepare(it, h):
                dve.wait_ge(s("factors_in"), (2 * it + h + 1) * 6)
                r = r5[:, h, :, :]
                dotted = c2.do(V.tensor_tensor(fr3, f5[:, :, 0:3, :], bc(r[:, :, 0:3], CV, 3), ALU.mult), False)
                yield
                c2.now(dotted)
                added = c2.do(V.tensor_tensor(d16[:, h, :, MUL:], fr3[:, :, 0, :], fr3[:, :, 1, :], ALU.add), False)
                c2.now(added)
                c2.do(V.tensor_tensor(d16[:, h, :, MUL:], d16[:, h, :, MUL:], fr3[:, :, 2, :], ALU.add))
                yield

            def finish_messages(it, h):
                m1 = xT[:, h, MUL:F, 1:W1].rearrange("p (o u) t -> p t o u", o=3)
                dve.wait_ge(s("pairs_out"), (2 * it + h + 1) * (3 * C // (2 * G)))
                scaled = c2.do(V.tensor_tensor(fr3, bc(sv[:, h, :, :], CV, 2), bc(rvec[:, bass.ds(it * (2 * C) + h * C, C), :], CV, 3), ALU.mult), False)
                yield
                c2.now(scaled)
                c2.do(V.tensor_tensor(m1, fr3, red[:, h, :, :].rearrange("p t (u o) -> p t o u", o=3), ALU.add), False)
                yield
                dve.wait_ge(s(f"keep_ready_{h}"), 2 * ITERS + it + 1)
                whole = c2.do(V.tensor_copy(xT[:, h, :, 0], sc[:, 1 - h, :, C]), False)
                yield
                if past(OLD[2] + it):
                    dve.wait_ge(s(f"rows_ready_{h}"), OLD[2] + it)
                c2.now(whole)
                V.tensor_tensor_scan(sc[:, h, :, :].rearrange("p f t -> p (f t)"), keep[:, h, :, :].rearrange("p f t -> p (f t)"),
                                     xT[:, h, :, :].rearrange("p f t -> p (f t)"), 0.0, ALU.mult, ALU.add).then_inc(s(f"scanned_{h}"), 1)
                yield
                dve.wait_ge(s(f"scanned_{h}"), 2 * ITERS + it + 1)
                yield

            def layer2(it):
                first, last = isinstance(it, int) and it == 0, isinstance(it, int) and it == ITERS - 1
                if not first:
                    c2.step(it)
                    c2.before = PREPARE - FINISH
                for h in range(2):
                    if h == 1:
                        chunk_before = finish_messages(it, 0)
                    else:
                        chunk_before = iter(()) if first else finish_messages(it - 1, 1)
                    if h == 0:
                        chunk_after = prepare(it, 1)
                    else:
                        chunk_after = iter(()) if last else prepare(it + 1, 0)
                    dve.wait_ge(s("crossed"), 2 * it + h + 1)
                    for g in range(C // G + 1):
                        n = (2 * it + h) * (C // G) + g
                        half, b = g % 2, g // 2
                        if g < C // G:
                            a = g * G
                            dve.wait_ge(s("r_done"), n + 1)
                            if g >= 2:
                                c2.now(reduced[half])
                            for c in range(G):
                                coefficients = bc(r_set[half][:, c * P:(c + 1) * P].rearrange("p (u w) -> p u w", w=PAIR), [P, MUL, 3, PAIR], 2)
                                factors = bc(fx[h][:, a + c, :, :], [P, MUL, 3, PAIR], 1)
                                if c < G - 1:
                                    place = prod[:, half * (G - 1) + c, :].rearrange("p (u o w) -> p u o w", o=3, w=PAIR)
                                else:
                                    past_sums = (2 * it + h) * (C // (2 * G)) + b - 1
                                    if half == 0 and past(past_sums):
                                        dve.wait_ge(s("pairs_summed"), past_sums)
                                    place = to_sum[b % 2][:, :, 2 * G * PAIR + half * VEC:2 * G * PAIR + (half + 1) * VEC].rearrange("p w (u o) -> p u o w", o=3)
                                c2.do(V.tensor_tensor(place, coefficients, factors, ALU.mult), False)
                            V.tensor_tensor(to_sum[b % 2][:, :, half * G * PAIR:(half + 1) * G * PAIR].rearrange("p w (t q) -> p t q w", q=PAIR),
                                            r_set[half][:, 512:512 + G * 2 * P].rearrange("p (t q w) -> p t q w", t=G, w=PAIR),
                                            bc(d16[:, h, a:a + G, :], [P, G, PAIR, PAIR], 2), ALU.mult).then_inc(s("r_used"), 1)
                        if g >= 1:
                            a = (g - 1) * G
                            dve.wait_ge(s("r_used"), n)
                            reduced[1 - half] = c2.do(V.tensor_reduce(red[:, h, a:a + G - 1, :].rearrange("p t q -> p (t q)"),
                                                                      prod[:, (1 - half) * (G - 1):(2 - half) * (G - 1), :].rearrange("p s (q w) -> p (s q) w", w=PAIR),
                                                                      AX, ALU.add), g == C // G)
                        for _ in range((0, 0, 0, 0, 1, 1, 2, 1, 1)[g]):
                            next(chunk_before, None)
                        for _ in range((0, 0, 1, 1, 0, 0, 0, 0, 1)[g]):
                            next(chunk_after, None)
                assert c2.n == c2.per + (PREPARE - FINISH if first else -PREPARE if last else 0), c2.n

            c2.step(0)
            reduced = [0, 0]
            for _ in prepare(0, 0):
                pass
            layer2(0)
            with dve.Fori(1, ITERS - 1) as step:
                layer2(step)
            layer2(ITERS - 1)
            c2.step(ITERS)
            c2.before = -FINISH
            for _ in finish_messages(ITERS - 1, 1):
                pass
            send_carries()
            finish_carries(2)
            for b in range(BLOCKS):
                js = node_sums(2, b)
                ch.do(V.tensor_tensor(xs[:, js, 0:MUL], xs[:, js, 0:MUL], ag[:, js, 0:MUL], ALU.add), False)
                for c, i in enumerate((2, 0, 1)):
                    ch.do(V.tensor_tensor(xs[:, js, MUL + i:F:3], xs[:, js, MUL + i:F:3], ag[:, js, MUL * (c + 1):MUL * (c + 2)], ALU.add), c == 2)
                layernorm(3, b)

            ch.do(V.memset(sc[:, 1, :, C], 0.0))
            c3 = Chain(dve, "dve_layer3", per_step=2)

            def layer3(it):
                c3.step(it)
                for h in range(2):
                    dve.wait_ge(s(f"turned_in_{h}"), 3 * ITERS + it + 1)
                    scan(c3, 3, it, h)
            steps(dve, layer3)
            send_carries()
            finish_carries(3)
            for b in range(BLOCKS):
                js = node_sums(3, b)
                ch.do(V.tensor_tensor(ag[:, js, :], ag[:, js, :], hn[:, js, :], ALU.add))
                V.tensor_tensor(stage[:, :, 0:F], ag[:, js, :], bc(isd[:, js], BN, 2), ALU.mult).then_inc(s("staged3"), 1)
                relu_dense(3, b, js, b_gcn_s)
                dve.sem_inc(s("x_done"), 1)


_INS = ["x", "src", "dst", "edge_attr_3", "edge_weight", "L0_gnn_W", "L0_gnn_b", "L2_gnn_w1", "L2_gnn_b1", "L2_gnn_w2", "L2_gnn_b2", "L3_gnn_W", "L3_gnn_bias"]


def kernel(**inputs):
    import numpy as np
    import concourse.bacc as bacc
    from concourse import mybir as mb
    from concourse.bass_utils import run_bass_kernel_spmd

    nc = bacc.Bacc("TRN2", target_bir_lowering=False, num_devices=1)
    arrays, args = {}, []
    for name in _INS:
        a = np.ascontiguousarray(inputs[name])
        arrays[f"in_{name}"] = a
        args.append(nc.dram_tensor(f"in_{name}", a.shape, mb.dt.from_np(a.dtype), kind="ExternalInput").ap())
    args.append(nc.dram_tensor("out_x", (N, F), mb.dt.float32, kind="ExternalOutput").ap())
    gnn_program(nc, *args)
    result = run_bass_kernel_spmd(nc, [arrays], core_ids=[0])
    return result.results[0]["out_x"]
```
